# Optimizing a Trainium2 kernel written in Bass

```python
import numpy as np
import jax
import jax.numpy as jnp

def _softmax(x, axis=-1):
    return jax.nn.softmax(x, axis=axis)

def _gelu(x):
    return jax.nn.gelu(x, approximate=True)

def _silu(x):
    return jax.nn.silu(x)

def _sigmoid(x):
    return jax.nn.sigmoid(x)

def _layernorm(x, axis=-1, eps=1e-05):
    m = jnp.mean(x, axis=axis, keepdims=True)
    v = jnp.var(x, axis=axis, keepdims=True)
    return (x - m) / jnp.sqrt(v + eps)

def _scatter_add(tgt, idx, src, axis=0):
    return tgt.at[idx].add(src)

def _segment_sum(src, seg, n):
    return jax.ops.segment_sum(src, seg, n)
kernel_name = 'mk_adaln_d2_jaxref_r8_4d150e'

def setup_inputs(seed: int=0):
    np.random.seed(seed)
    _w = jnp.asarray

    def _L0_attn_setup():
        import jax, jax.numpy as jnp
        import numpy as np
        B, T, C = (4, 256, 128)
        key = jax.random.key(seed)
        k1, k2, k3 = jax.random.split(key, 3)
        x = jax.random.normal(k1, (B, T, C), dtype=jnp.float32)
        qkv_w = jax.random.normal(k2, (3 * C, C), dtype=jnp.float32) * (1.0 / np.sqrt(C))
        out_w = jax.random.normal(k3, (C, C), dtype=jnp.float32) * (1.0 / np.sqrt(C))
        out_b = jnp.zeros((C,), dtype=jnp.float32)
        return {'x': x, 'qkv_w': qkv_w, 'out_w': out_w, 'out_b': out_b}
    _L0_attn_in = _L0_attn_setup()

    def _L0_ffn_setup():
        import jax, jax.numpy as jnp
        import numpy as np
        TOP_K = 2
        key = jax.random.key(seed)
        ks = jax.random.split(key, 5)
        B, N, C, FF, E = (2, 256, 128, 512, 8)
        x = jax.random.normal(ks[0], (B, N, C), dtype=jnp.float32)
        router_w = jax.random.normal(ks[1], (E, C), dtype=jnp.float32) * 0.02
        lim1 = np.sqrt(6.0 / (FF + C))
        expert_w1 = jax.random.uniform(ks[2], (E, FF, C), dtype=jnp.float32, minval=-lim1, maxval=lim1)
        expert_b1 = jnp.zeros((E, FF), dtype=jnp.float32)
        expert_w2 = jax.random.uniform(ks[3], (E, C, FF), dtype=jnp.float32, minval=-lim1, maxval=lim1)
        expert_b2 = jnp.zeros((E, C), dtype=jnp.float32)
        return {'x': x, 'router_w': router_w, 'expert_w1': expert_w1, 'expert_b1': expert_b1, 'expert_w2': expert_w2, 'expert_b2': expert_b2}
    _L0_ffn_in = _L0_ffn_setup()
    _L0_c = _w((lambda *s: np.random.randn(*s).astype(np.float32) * 0.05)(4, 128))
    _L0_wmod = _w((lambda *s: np.random.randn(*s).astype(np.float32) * 0.05)(128, 6 * 128) * 128 ** (-0.5))

    def _L1_attn_setup():
        import jax, jax.numpy as jnp
        import numpy as np
        import math
        B, S, D, H, R, DFF = (4, 128, 128, 16, 64, 512)

        def _layernorm(x, g, b, eps=1e-05):
            m = jnp.mean(x, axis=-1, keepdims=True)
            v = jnp.var(x, axis=-1, keepdims=True)
            return (x - m) / jnp.sqrt(v + eps) * g + b
        key = jax.random.key(seed)
        ks = jax.random.split(key, 12)
        sc = 0.02
        return {'src': jax.random.normal(ks[0], (B, S, D), jnp.float32), 'in_proj_w': jax.random.normal(ks[1], (3 * D, D), jnp.float32) * sc, 'in_proj_b': jnp.zeros((3 * D,), jnp.float32), 'out_proj_w': jax.random.normal(ks[2], (D, D), jnp.float32) * sc, 'out_proj_b': jnp.zeros((D,), jnp.float32), 'Qp_w': jax.random.normal(ks[3], (R, D), jnp.float32) * sc, 'Qp_b': jnp.zeros((R,), jnp.float32), 'Kp_w': jax.random.normal(ks[4], (R, D), jnp.float32) * sc, 'Kp_b': jnp.zeros((R,), jnp.float32), 'Vp_w': jax.random.normal(ks[5], (D, D), jnp.float32) * sc, 'Vp_b': jnp.zeros((D,), jnp.float32), 'lam': jnp.float32(0.5), 'ff1_w': jax.random.normal(ks[6], (DFF, D), jnp.float32) * sc, 'ff1_b': jnp.zeros((DFF,), jnp.float32), 'ff2_w': jax.random.normal(ks[7], (D, DFF), jnp.float32) * sc, 'ff2_b': jnp.zeros((D,), jnp.float32), 'ln1_g': jnp.ones((D,), jnp.float32), 'ln1_b': jnp.zeros((D,), jnp.float32), 'ln2_g': jnp.ones((D,), jnp.float32), 'ln2_b': jnp.zeros((D,), jnp.float32)}
    _L1_attn_in = _L1_attn_setup()

    def _L1_ffn_setup():
        import jax, jax.numpy as jnp
        import numpy as np
        K = 2
        CAP_FACTOR = 1.25
        key = jax.random.key(seed)
        ks = jax.random.split(key, 6)
        B, T, C, H, E = (8, 256, 128, 512, 8)
        return {'x': jax.random.normal(ks[0], (B, T, C), dtype=jnp.float32), 'Wr': jax.random.normal(ks[1], (C, E), dtype=jnp.float32) * 0.02, 'W1': jax.random.normal(ks[2], (E, C, H), dtype=jnp.float32) * 0.02, 'b1': jax.random.normal(ks[3], (E, H), dtype=jnp.float32) * 0.02, 'W2': jax.random.normal(ks[4], (E, H, C), dtype=jnp.float32) * 0.02, 'b2': jax.random.normal(ks[5], (E, C), dtype=jnp.float32) * 0.02}
    _L1_ffn_in = _L1_ffn_setup()
    _L1_c = _w((lambda *s: np.random.randn(*s).astype(np.float32) * 0.05)(4, 128))
    _L1_wmod = _w((lambda *s: np.random.randn(*s).astype(np.float32) * 0.05)(128, 6 * 128) * 128 ** (-0.5))
    _d = {'L0_attn_x': _L0_attn_in['x'], 'L0_attn_qkv_w': _L0_attn_in['qkv_w'], 'L0_attn_out_w': _L0_attn_in['out_w'], 'L0_attn_out_b': _L0_attn_in['out_b'], 'L0_ffn_router_w': _L0_ffn_in['router_w'], 'L0_ffn_expert_w1': _L0_ffn_in['expert_w1'], 'L0_ffn_expert_b1': _L0_ffn_in['expert_b1'], 'L0_ffn_expert_w2': _L0_ffn_in['expert_w2'], 'L0_ffn_expert_b2': _L0_ffn_in['expert_b2'], 'L0_c': _L0_c, 'L0_wmod': _L0_wmod, 'L1_attn_in_proj_w': _L1_attn_in['in_proj_w'], 'L1_attn_in_proj_b': _L1_attn_in['in_proj_b'], 'L1_attn_out_proj_w': _L1_attn_in['out_proj_w'], 'L1_attn_out_proj_b': _L1_attn_in['out_proj_b'], 'L1_attn_Qp_w': _L1_attn_in['Qp_w'], 'L1_attn_Qp_b': _L1_attn_in['Qp_b'], 'L1_attn_Kp_w': _L1_attn_in['Kp_w'], 'L1_attn_Kp_b': _L1_attn_in['Kp_b'], 'L1_attn_Vp_w': _L1_attn_in['Vp_w'], 'L1_attn_Vp_b': _L1_attn_in['Vp_b'], 'L1_attn_lam': _L1_attn_in['lam'], 'L1_attn_ff1_w': _L1_attn_in['ff1_w'], 'L1_attn_ff1_b': _L1_attn_in['ff1_b'], 'L1_attn_ff2_w': _L1_attn_in['ff2_w'], 'L1_attn_ff2_b': _L1_attn_in['ff2_b'], 'L1_attn_ln1_g': _L1_attn_in['ln1_g'], 'L1_attn_ln1_b': _L1_attn_in['ln1_b'], 'L1_attn_ln2_g': _L1_attn_in['ln2_g'], 'L1_attn_ln2_b': _L1_attn_in['ln2_b'], 'L1_ffn_Wr': _L1_ffn_in['Wr'], 'L1_ffn_W1': _L1_ffn_in['W1'], 'L1_ffn_b1': _L1_ffn_in['b1'], 'L1_ffn_W2': _L1_ffn_in['W2'], 'L1_ffn_b2': _L1_ffn_in['b2'], 'L1_c': _L1_c, 'L1_wmod': _L1_wmod}
    _x0 = _d['L0_attn_x']
    _d['L0_attn_x'] = jax.random.normal(jax.random.fold_in(jax.random.key(seed), 1), (4, 1024, 128), dtype=_x0.dtype)
    del _x0
    return _d

def reference(L0_attn_x, L0_attn_qkv_w, L0_attn_out_w, L0_attn_out_b, L0_ffn_router_w, L0_ffn_expert_w1, L0_ffn_expert_b1, L0_ffn_expert_w2, L0_ffn_expert_b2, L0_c, L0_wmod, L1_attn_in_proj_w, L1_attn_in_proj_b, L1_attn_out_proj_w, L1_attn_out_proj_b, L1_attn_Qp_w, L1_attn_Qp_b, L1_attn_Kp_w, L1_attn_Kp_b, L1_attn_Vp_w, L1_attn_Vp_b, L1_attn_lam, L1_attn_ff1_w, L1_attn_ff1_b, L1_attn_ff2_w, L1_attn_ff2_b, L1_attn_ln1_g, L1_attn_ln1_b, L1_attn_ln2_g, L1_attn_ln2_b, L1_ffn_Wr, L1_ffn_W1, L1_ffn_b1, L1_ffn_W2, L1_ffn_b2, L1_c, L1_wmod):

    def _L0_attn_ref(x, qkv_w, out_w, out_b):
        import jax, jax.numpy as jnp
        import numpy as np
        B, T, C = (4, 256, 128)
        scale = 1.0 / jnp.sqrt(jnp.asarray(x.shape[-1], x.dtype))
        qkv = jnp.einsum('btc,dc->btd', x, qkv_w)
        q, k, v = jnp.split(qkv, 3, axis=-1)
        att = jnp.einsum('btc,bsc->bts', q, k) * scale
        causal = jnp.triu(jnp.ones((x.shape[1], x.shape[1]), dtype=bool), k=1)
        att = jnp.where(causal[None, :, :], jnp.asarray(-jnp.inf, att.dtype), att)
        att = jax.nn.softmax(att, axis=-1)
        out = jnp.einsum('bts,bsc->btc', att, v)
        return jnp.einsum('btc,dc->btd', out, out_w) + out_b

    def _L0_ffn_ref(x, router_w, expert_w1, expert_b1, expert_w2, expert_b2):
        import jax, jax.numpy as jnp
        import numpy as np
        TOP_K = 2
        router_logits = jnp.einsum('bnc,ec->bne', x, router_w)
        router_probs = jax.nn.softmax(router_logits, axis=-1)
        expert_weights, expert_idx = jax.lax.top_k(router_probs, TOP_K)
        expert_weights = expert_weights / (expert_weights.sum(axis=-1, keepdims=True) + 1e-09)
        h = jnp.einsum('bnc,efc->bnef', x, expert_w1) + expert_b1
        h = jax.nn.gelu(h, approximate=False)
        out_all = jnp.einsum('bnef,ecf->bnec', h, expert_w2) + expert_b2
        out_k = jnp.take_along_axis(out_all, expert_idx[..., None], axis=2)
        return (out_k * expert_weights[..., None]).sum(axis=2)

    def _L1_attn_ref(src, in_proj_w, in_proj_b, out_proj_w, out_proj_b, Qp_w, Qp_b, Kp_w, Kp_b, Vp_w, Vp_b, lam, ff1_w, ff1_b, ff2_w, ff2_b, ln1_g, ln1_b, ln2_g, ln2_b):
        import jax, jax.numpy as jnp
        import numpy as np
        import math
        B, S, D, H, R, DFF = (4, 128, 128, 16, 64, 512)

        def _layernorm(x, g, b, eps=1e-05):
            m = jnp.mean(x, axis=-1, keepdims=True)
            v = jnp.var(x, axis=-1, keepdims=True)
            return (x - m) / jnp.sqrt(v + eps) * g + b
        b, s, d = src.shape
        dh = d // H
        qkv = src @ in_proj_w.T + in_proj_b
        q, k, v = jnp.split(qkv, 3, axis=-1)
        q = q.reshape(b, s, H, dh).transpose(0, 2, 1, 3)
        k = k.reshape(b, s, H, dh).transpose(0, 2, 1, 3)
        v = v.reshape(b, s, H, dh).transpose(0, 2, 1, 3)
        scores = jnp.einsum('bhqd,bhkd->bhqk', q, k) / math.sqrt(dh)
        attn = jax.nn.softmax(scores, axis=-1)
        ctx = jnp.einsum('bhqk,bhkd->bhqd', attn, v)
        ctx = ctx.transpose(0, 2, 1, 3).reshape(b, s, d)
        dense_output = ctx @ out_proj_w.T + out_proj_b
        Q = src @ Qp_w.T + Qp_b
        K = src @ Kp_w.T + Kp_b
        V = src @ Vp_w.T + Vp_b
        QK = jnp.einsum('bqr,bkr->bqk', Q, K) / math.sqrt(R)
        aw = jax.nn.softmax(QK, axis=-1)
        kk = max(1, int(s * 0.2))
        topv, topi = jax.lax.top_k(aw, kk)
        bi = jnp.arange(b)[:, None, None]
        si = jnp.arange(s)[None, :, None]
        sparse_attn = jnp.zeros_like(aw).at[bi, si, topi].set(topv)
        sparse_attn = sparse_attn / (jnp.sum(sparse_attn, axis=-1, keepdims=True) + 1e-09)
        sparse_output = jnp.einsum('bqk,bkd->bqd', sparse_attn, V)
        sig = jax.nn.sigmoid(lam)
        fused = sig * dense_output + (1.0 - sig) * sparse_output
        x = _layernorm(src + fused, ln1_g, ln1_b)
        ff = jax.nn.relu(x @ ff1_w.T + ff1_b) @ ff2_w.T + ff2_b
        return _layernorm(x + ff, ln2_g, ln2_b)

    def _L1_ffn_ref(x, Wr, W1, b1, W2, b2):
        import jax, jax.numpy as jnp
        import numpy as np
        K = 2
        CAP_FACTOR = 1.25
        B, T, C = x.shape
        E = Wr.shape[1]
        capacity = int(T / E * CAP_FACTOR)
        probs = jax.nn.softmax(x @ Wr, axis=-1)
        topk_probs, topk_experts = jax.lax.top_k(probs, K)
        S = T * K
        e_flat = topk_experts.reshape(B, S)
        p_flat = topk_probs.reshape(B, S)
        x_rep = jnp.repeat(x, K, axis=1)
        onehot = jax.nn.one_hot(e_flat, E, dtype=jnp.int32)
        pos_all = jnp.cumsum(onehot, axis=1) - onehot
        pos = jnp.take_along_axis(pos_all, e_flat[..., None], axis=-1)[..., 0]
        keep = pos < capacity
        pos_c = jnp.minimum(pos, capacity - 1)
        b_idx = jnp.broadcast_to(jnp.arange(B)[:, None], (B, S))
        buf = jnp.zeros((E, B, capacity, C), dtype=x.dtype)
        buf = buf.at[e_flat, b_idx, pos_c].add(x_rep * keep[..., None].astype(x.dtype))
        h = jax.nn.relu(jnp.einsum('ebnc,ech->ebnh', buf, W1) + b1[:, None, None, :])
        y = jnp.einsum('ebnh,ehc->ebnc', h, W2) + b2[:, None, None, :]
        y_tok = y[e_flat, b_idx, pos_c]
        y_tok = y_tok * keep[..., None].astype(x.dtype) * p_flat[..., None]
        out = y_tok.reshape(B, T, K, C).sum(axis=2)
        return out
    x = L0_attn_x
    mod = (_silu(L0_c) @ L0_wmod).reshape(L0_c.shape[0], 6, 1, -1)
    sa, ca, ga, sb, cb, gb = (mod[:, 0], mod[:, 1], mod[:, 2], mod[:, 3], mod[:, 4], mod[:, 5])
    ga = (2 * (ga >= 0) - 1) * jnp.maximum(jnp.abs(ga), 0.25)
    gb = (2 * (gb >= 0) - 1) * jnp.maximum(jnp.abs(gb), 0.25)
    h = _layernorm(x, axis=-1) * (1 + ca) + sa
    x = x + ga * _L0_attn_ref(h, L0_attn_qkv_w, L0_attn_out_w, L0_attn_out_b)
    h = _layernorm(x, axis=-1) * (1 + cb) + sb
    x = x + gb * _L0_ffn_ref(h, L0_ffn_router_w, L0_ffn_expert_w1, L0_ffn_expert_b1, L0_ffn_expert_w2, L0_ffn_expert_b2)
    mod = (_silu(L1_c) @ L1_wmod).reshape(L1_c.shape[0], 6, 1, -1)
    sa, ca, ga, sb, cb, gb = (mod[:, 0], mod[:, 1], mod[:, 2], mod[:, 3], mod[:, 4], mod[:, 5])
    ga = (2 * (ga >= 0) - 1) * jnp.maximum(jnp.abs(ga), 0.25)
    gb = (2 * (gb >= 0) - 1) * jnp.maximum(jnp.abs(gb), 0.25)
    h = _layernorm(x, axis=-1) * (1 + ca) + sa
    x = x + ga * _L1_attn_ref(h, L1_attn_in_proj_w, L1_attn_in_proj_b, L1_attn_out_proj_w, L1_attn_out_proj_b, L1_attn_Qp_w, L1_attn_Qp_b, L1_attn_Kp_w, L1_attn_Kp_b, L1_attn_Vp_w, L1_attn_Vp_b, L1_attn_lam, L1_attn_ff1_w, L1_attn_ff1_b, L1_attn_ff2_w, L1_attn_ff2_b, L1_attn_ln1_g, L1_attn_ln1_b, L1_attn_ln2_g, L1_attn_ln2_b)
    h = _layernorm(x, axis=-1) * (1 + cb) + sb
    x = x + gb * _L1_ffn_ref(h, L1_ffn_Wr, L1_ffn_W1, L1_ffn_b1, L1_ffn_W2, L1_ffn_b2)
    return x

_drawn_inputs = setup_inputs


def setup_inputs(seed=0):
    import zlib

    import numpy as np

    out = dict(_drawn_inputs(seed))
    spreads = {'L0_attn_out_b': (0.0, 0.281),
     'L0_ffn_expert_b1': (0.0, 0.555),
     'L0_ffn_expert_b2': (0.0, 0.442),
     'L1_attn_in_proj_b': (0.0, 0.8),
     'L1_attn_out_proj_b': (0.0, 0.514),
     'L1_attn_Qp_b': (0.0, 0.8),
     'L1_attn_Kp_b': (0.0, 2.0),
     'L1_attn_Vp_b': (0.0, 0.767),
     'L1_attn_ff1_b': (0.0, 0.8),
     'L1_attn_ff2_b': (0.0, 0.331),
     'L1_attn_ln1_g': (1.0, 0.2),
     'L1_attn_ln1_b': (0.0, 0.376),
     'L1_attn_ln2_g': (1.0, 0.2),
     'L1_attn_ln2_b': (0.0, 0.297)}
    factors = {'L1_attn_in_proj_w': 8.0,
     'L1_attn_out_proj_w': 8.0,
     'L1_attn_Qp_w': 8.0,
     'L1_attn_Kp_w': 8.0,
     'L1_attn_Vp_w': 8.0,
     'L1_attn_ff1_w': 3.821,
     'L1_attn_ff2_w': 3.006,
     'L1_ffn_Wr': 8.0,
     'L1_ffn_W1': 8.0,
     'L1_ffn_b1': 8.0,
     'L1_ffn_W2': 8.0,
     'L1_ffn_b2': 26.897}
    for name, (base, spread) in spreads.items():
        noise = np.random.default_rng([zlib.crc32(name.encode()), seed]).standard_normal(out[name].shape)
        drawn = base * np.exp(spread * noise) if base else spread * noise
        out[name] = jnp.asarray(drawn.astype(out[name].dtype))
    for name, factor in factors.items():
        out[name] = (out[name] * factor).astype(out[name].dtype)
    return out
```

```python
from contextlib import ExitStack

import numpy as np

import concourse.bass as bass
from concourse import mybir

ALU = mybir.AluOpType
ACT = mybir.ActivationFunctionType
AX = mybir.AxisListType
F32 = mybir.dt.float32
BF16 = mybir.dt.bfloat16
I32 = mybir.dt.int32

P = 128
B, T, C = 4, 1024, 128
NT = T // P
TILES = B * NT
E, FF = 8, 512
RQ = 64
FC = FF // P
LN_EPS = 1e-5

W_QKV0, W_OUT0 = 0, 3
W_UP0 = 4
W_DOWN0 = W_UP0 + E * FC
W_QKV1 = W_DOWN0 + E * FC
W_OUT1 = W_QKV1 + 3
W_QK1 = W_OUT1 + 1
W_ROUTER0 = W_QK1 + 1
W_V1 = W_ROUTER0 + 1
W_FF1 = W_V1 + 1
W_FF2 = W_FF1 + FC
W_BIAS = W_FF2 + FC
W_SLOTS = W_BIAS + 1
W_SLOTS_L0 = W_QKV1

B_UP0, B_UP1, B_FF1, B_Q1, B_K1, B_SQ1, B_SK1 = 0, E * FC, 2 * E * FC, 2 * E * FC + FC, 2 * E * FC + FC + 1, 2 * E * FC + FC + 2, 2 * E * FC + FC + 3
CAPACITY = int(T / E * 1.25)

SA, CA, GA, SB, CB, GB = range(6)


class Alloc:

    def __init__(self, nc, ctx, tag=""):
        self.nc, self.ctx, self.tag = nc, ctx, tag
        self.sems = []

    def sb(self, name, shape, dt=F32):
        return self.ctx.enter_context(self.nc.sbuf_tensor(name + self.tag, shape, dt))

    def ps(self, name, shape, dt=F32):
        return self.ctx.enter_context(self.nc.psum_tensor(name + self.tag, shape, dt))

    def sem(self, name):
        self.sems.append(self.ctx.enter_context(self.nc.semaphore(name + self.tag)))
        return self.sems[-1]

    def clear_sems(self):
        nums = sorted(s.num for s in self.sems)
        firsts = [n for n in nums if n - 1 not in nums]
        lasts = [n for n in nums if n + 1 not in nums]
        with self.nc.Block() as block:

            @block.gpsimd
            def _(pool):
                for first, last in zip(firsts, lasts):
                    pool.sem_clear(range(first, last + 1))


class Steps:

    def __init__(self, eng, sem):
        self.eng, self.sem, self.n = eng, sem, 0

    def __call__(self, ins):
        self.n += 1
        return ins.then_inc(self.sem, 1)

    def settle(self):
        self.eng.wait_ge(self.sem, self.n)

    def again(self):
        self.settle()
        self.eng.sem_clear(self.sem)


def bc(ap, n):
    return ap.unsqueeze(1).to_broadcast([ap.shape[0], n, ap.shape[1]])


def setup(nc, g, dram):
    with ExitStack() as ctx:
        a = Alloc(nc, ctx)
        nat = a.sb("weights_natural", [P, W_SLOTS, P])
        wmod = a.sb("wmod", [P, 2, 6 * C])
        cond = a.sb("cond", [2 * B, C])
        cond_t = a.sb("cond_t", [P, 2 * B])
        cond_e = a.sb("cond_e", [P, 2 * B])
        silu = a.sb("silu", [P, 2 * B])
        silu_b = a.sb("silu_b", [P, 2 * B, P])
        gate_sign = a.sb("gate_sign", [P, 2, 2 * B, C])
        weight_ps = [a.ps(f"weight_ps{i}", [P, 4, P]) for i in range(4)]
        mod_ps = [a.ps(f"mod_ps{i}", [P, 512]) for i in range(4)]
        cond_loaded = a.sem("cond_loaded")
        w0_loaded = a.sem("w0_loaded")
        w1_loaded = a.sem("w1_loaded")
        x_loaded = a.sem("x_loaded")
        rows_loaded = a.sem("rows_loaded")
        zeroed = a.sem("zeroed")
        ident_ready = a.sem("ident_ready")
        turned = a.sem("turned")
        kept_act = a.sem("kept_act")
        kept_dve = a.sem("kept_dve")
        cond_turned = a.sem("cond_turned")
        cond_kept = a.sem("cond_kept")
        cond_exp = a.sem("cond_exp")
        silu_ready = a.sem("silu_ready")
        mod_ready = a.sem("mod_ready")
        mod_kept = a.sem("mod_kept")
        vec = a.sem("setup_vec")
        GROUPS = -(-W_SLOTS // 4)
        W0_GROUPS = W_SLOTS_L0 // 4
        MODS = 2 * B * 2
        HALF = 3 * C

        def group(i):
            return 4 * i, min(4, W_SLOTS - 4 * i)

        with nc.Block() as block:

            @block.sync
            def _(sp):
                for half in range(2):
                    sp.dma_start(cond[half * B : half * B + B, :], dram[f"L{half}_c"]).then_inc(cond_loaded, 16)
                sp.dma_start(nat[:, W_QKV0 : W_QKV0 + 3, :], dram["L0_attn_qkv_w"].rearrange("(n p) c -> p n c", p=P)).then_inc(w0_loaded, 16)
                sp.dma_start(nat[:, W_OUT0, :], dram["L0_attn_out_w"]).then_inc(w0_loaded, 16)
                sp.dma_start(
                    nat[:, W_UP0 : W_UP0 + E * FC, :], dram["L0_ffn_expert_w1"].rearrange("e (k p) c -> p (e k) c", p=P)
                ).then_inc(w0_loaded, 16)
                sp.dma_start(
                    nat[:, W_DOWN0 : W_DOWN0 + E * FC, :].rearrange("p (e k) f -> p e (k f)", e=E),
                    dram["L0_ffn_expert_w2"].rearrange("e c f -> c e f"),
                ).then_inc(w0_loaded, 16)
                for half in range(2):
                    sp.dma_start(wmod[:, half, :], dram[f"L{half}_wmod"]).then_inc(cond_loaded, 16)
                sp.dma_start(g.x[:], dram["L0_attn_x"].rearrange("b (n p) c -> p (b n) c", p=P)).then_inc(x_loaded, 16)
                sp.wait_ge(x_loaded, 16)

            @block.gpsimd
            def _(pool):
                pool.memset(nat[:, W_ROUTER0, :], 0.0).then_inc(zeroed, 1)
                pool.memset(nat[:, W_BIAS, :], 0.0).then_inc(zeroed, 1)
                pool.memset(g.ident[:], 0.0).then_inc(zeroed, 1)
                pool.memset(g.causal[:], 0.0).then_inc(zeroed, 1)
                pool.memset(g.minus_half[:], -0.5)
                for e in range(E):
                    pool.memset(g.expert_rank[:, e : e + 1], float(E - e))
                pool.memset(g.ones_b[:], 1.0).then_inc(zeroed, 1)
                pool.wait_ge(zeroed, 5)
                pool.affine_select(
                    out=g.ident[:], in_=g.ident[:], compare_op=ALU.not_equal, fill=1.0, base=0, pattern=[[-1, P]], channel_multiplier=1
                ).then_inc(ident_ready, 1)
                pool.affine_select(
                    out=g.causal[:], in_=g.causal[:], compare_op=ALU.is_ge, fill=-1e30, base=0, pattern=[[-1, P]], channel_multiplier=1
                )
                pool.affine_select(
                    out=g.before[:], in_=g.ones_b[:], compare_op=ALU.is_gt, fill=0.0, base=0, pattern=[[1, P]], channel_multiplier=-1
                )

            @block.scalar
            def _(act):
                act.wait_ge(zeroed, 2)
                act.dma_start(nat[0:E, W_ROUTER0, :], dram["L0_ffn_router_w"]).then_inc(w1_loaded, 16)
                act.dma_start(nat[:, W_QKV1 : W_QKV1 + 3, :], dram["L1_attn_in_proj_w"].rearrange("(n p) c -> p n c", p=P)).then_inc(w1_loaded, 16)
                act.dma_start(nat[:, W_OUT1, :], dram["L1_attn_out_proj_w"]).then_inc(w1_loaded, 16)
                act.dma_start(nat[0:RQ, W_QK1, :], dram["L1_attn_Qp_w"]).then_inc(w1_loaded, 16)
                act.dma_start(nat[RQ : 2 * RQ, W_QK1, :], dram["L1_attn_Kp_w"]).then_inc(w1_loaded, 16)
                act.dma_start(nat[:, W_V1, :], dram["L1_attn_Vp_w"]).then_inc(w1_loaded, 16)
                act.dma_start(nat[:, W_FF1 : W_FF1 + FC, :], dram["L1_attn_ff1_w"].rearrange("(k p) c -> p k c", p=P)).then_inc(w1_loaded, 16)
                act.dma_start(nat[:, W_FF2 : W_FF2 + FC, :].rearrange("p k f -> p (k f)"), dram["L1_attn_ff2_w"]).then_inc(w1_loaded, 16)
                bias = nat[:, W_BIAS, :]
                act.dma_start(bias[B_UP0 : B_UP0 + E * FC, :], dram["L0_ffn_expert_b1"].rearrange("e (k p) -> (e k) p", p=P)).then_inc(w1_loaded, 16)
                act.dma_start(bias[B_UP1 : B_UP1 + E * FC, :], dram["L1_ffn_b1"].rearrange("e (k p) -> (e k) p", p=P)).then_inc(w1_loaded, 16)
                act.dma_start(bias[B_FF1 : B_FF1 + FC, :], dram["L1_attn_ff1_b"].rearrange("(k p) -> k p", p=P)).then_inc(w1_loaded, 16)
                act.dma_start(bias[B_Q1 : B_Q1 + 2, :], dram["L1_attn_in_proj_b"][0 : 2 * C].rearrange("(k p) -> k p", p=P)).then_inc(w1_loaded, 16)
                act.dma_start(bias[B_SQ1 : B_SQ1 + 1, 0:RQ], dram["L1_attn_Qp_b"].rearrange("(a r) -> a r", a=1)).then_inc(w1_loaded, 16)
                act.dma_start(bias[B_SK1 : B_SK1 + 1, 0:RQ], dram["L1_attn_Kp_b"].rearrange("(a r) -> a r", a=1)).then_inc(w1_loaded, 16)
                for dst, src in g.small_loads(dram):
                    act.dma_start(dst, src).then_inc(rows_loaded, 16)
                act.wait_ge(cond_kept, 1)
                act.activation(cond_e[:], cond_t[:], ACT.Exp, scale=-1.0).then_inc(cond_exp, 1)
                for i in range(0, GROUPS, 2):
                    first, n = group(i)
                    act.wait_ge(turned, i + 1)
                    act.activation(g.weights(first, n), weight_ps[i % 4][:, 0:n, :], ACT.Copy).then_inc(kept_act, 1)
                for i in range(MODS):
                    col, part = i // 2, i % 2
                    act.wait_ge(mod_ready, i + 1)
                    act.activation(g.mod[:, col, part * HALF : part * HALF + HALF], mod_ps[i % 4][:, 0:HALF], ACT.Copy).then_inc(mod_kept, 1)
                act.wait_ge(rows_loaded, 16 * len(g.small_loads(dram)))

            @block.vector
            def _(dve):
                step = Steps(dve, vec)
                dve.wait_ge(cond_turned, 1)
                step(dve.tensor_copy(cond_t[:], mod_ps[0][:, 0 : 2 * B]))
                step.settle()
                dve.tensor_copy(cond_t[:], cond_t[:]).then_inc(cond_kept, 1)
                dve.wait_ge(cond_exp, 1)
                step(dve.tensor_scalar(cond_e[:], cond_e[:], 1.0, None, ALU.add))
                step.settle()
                step(dve.reciprocal(cond_e[:], cond_e[:]))
                step.settle()
                step(dve.tensor_tensor(silu[:], cond_t[:], cond_e[:], ALU.mult))
                step.settle()
                dve.tensor_copy(silu_b[:], silu[:].unsqueeze(2).to_broadcast([P, 2 * B, P])).then_inc(silu_ready, 1)
                for i in range(1, GROUPS, 2):
                    first, n = group(i)
                    dve.wait_ge(turned, i + 1)
                    dve.tensor_copy(g.weights(first, n), weight_ps[i % 4][:, 0:n, :]).then_inc(kept_dve, 1)
                dve.wait_ge(mod_kept, MODS)
                for part in (CA, CB):
                    v = g.mod[:, :, part * C : part * C + C]
                    step(dve.tensor_scalar(v, v, 1.0, None, ALU.add))
                for k, part in enumerate((GA, GB)):
                    v, s = g.mod[:, :, part * C : part * C + C], gate_sign[:, k]
                    step(dve.tensor_scalar(s, v, 0.0, 2.0, ALU.is_ge, ALU.mult))
                    step.settle()
                    step(dve.tensor_scalar(s, s, -1.0, None, ALU.add))
                    step.settle()
                    step(dve.tensor_tensor(v, v, s, ALU.mult))
                    step.settle()
                    step(dve.scalar_tensor_tensor(out=v, in0=v, scalar=0.25, in1=s, op0=ALU.max, op1=ALU.mult))

            @block.tensor
            def _(pe):
                pe.wait_ge(ident_ready, 1)
                pe.wait_ge(cond_loaded, 64)
                pe.transpose(mod_ps[0][:, 0 : 2 * B], cond[:], g.ident[0 : 2 * B, 0 : 2 * B]).then_inc(cond_turned, 1)
                for i in range(GROUPS):
                    if i == 0:
                        pe.wait_ge(w0_loaded, 64)
                    if i == W0_GROUPS:
                        pe.wait_ge(w1_loaded, 224)
                    if i >= 4:
                        pe.wait_ge(kept_dve if i % 2 else kept_act, (i - 4) // 2 + 1)
                    first, n = group(i)
                    for k in range(n):
                        ins = pe.transpose(weight_ps[i % 4][:, k, :], nat[:, first + k, :], g.ident[:])
                    ins.then_inc(turned, 1)
                pe.wait_ge(silu_ready, 1)
                for i in range(MODS):
                    col, part = i // 2, i % 2
                    if i >= 4:
                        pe.wait_ge(mod_kept, i - 3)
                    pe.matmul(
                        mod_ps[i % 4][:, 0:HALF], silu_b[:, col, :], wmod[:, col // B, part * HALF : part * HALF + HALF], start=True, stop=True
                    ).then_inc(mod_ready, 1)
        a.clear_sems()


def layer_norm(dve, step, st, rows, out, scale, rstd_wait):
    for n in range(NT):
        step(dve.bn_stats(st.stats[:, n, :], rows[:, n, :]))
    step.settle()
    for n in range(NT):
        step(dve.bn_aggr(st.mean_var[:, n, :], st.stats[:, n, :]))
    step.settle()
    dve.tensor_scalar(st.var_eps[:], st.mean_var[:, :, 1], LN_EPS, None, ALU.add).then_inc(st.var_ready, 1)
    rstd_wait()
    for n in range(NT):
        step(
            dve.tensor_scalar(
                out[:, n, :], rows[:, n, :], st.mean_var[:, n, 0:1], st.rstd[:, n : n + 1], ALU.subtract, ALU.mult
            )
        )
    step.settle()
    step(dve.tensor_tensor(out, out, scale, ALU.mult))
    step.settle()


class Norm:

    def __init__(self, a, name, minus_half):
        self.stats = a.sb(f"{name}_stats", [P, NT, 6])
        self.mean_var = a.sb(f"{name}_mean_var", [P, NT, 2])
        self.var_eps = a.sb(f"{name}_var_eps", [P, NT])
        self.rstd = a.sb(f"{name}_rstd", [P, NT])
        self.var_ready = a.sem(f"{name}_var_ready")
        self.rstd_ready = a.sem(f"{name}_rstd_ready")
        self.minus_half = minus_half

    def pool(self, pool, n):
        pool.wait_ge(self.var_ready, n)
        pool.tensor_tensor(self.rstd[:], self.var_eps[:], self.minus_half[:, 0:NT], ALU.pow).then_inc(self.rstd_ready, 1)


def causal_attention(nc, g, dram):
    SCALE = float(C) ** -0.5
    with ExitStack() as ctx:
        a = Alloc(nc, ctx)
        norm = Norm(a, "ln0", g.minus_half)
        h = a.sb("h0", [P, NT, C])
        h_t = a.sb("h0_t", [P, T])
        q_t = a.sb("q0_t", [P, T])
        k_t = a.sb("k0_t", [P, T])
        v = a.sb("v0", [P, NT, C])
        probs = a.sb("probs0", [P, 2, T])
        probs_t = a.sb("probs0_t", [P, NT, P])
        ctx_t = a.sb("ctx0_t", [P, 2, P])
        mx = a.sb("max0", [P, 2])
        nmx = a.sb("minus_max0", [P, 2])
        total = a.sb("total0", [P, NT])
        inv = a.sb("inv0", [P, 2])
        o = a.sb("o0", [P, 2, C])
        scores_ps = [a.ps(f"scores0_ps{i}", [P, T]) for i in range(2)]
        turn_ps = a.ps("turn0_ps", [P, T])
        ctx_ps = a.ps("ctx0_ps", [P, 512])
        out_ps = a.ps("out0_ps", [P, 512])
        vec = a.sem("attn0_vec")
        h_ready = a.sem("h0_ready")
        h_turned = a.sem("h0_turned")
        h_t_ready = a.sem("h0_t_ready")
        q_made = a.sem("q0_made")
        k_made = a.sem("k0_made")
        v_made = a.sem("v0_made")
        q_ready = a.sem("q0_ready")
        k_ready = a.sem("k0_ready")
        v_ready = a.sem("v0_ready")
        scored = a.sem("scored0")
        max_ready = a.sem("max0_ready")
        probs_ready = a.sem("probs0_ready")
        probs_turned = a.sem("probs0_turned")
        probs_t_act = a.sem("probs0_t_act")
        probs_t_dve = a.sem("probs0_t_dve")
        ctx_made = a.sem("ctx0_made")
        ctx_ready = a.sem("ctx0_ready")
        out_made = a.sem("out0_made")
        out_used = a.sem("out0_used")
        H = NT // 2

        with nc.Block() as block:

            @block.gpsimd
            def _(pool):
                with pool.Fori(0, B) as b:
                    norm.pool(pool, b + 1)

            @block.vector
            def _(dve):
                with dve.Fori(0, B) as b:
                    step = Steps(dve, vec)
                    rows = g.x[:, bass.ds(b * NT, NT), :]
                    layer_norm(dve, step, norm, rows, h[:], g.mod_row(0, b, CA), lambda: dve.wait_ge(norm.rstd_ready, b + 1))
                    dve.tensor_tensor(h[:], h[:], g.mod_row(0, b, SA), ALU.add).then_inc(h_ready, 1)
                    dve.wait_ge(k_made, b + 1)
                    dve.tensor_copy(k_t[:], scores_ps[1][:]).then_inc(k_ready, 1)

                    def row_max(i):
                        n = (i + 1) * P
                        s = scores_ps[i % 2]
                        dve.wait_ge(scored, b * NT + i + 1)
                        step(dve.tensor_tensor(s[:, n - P : n], s[:, n - P : n], g.causal[:], ALU.add))
                        step.settle()
                        step(dve.reduce_max(mx[:, i % 2 : i % 2 + 1], s[:, 0:n], AX.X))
                        step.settle()
                        dve.tensor_scalar(nmx[:, i % 2 : i % 2 + 1], mx[:, i % 2 : i % 2 + 1], -SCALE, None, ALU.mult).then_inc(max_ready, 1)

                    def keep_probs(i):
                        if i >= H:
                            dve.wait_ge(probs_turned, b * NT + i + 1)
                            dve.tensor_copy(
                                probs_t[:, H : i + 1, :], turn_ps[:, H * P : (i + 1) * P].rearrange("p (n c) -> p n c", c=P)
                            ).then_inc(probs_t_dve, 1)

                    def residual(i):
                        one = slice(i % 2, i % 2 + 1)
                        dve.wait_ge(out_made, b * NT + i + 1)
                        step(dve.reciprocal(inv[:, one], total[:, i : i + 1]))
                        step.settle()
                        dve.scalar_tensor_tensor(
                            out=o[:, i % 2, :], in0=out_ps[:, 0:C], scalar=inv[:, one], in1=g.row("L0_attn_out_b"), op0=ALU.mult, op1=ALU.add
                        ).then_inc(out_used, 1)
                        dve.wait_ge(out_used, b * NT + i + 1)
                        step(dve.tensor_tensor(o[:, i % 2, :], o[:, i % 2, :], g.mod_part(0, b, GA), ALU.mult))
                        step.settle()
                        xr = g.x[:, bass.ds(b * NT + i, 1), :].rearrange("p n c -> p (n c)")
                        step(dve.tensor_tensor(xr, xr, o[:, i % 2, :], ALU.add))

                    row_max(0)
                    for i in range(NT):
                        if i + 1 < NT:
                            row_max(i + 1)
                        keep_probs(i)
                        if i >= 1:
                            residual(i - 1)
                    residual(NT - 1)
                    step.again()

            @block.scalar
            def _(act):
                with act.Fori(0, B) as b:
                    for k in range(2):
                        act.wait_ge(h_turned, b * 2 + k + 1)
                        act.activation(h_t[:, k * 512 : k * 512 + 512], turn_ps[:, k * 512 : k * 512 + 512], ACT.Copy).then_inc(h_t_ready, 1)
                    act.wait_ge(q_made, b + 1)
                    act.activation(q_t[:], scores_ps[0][:], ACT.Copy).then_inc(q_ready, 1)
                    act.wait_ge(v_made, b + 1)
                    act.activation(v[:], turn_ps[:].rearrange("p (n c) -> p n c", c=C), ACT.Copy).then_inc(v_ready, 1)

                    def exp(i):
                        one = slice(i % 2, i % 2 + 1)
                        n = (i + 1) * P
                        act.wait_ge(max_ready, b * NT + i + 1)
                        act.activation(
                            probs[:, i % 2, 0:n], scores_ps[i % 2][:, 0:n], ACT.Exp, bias=nmx[:, one], scale=SCALE, accum_out=total[:, i : i + 1]
                        ).then_inc(probs_ready, 1)

                    exp(0)
                    for i in range(NT):
                        m = min(i + 1, H)
                        act.wait_ge(probs_turned, b * NT + i + 1)
                        act.activation(probs_t[:, 0:m, :], turn_ps[:, 0 : m * P].rearrange("p (n c) -> p n c", c=P), ACT.Copy).then_inc(probs_t_act, 1)
                        if i + 1 < NT:
                            exp(i + 1)
                        act.wait_ge(ctx_made, b * NT + i + 1)
                        act.activation(ctx_t[:, i % 2, :], ctx_ps[:, 0:P], ACT.Copy).then_inc(ctx_ready, 1)

            @block.tensor
            def _(pe):
                with pe.Fori(0, B) as b:
                    pe.wait_ge(h_ready, b + 1)
                    for n in range(NT):
                        ins = pe.transpose(turn_ps[:, n * P : n * P + P], h[:, n, :], g.ident[:])
                        if n % H == H - 1:
                            ins.then_inc(h_turned, 1)
                    for k in range(2):
                        cols = slice(k * 512, k * 512 + 512)
                        pe.wait_ge(h_t_ready, b * 2 + k + 1)
                        q_ins = pe.matmul(scores_ps[0][:, cols], g.weights(W_QKV0), h_t[:, cols], start=True, stop=True)
                        if k == 1:
                            q_ins.then_inc(q_made, 1)
                        k_ins = pe.matmul(scores_ps[1][:, cols], g.weights(W_QKV0 + 1), h_t[:, cols], start=True, stop=True)
                        if k == 1:
                            k_ins.then_inc(k_made, 1)
                    for n in range(NT):
                        ins = pe.matmul(turn_ps[:, n * P : n * P + P], h_t[:, n * P : n * P + P], g.weights(W_QKV0 + 2), start=True, stop=True)
                    ins.then_inc(v_made, 1)
                    pe.wait_ge(q_ready, b + 1)
                    pe.wait_ge(k_ready, b + 1)

                    def score(i):
                        n = (i + 1) * P
                        if i >= 2:
                            pe.wait_ge(probs_ready, b * NT + i - 1)
                        for c0 in range(0, n, 512):
                            c1 = min(n, c0 + 512)
                            ins = pe.matmul(scores_ps[i % 2][:, c0:c1], q_t[:, i * P : i * P + P], k_t[:, c0:c1], start=True, stop=True)
                        ins.then_inc(scored, 1)

                    def project(i):
                        pe.wait_ge(ctx_ready, b * NT + i + 1)
                        if i >= 1:
                            pe.wait_ge(out_used, b * NT + i)
                        pe.matmul(out_ps[:, 0:C], ctx_t[:, i % 2, :], g.weights(W_OUT0), start=True, stop=True).then_inc(out_made, 1)

                    score(0)
                    pe.wait_ge(v_ready, b + 1)
                    for i in range(NT):
                        if i + 1 < NT:
                            score(i + 1)
                        pe.wait_ge(probs_ready, b * NT + i + 1)
                        for n in range(i + 1):
                            ins = pe.transpose(turn_ps[:, n * P : n * P + P], probs[:, i % 2, n * P : n * P + P], g.ident[:])
                        ins.then_inc(probs_turned, 1)
                        if i >= 1:
                            project(i - 1)
                        pe.wait_ge(probs_t_act, b * NT + i + 1)
                        if i >= H:
                            pe.wait_ge(probs_t_dve, b * H + i - H + 1)
                        for n in range(i + 1):
                            ins = pe.matmul(ctx_ps[:, 0:P], v[:, n, :], probs_t[:, n, :], start=(n == 0), stop=(n == i))
                        ins.then_inc(ctx_made, 1)
                    project(NT - 1)
        a.clear_sems()


def route(nc, g, moe, dram, layer):
    with ExitStack() as ctx:
        a = Alloc(nc, ctx, f"_{layer}")
        norm = Norm(a, f"ln_moe{layer}", g.minus_half)
        h = a.sb("moe_h", [P, NT, C])
        h_t = a.sb("moe_h_t_batch", [P, T])
        logits = a.sb("logits", [P, NT, E])
        expl = a.sb("exp_logits", [P, NT, E])
        first = a.sb("first_choice", [P, NT, E])
        second = a.sb("second_choice", [P, NT, E])
        sel = a.sb("selected", [P, NT, E])
        sel_b = a.sb("selected_bf16", [P, NT, E], BF16)
        m1 = a.sb("best_logit", [P, NT])
        m2 = a.sb("next_logit", [P, NT])
        rank = a.sb("best_rank", [P, NT])
        total = a.sb("total_exp", [P, NT])
        share = a.sb("share", [P, NT])
        turn_ps = a.ps("moe_turn_ps", [P, T])
        logits_ps = a.ps("logits_ps", [P, 512])
        pos_ps = a.ps("pos_ps", [P, 512])
        vec = a.sem("route_vec")
        h_ready = a.sem("moe_h_ready")
        h_turned = a.sem("moe_h_turned")
        h_t_ready = a.sem("moe_h_t_ready")
        h_t_stored = a.sem("moe_h_t_stored")
        scored = a.sem("logits_made")
        shifted = a.sem("logits_shifted")
        exp_ready = a.sem("logits_exp")
        sel_ready = a.sem("selected_ready")
        pos_made = a.sem("pos_made")
        loaded = a.sem("moe_loaded")
        H = NT // 2

        def tall(ap):
            return ap.unsqueeze(2).to_broadcast([P, NT, E])

        with nc.Block() as block:

            @block.sync
            def _(sp):
                for dst, src in moe.loads(dram):
                    sp.dma_start(dst, src).then_inc(loaded, 16)
                sp.wait_ge(loaded, 16 * len(moe.loads(dram)))

            @block.gpsimd
            def _(pool):
                with pool.Fori(0, B) as b:
                    norm.pool(pool, b + 1)
                    pool.wait_ge(h_t_ready, 2 * b + 2)
                    pool.tensor_copy(moe.h_t[:, bass.ds(b * T, T)], h_t[:]).then_inc(h_t_stored, 1)

            @block.vector
            def _(dve):
                with dve.Fori(0, B) as b:
                    step = Steps(dve, vec)
                    rows = g.x[:, bass.ds(b * NT, NT), :]
                    layer_norm(dve, step, norm, rows, h[:], g.mod_row(layer, b, CB), lambda: dve.wait_ge(norm.rstd_ready, b + 1))
                    dve.tensor_tensor(h[:], h[:], g.mod_row(layer, b, SB), ALU.add).then_inc(h_ready, 1)
                    dve.wait_ge(scored, b + 1)
                    step(dve.tensor_copy(logits[:].rearrange("p n e -> p (n e)"), logits_ps[:, 0 : NT * E]))
                    step.settle()
                    step(dve.reduce_max(m1[:], logits[:], AX.X))
                    step.settle()
                    dve.tensor_tensor(expl[:], logits[:], tall(m1[:]), ALU.subtract).then_inc(shifted, 1)

                    def choose(chosen, of, best):
                        step(dve.tensor_tensor(chosen[:], of[:], tall(best[:]), ALU.is_equal))
                        step.settle()
                        step(dve.tensor_tensor(chosen[:], chosen[:], bc(g.expert_rank[:], NT), ALU.mult))
                        step.settle()
                        step(dve.reduce_max(rank[:], chosen[:], AX.X))
                        step.settle()
                        step(dve.tensor_tensor(chosen[:], chosen[:], tall(rank[:]), ALU.is_equal))
                        step.settle()

                    choose(first, logits, m1)
                    step(dve.scalar_tensor_tensor(out=sel[:], in0=first[:], scalar=-1e30, in1=logits[:], op0=ALU.mult, op1=ALU.add))
                    step.settle()
                    step(dve.reduce_max(m2[:], sel[:], AX.X))
                    step.settle()
                    choose(second, sel, m2)
                    step(dve.tensor_tensor(sel[:], first[:], second[:], ALU.add))
                    step.settle()
                    if layer == 1:
                        dve.tensor_copy(sel_b[:], sel[:]).then_inc(sel_ready, 1)
                    dve.wait_ge(exp_ready, b + 1)
                    step(dve.reduce_sum(total[:], expl[:], AX.X))
                    step(dve.tensor_tensor(first[:], expl[:], sel[:], ALU.mult))
                    step.settle()
                    if layer == 0:
                        step(dve.reduce_sum(share[:], first[:], AX.X))
                        step.settle()
                        step(dve.scalar_tensor_tensor(out=total[:], in0=total[:], scalar=1e-9, in1=share[:], op0=ALU.mult, op1=ALU.add))
                        step.settle()
                    else:
                        dve.wait_ge(pos_made, b + 1)
                        step(
                            dve.scalar_tensor_tensor(
                                out=first[:], in0=pos_ps[:, 0 : NT * E].rearrange("p (n e) -> p n e", e=E), scalar=float(CAPACITY), in1=first[:], op0=ALU.is_lt, op1=ALU.mult
                            )
                        )
                    step(dve.reciprocal(share[:], total[:]))
                    step.settle()
                    step(dve.tensor_tensor(moe.gates[:, bass.ds(b * NT, NT), :], first[:], tall(share[:]), ALU.mult))
                    step.again()

            @block.scalar
            def _(act):
                with act.Fori(0, B) as b:
                    for k in range(2):
                        act.wait_ge(h_turned, b * 2 + k + 1)
                        act.activation(h_t[:, k * 512 : k * 512 + 512], turn_ps[:, k * 512 : k * 512 + 512], ACT.Copy).then_inc(h_t_ready, 1)
                    act.wait_ge(shifted, b + 1)
                    act.activation(expl[:], expl[:], ACT.Exp).then_inc(exp_ready, 1)
                    act.wait_ge(h_t_stored, b + 1)

            @block.tensor
            def _(pe):
                router = g.weights(W_ROUTER0)[:, 0:E] if layer == 0 else g.wr1[:]
                with pe.Fori(0, B) as b:
                    pe.wait_ge(h_ready, b + 1)
                    for n in range(NT):
                        ins = pe.transpose(turn_ps[:, n * P : n * P + P], h[:, n, :], g.ident[:])
                        if n % H == H - 1:
                            ins.then_inc(h_turned, 1)
                    pe.wait_ge(h_t_ready, b * 2 + 2)
                    for n in range(NT):
                        ins = pe.matmul(logits_ps[:, n * E : n * E + E], h_t[:, n * P : n * P + P], router, start=True, stop=True)
                    ins.then_inc(scored, 1)
                    if layer == 1:
                        pe.wait_ge(sel_ready, b + 1)
                        for n in range(NT):
                            for m in range(n + 1):
                                ins = pe.matmul(
                                    pos_ps[:, n * E : n * E + E], g.before[:] if m == n else g.ones_b[:], sel_b[:, m, :], start=(m == 0), stop=(m == n)
                                )
                        ins.then_inc(pos_made, 1)


def experts(nc, g, moe, layer):
    TB = 512
    NB = TB // P
    kind = ACT.Gelu if layer == 0 else ACT.Relu
    with ExitStack() as ctx:
        a = Alloc(nc, ctx, f"_{layer}")
        hidden = a.sb("hidden", [P, 2, FC, TB])
        acc = a.sb("moe_acc", [P, NB, C])
        up_ps = [a.ps(f"up_ps{k}", [P, TB]) for k in range(FC)]
        down_ps = [a.ps(f"down_ps{k}", [P, NB, C]) for k in range(2)]
        vec = a.sem("experts_vec")
        up_made = a.sem("up_made")
        hidden_ready = a.sem("hidden_ready")
        down_made = a.sem("down_made")
        down_used = a.sem("down_used")
        up, down, b2 = moe.up_weights, moe.down_weights, moe.b2
        bias0 = B_UP0 if layer == 0 else B_UP1

        with nc.Block() as block:

            @block.vector
            def _(dve):
                with dve.Fori(0, B * T // TB) as i:
                    step = Steps(dve, vec)
                    step(dve.memset(acc[:], 0.0))
                    step.settle()
                    gate = lambda e, n: moe.gates[:, bass.ds(i * NB + n, 1), e : e + 1].rearrange("p n e -> p (n e)")
                    for e in range(E):
                        for n in range(NB):
                            step(dve.scalar_tensor_tensor(out=acc[:, n, :], in0=b2[:, e, :], scalar=gate(e, n), in1=acc[:, n, :], op0=ALU.mult, op1=ALU.add))
                        step.settle()
                        dve.wait_ge(down_made, i * E + e + 1)
                        for n in range(NB):
                            ins = dve.scalar_tensor_tensor(
                                out=acc[:, n, :], in0=down_ps[e % 2][:, n, :], scalar=gate(e, n), in1=acc[:, n, :], op0=ALU.mult, op1=ALU.add
                            )
                            step(ins) if n < NB - 1 else ins.then_inc(down_used, 1)
                        step.settle()
                        dve.wait_ge(down_used, i * E + e + 1)
                    step(dve.tensor_tensor(acc[:], acc[:], g.mod_part(layer, i // 2, GB).unsqueeze(1).to_broadcast([P, NB, C]), ALU.mult))
                    step.settle()
                    xr = g.x[:, bass.ds(i * NB, NB), :]
                    step(dve.tensor_tensor(xr, xr, acc[:], ALU.add))
                    step.again()

            @block.scalar
            def _(act):
                with act.Fori(0, B * T // TB) as i:
                    for e in range(E):
                        for k in range(FC):
                            act.wait_ge(up_made, i * E * FC + e * FC + k + 1)
                            act.activation(hidden[:, e % 2, k, :], up_ps[k][:], kind, bias=g.bias(bias0 + e * FC + k)).then_inc(hidden_ready, 1)

            @block.tensor
            def _(pe):
                with pe.Fori(0, B * T // TB) as i:
                    tok = moe.h_t[:, bass.ds(i * TB, TB)]
                    base = i * E * FC

                    def go_up(e):
                        for k in range(FC):
                            if e >= 1:
                                pe.wait_ge(hidden_ready, base + (e - 1) * FC + k + 1)
                            pe.matmul(up_ps[k][:], up(e, k), tok, start=True, stop=True).then_inc(up_made, 1)

                    def go_down(e):
                        if e >= 2:
                            pe.wait_ge(down_used, i * E + e - 1)
                        pe.wait_ge(hidden_ready, base + e * FC + FC)
                        for n in range(NB):
                            for k in range(FC):
                                ins = pe.matmul(down_ps[e % 2][:, n, :], hidden[:, e % 2, k, n * P : n * P + P], down(e, k), start=(k == 0), stop=(k == FC - 1))
                        ins.then_inc(down_made, 1)

                    go_up(0)
                    for e in range(1, E):
                        go_up(e)
                        go_down(e - 1)
                    go_down(E - 1)
                    pe.wait_ge(down_used, i * E + E)


ROWS = ["L0_attn_out_b", "L1_attn_out_proj_b", "L1_attn_Vp_b", "L1_attn_ff2_b", "L1_attn_ln1_g", "L1_attn_ln1_b", "L1_attn_ln2_g", "L1_attn_ln2_b"]


class Shared:

    def __init__(self, a):
        self.x = a.sb("x", [P, TILES, C])
        self.ident = a.sb("ident", [P, P])
        self.causal = a.sb("causal", [P, P])
        self.minus_half = a.sb("minus_half", [P, 16])
        self.mod = a.sb("mod", [P, 2 * B, 6 * C])
        self.wt1 = a.sb("weights1_t", [P, W_SLOTS - W_SLOTS_L0, P])
        self.rows = a.sb("bias_rows", [P, len(ROWS), C])
        self.lam = a.sb("lam", [P, 1])
        self.v_bias = a.sb("v_bias", [P, C])
        self.expert_rank = a.sb("expert_rank", [P, E])
        self.before = a.sb("before", [P, P], BF16)
        self.ones_b = a.sb("ones_bf16", [P, P], BF16)
        self.wr1 = a.sb("router1", [C, E])

    def bias(self, row):
        return self.weights(W_BIAS)[:, row : row + 1]

    def weights(self, slot, n=None):
        w, at = (self.wt0, slot) if slot < W_SLOTS_L0 else (self.wt1, slot - W_SLOTS_L0)
        return w[:, at, :] if n is None else w[:, at : at + n, :]

    def row(self, name):
        return self.rows[:, ROWS.index(name), :]

    def mod_part(self, layer, b, part):
        return self.mod[:, bass.ds(b + layer * B, 1), part * C : part * C + C].rearrange("p n c -> p (n c)")

    def mod_row(self, layer, b, part):
        return self.mod[:, bass.ds(b + layer * B, 1), part * C : part * C + C].to_broadcast([P, NT, C])

    def small_loads(self, dram):
        return [(self.rows[:, i, :], dram[n].partition_broadcast(P)) for i, n in enumerate(ROWS)] + [
            (self.wr1[:], dram["L1_ffn_Wr"]),
            (self.lam[:], dram["L1_attn_lam"].partition_broadcast(P)),
            (self.v_bias[:], dram["L1_attn_in_proj_b"][2 * C : 3 * C].partition_broadcast(P)),
        ]


def store(nc, g, out):
    with ExitStack() as ctx:
        a = Alloc(nc, ctx)
        stored = a.sem("stored")
        with nc.Block() as block:

            @block.sync
            def _(sp):
                sp.dma_start(out.rearrange("b (n p) c -> p (b n) c", p=P), g.x[:]).then_inc(stored, 16)
                sp.wait_ge(stored, 16)


HEADS, DH = 16, 8
GROUPS = HEADS // 4
PIECES = 3
SHIFT_ROW = PIECES * PIECES * DH
PACK_ROWS = SHIFT_ROW + PIECES
TOP = max(1, int(T * 0.2))
SCALE1 = float(DH) ** -0.5
HEADROOM = 60.0
FLOOR = 50.0


class Scratch:

    def __init__(self, nc):
        self.q = nc.dram_tensor("q_pieces_dram", [B, PIECES, C, T], BF16, kind="Internal").ap()
        self.k = nc.dram_tensor("k_pieces_dram", [B, PIECES, C, T], BF16, kind="Internal").ap()
        self.shift = nc.dram_tensor("shift_pieces_dram", [B, PIECES, HEADS, T], BF16, kind="Internal").ap()
        self.v = nc.dram_tensor("v_dram", [B, NT, P, C], F32, kind="Internal").ap()
        self.sparse_q = nc.dram_tensor("sparse_q_dram", [B, RQ, T], F32, kind="Internal").ap()
        self.sparse_out = nc.dram_tensor("sparse_out_dram", [B, NT, P, C], F32, kind="Internal").ap()


class Fused:

    def __init__(self, a):
        self.v = a.sb("v1", [P, TILES, C])
        self.sparse_k = a.sb("sparse_k", [P, B * T])
        self.sparse_v = a.sb("sparse_v", [P, TILES, C])
        self.doubt = a.sb("doubt", [P, 2])


def prepare(nc, g, f, scratch, dram):
    with ExitStack() as ctx:
        a = Alloc(nc, ctx)
        norm = Norm(a, "ln1", g.minus_half)
        h = a.sb("h1", [P, NT, C])
        h_t = a.sb("h1_t", [P, T])
        q = a.sb("q1", [P, T])
        k = a.sb("k1", [P, T])
        rest = a.sb("rest", [P, 2, T])
        q_p = a.sb("q1_pieces", [P, PIECES, T], BF16)
        k_p = a.sb("k1_pieces", [P, PIECES, T], BF16)
        square = a.sb("square", [P, 2, T])
        head_sum = a.sb("head_sum", [P, HEADS])
        bound = a.sb("bound", [HEADS, T])
        shift = a.sb("shift", [HEADS, T])
        shift_rest = a.sb("shift_rest", [HEADS, T])
        shift_p = a.sb("shift_pieces", [HEADS, PIECES, T], BF16)
        k_max = a.sb("k_max", [HEADS, 1])
        sq = a.sb("sparse_q_t", [P, T])
        sq_w = a.sb("sparse_q_w", [P, P])
        sk_w = a.sb("sparse_k_w", [P, P])
        ps_a = a.ps("prep_ps_a", [P, T])
        ps_b = a.ps("prep_ps_b", [P, T])
        ps_c = a.ps("prep_ps_c", [P, T])
        ps_d = a.ps("prep_ps_d", [P, T])
        vec = a.sem("prep_vec")
        const_ready = a.sem("prep_const")
        pads_ready = a.sem("pads_ready")
        h_ready = a.sem("h1_ready")
        h_turned = a.sem("h1_turned")
        h_t_ready = a.sem("h1_t_ready")
        q_made = a.sem("q1_made")
        k_made = a.sem("k1_made")
        v_made = a.sem("v1_made")
        q_ready = a.sem("q1_ready")
        k_ready = a.sem("k1_ready")
        v_ready = a.sem("v1_ready")
        sq_made = a.sem("sparse_q_made")
        sk_made = a.sem("sparse_k_made")
        sv_made = a.sem("sparse_v_made")
        sq_ready = a.sem("sparse_q_ready")
        sk_ready = a.sem("sparse_k_ready")
        q_squared = a.sem("q1_squared")
        k_squared = a.sem("k1_squared")
        norms_made = a.sem("norms_made")
        norms_used = a.sem("norms_used")
        bound_ready = a.sem("bound_ready")
        sqrt_ready = a.sem("sqrt_ready")
        piece = a.sem("pieces_act")
        left = a.sem("pieces_dve")
        shift_ready = a.sem("shift_ready")
        stored = a.sem("prep_stored")
        sp_rounds = a.sem("prep_sp_rounds")
        STORES = 3 * PIECES + 2

        with nc.Block() as block:

            @block.gpsimd
            def _(pool):
                pool.memset(head_sum[:], 1.0).then_inc(const_ready, 1)
                pool.wait_ge(const_ready, 1)
                pool.affine_select(
                    out=head_sum[:], in_=head_sum[:], compare_op=ALU.is_ge, fill=0.0, base=0, pattern=[[-DH, HEADS]], channel_multiplier=1
                ).then_inc(const_ready, 1)
                pool.wait_ge(const_ready, 2)
                pool.affine_select(
                    out=head_sum[:], in_=head_sum[:], compare_op=ALU.is_ge, fill=0.0, base=DH - 1, pattern=[[DH, HEADS]], channel_multiplier=-1
                ).then_inc(const_ready, 1)
                with pool.Fori(0, B) as b:
                    norm.pool(pool, b + 1)

            @block.vector
            def _(dve):
                step = Steps(dve, vec)
                step(dve.memset(sq_w[:], 0.0))
                step(dve.memset(sk_w[:], 0.0))
                step.settle()
                dve.tensor_copy(sq_w[:, 0:RQ], g.weights(W_QK1)[:, 0:RQ]).then_inc(pads_ready, 1)
                dve.tensor_copy(sk_w[:, 0:RQ], g.weights(W_QK1)[:, RQ : 2 * RQ]).then_inc(pads_ready, 1)
                step.again()
                with dve.Fori(0, B) as b:
                    step = Steps(dve, vec)
                    rows = g.x[:, bass.ds(b * NT, NT), :]
                    layer_norm(dve, step, norm, rows, h[:], g.mod_row(1, b, CA), lambda: dve.wait_ge(norm.rstd_ready, b + 1))
                    dve.tensor_tensor(h[:], h[:], g.mod_row(1, b, SA), ALU.add).then_inc(h_ready, 1)
                    dve.wait_ge(k_made, b + 1)
                    dve.tensor_scalar(k[:], ps_c[:], g.bias(B_K1), None, ALU.add).then_inc(k_ready, 1)
                    dve.wait_ge(v_made, b + 1)
                    dve.tensor_tensor(
                        f.v[:, bass.ds(b * NT, NT), :], ps_a[:].rearrange("p (n c) -> p n c", c=C), bc(g.v_bias[:], NT), ALU.add
                    ).then_inc(v_ready, 1)
                    dve.wait_ge(sq_made, b + 1)
                    dve.tensor_scalar(sq[:], ps_b[:], g.bias(B_SQ1), float(RQ) ** -0.5, ALU.add, ALU.mult).then_inc(sq_ready, 1)
                    for i in range(PIECES - 1):
                        for n, (whole, pieces) in enumerate(((q, q_p), (k, k_p))):
                            dve.wait_ge(piece, b * 4 + 2 * i + n + 1)
                            of = whole[:] if i == 0 else rest[:, n, :]
                            to = rest[:, n, :] if i == 0 else pieces[:, 2, :]
                            dve.tensor_tensor(to, of, pieces[:, i, :], ALU.subtract).then_inc(left, 1)
                    dve.wait_ge(sv_made, b + 1)
                    step(
                        dve.tensor_tensor(
                            f.sparse_v[:, bass.ds(b * NT, NT), :], ps_a[:].rearrange("p (n c) -> p n c", c=C), bc(g.row("L1_attn_Vp_b"), NT), ALU.add
                        )
                    )
                    dve.wait_ge(norms_made, 2 * b + 1)
                    dve.reduce_max(k_max[:], ps_d[0:HEADS, :], AX.X).then_inc(norms_used, 1)
                    dve.wait_ge(norms_used, 2 * b + 1)
                    dve.wait_ge(norms_made, 2 * b + 2)
                    dve.tensor_scalar(bound[:], ps_d[0:HEADS, :], k_max[:, 0:1], 1e-30, ALU.mult, ALU.max).then_inc(norms_used, 1)
                    dve.wait_ge(sqrt_ready, b + 1)
                    step(dve.tensor_scalar(shift[:], bound[:], -1.0, HEADROOM / SCALE1, ALU.mult, ALU.add))
                    step.settle()
                    step(dve.tensor_copy(shift_p[:, 0, :], shift[:]))
                    step.settle()
                    step(dve.tensor_tensor(shift_rest[:], shift[:], shift_p[:, 0, :], ALU.subtract))
                    step.settle()
                    step(dve.tensor_copy(shift_p[:, 1, :], shift_rest[:]))
                    step.settle()
                    dve.tensor_tensor(shift_p[:, 2, :], shift_rest[:], shift_p[:, 1, :], ALU.subtract).then_inc(shift_ready, 1)
                    step.again()

            @block.scalar
            def _(act):
                with act.Fori(0, B) as b:
                    for n in range(2):
                        act.wait_ge(h_turned, b * 2 + n + 1)
                        act.activation(h_t[:, n * 512 : n * 512 + 512], ps_a[:, n * 512 : n * 512 + 512], ACT.Copy).then_inc(h_t_ready, 1)
                    act.wait_ge(q_made, b + 1)
                    act.activation(q[:], ps_b[:], ACT.Identity, bias=g.bias(B_Q1)).then_inc(q_ready, 1)
                    act.wait_ge(q_ready, b + 1)
                    act.activation(q_p[:, 0, :], q[:], ACT.Copy).then_inc(piece, 1)
                    act.wait_ge(k_ready, b + 1)
                    act.activation(k_p[:, 0, :], k[:], ACT.Copy).then_inc(piece, 1)
                    act.activation(square[:, 0, :], k[:], ACT.Square).then_inc(k_squared, 1)
                    act.activation(square[:, 1, :], q[:], ACT.Square).then_inc(q_squared, 1)
                    act.wait_ge(sk_made, b + 1)
                    act.activation(f.sparse_k[:, bass.ds(b * T, T)], ps_c[:], ACT.Identity, bias=g.bias(B_SK1)).then_inc(sk_ready, 1)
                    for n, pieces in enumerate((q_p, k_p)):
                        act.wait_ge(left, b * 4 + n + 1)
                        act.activation(pieces[:, 1, :], rest[:, n, :], ACT.Copy).then_inc(piece, 1)
                    act.wait_ge(norms_used, 2 * b + 2)
                    act.activation(bound[:], bound[:], ACT.Sqrt).then_inc(sqrt_ready, 1)
                    act.wait_ge(stored, 16 * STORES * (b + 1))

            @block.sync
            def _(sp):
                with sp.Fori(0, B) as b:

                    def keep(to, of):
                        sp.dma_start(to, of).then_inc(stored, 16)

                    at = bass.ds(b, 1)
                    sp.wait_ge(sq_ready, b + 1)
                    keep(scratch.sparse_q[at].rearrange("b r t -> (b r) t"), sq[0:RQ, :])
                    sp.wait_ge(v_ready, b + 1)
                    keep(scratch.v[at].rearrange("b n p c -> p (b n) c"), f.v[:, bass.ds(b * NT, NT), :])
                    sp.wait_ge(left, b * 4 + 4)
                    for i in range(PIECES):
                        keep(scratch.q[at, i].rearrange("b r t -> (b r) t"), q_p[:, i, :])
                        keep(scratch.k[at, i].rearrange("b r t -> (b r) t"), k_p[:, i, :])
                    sp.wait_ge(shift_ready, b + 1)
                    for i in range(PIECES):
                        keep(scratch.shift[at, i].rearrange("b r t -> (b r) t"), shift_p[:, i, :])
                    sp.wait_ge(stored, 16 * STORES * (b + 1))
                    sp.sem_inc(sp_rounds, 1)

            @block.tensor
            def _(pe):
                pe.wait_ge(const_ready, 3)
                pe.wait_ge(pads_ready, 2)
                with pe.Fori(0, B) as b:

                    def project(to, w, of):
                        for n in range(2):
                            cols = slice(n * 512, n * 512 + 512)
                            ins = pe.matmul(to[0 : w.shape[1], cols], w, of[:, cols], start=True, stop=True)
                        return ins

                    def values(slot):
                        for n in range(NT):
                            ins = pe.matmul(ps_a[:, n * P : n * P + P], h_t[:, n * P : n * P + P], g.weights(slot), start=True, stop=True)
                        return ins

                    pe.wait_ge(h_ready, b + 1)
                    for n in range(NT):
                        ins = pe.transpose(ps_a[:, n * P : n * P + P], h[:, n, :], g.ident[:])
                        if n % 4 == 3:
                            ins.then_inc(h_turned, 1)
                    pe.wait_ge(h_t_ready, b * 2 + 2)
                    project(ps_b, g.weights(W_QKV1), h_t).then_inc(q_made, 1)
                    project(ps_c, g.weights(W_QKV1 + 1), h_t).then_inc(k_made, 1)
                    values(W_QKV1 + 2).then_inc(v_made, 1)
                    pe.wait_ge(q_ready, b + 1)
                    project(ps_b, sq_w[:], h_t).then_inc(sq_made, 1)
                    pe.wait_ge(k_ready, b + 1)
                    project(ps_c, sk_w[:], h_t).then_inc(sk_made, 1)
                    pe.wait_ge(v_ready, b + 1)
                    values(W_V1).then_inc(sv_made, 1)
                    pe.wait_ge(k_squared, b + 1)
                    project(ps_d, head_sum[:], square[:, 0, :]).then_inc(norms_made, 1)
                    pe.wait_ge(q_squared, b + 1)
                    pe.wait_ge(norms_used, 2 * b + 1)
                    project(ps_d, head_sum[:], square[:, 1, :]).then_inc(norms_made, 1)


SEARCH = 7
IN_MIN, IN_MAX = TOP - 7, TOP - 1
AIM = 0.5 * (IN_MIN + IN_MAX)
Z_TOP, Z_WIDE = 0.8416, 0.35
N_LOW, N_HIGH = 319.0, 119.0
MEAN_EXCESS = 0.3989423


def attend(nc, g, f, scratch):
    STEPS = 4 * NT
    PER = GROUPS * STEPS
    with ExitStack() as ctx:
        a = Alloc(nc, ctx)
        q_pack = a.sb("q_pack", [P, 2, 4, T], BF16)
        k_pack = a.sb("k_pack", [P, 2, 4, T], BF16)
        probs = a.sb("probs1", [P, 2, 4, T])
        v_pad = a.sb("v_pad", [P, 2, NT, 4, 32])
        pv = a.sb("pv", [P, T])
        inv = a.sb("pv_inv", [P, GROUPS, NT, 4])
        sq = a.sb("sparse_q_tile", [P, 2, P])
        s = a.sb("sparse_scores", [P, 2, T])
        e = a.sb("sparse_exp", [P, 2, T])
        junk = a.sb("junk", [P, T])
        w_t = a.sb("sparse_w_t", [P, NT, P])
        so = a.sb("sparse_out_tile", [P, 2, C])
        total = a.sb("row_sum", [P, 2])
        excess = a.sb("row_excess", [P, 2])
        mean = a.sb("row_mean", [P, 2])
        sigma = a.sb("row_sigma", [P, 2])
        nmax = a.sb("minus_row_max", [P, 2])
        z = a.sb("row_exp_sum", [P, 2])
        low = a.sb("low", [P, 2, 2])
        high = a.sb("high", [P, 2, 2])
        at = a.sb("at", [P, 2, 2])
        above = a.sb("above", [P, 2], I32)
        below = a.sb("below", [P, 2], I32)
        span = a.sb("span", [P, 2])
        fall = a.sb("fall", [P, 2])
        near = a.sb("near", [P, NT, 8])
        order = a.sb("order", [P, 8])
        pick = a.sb("pick", [P, 8])
        rank = a.sb("rank", [P, NT])
        cut = a.sb("cut", [P, NT])
        count = a.sb("count", [P, NT])
        nearer = a.sb("nearer", [P, NT, 8])
        wrong = a.sb("wrong", [P, NT])
        tied = a.sb("tied", [P, NT])
        worst = a.sb("worst", [P, 2])
        w_sum = a.sb("w_sum", [P, 2])
        scores_ps = [a.ps(f"scores1_ps{i}", [P, T]) for i in range(2)]
        pv_ps = a.ps("pv_ps", [P, 2, 512])
        misc = a.ps("misc_ps", [P, T])
        vec = a.sem("attend_vec")
        const_ready = a.sem("attend_const")
        packs_loaded = [a.sem(f"packs_loaded{i}") for i in range(2)]
        sq_loaded = [a.sem(f"sparse_q_loaded{i}") for i in range(2)]
        so_stored = [a.sem(f"sparse_out_stored{i}") for i in range(2)]
        v_staged = a.sem("v_staged")
        scored = a.sem("scored1")
        exp_done = a.sem("exp1_done")
        pv_done = a.sem("pv_done")
        pv_kept = a.sem("pv_kept")
        misc_made = a.sem("misc_made")
        misc_used = a.sem("misc_used")
        max_ready = a.sem("sparse_max_ready")
        sparse_exp = a.sem("sparse_exp_done")
        w_ready = a.sem("sparse_w_ready")
        w_t_ready = a.sem("sparse_w_t_ready")
        out_ready = a.sem("sparse_out_ready")
        sp_rounds = a.sem("attend_sp_rounds")
        USES = GROUPS * 7

        def use(b, group, k):
            if k < 2:
                n = k if group == 0 else 7 * group - 5 + k
            else:
                n = 7 * group + 2 + k if group < GROUPS - 1 else 7 * group + k
            return b * USES + n + 1

        def store_sparse(sp, b, tile):
            sp.wait_ge(out_ready, b * NT + tile + 1)
            sp.dma_start(scratch.sparse_out[bass.ds(b, 1), tile].rearrange("b p c -> (b p) c"), so[:, tile % 2, :]).then_inc(so_stored[tile % 2], 16)

        with nc.Block() as block:

            @block.sync
            def _(sp):
                sp.wait_ge(const_ready, 6)
                with sp.Fori(0, B) as b:
                    one = bass.ds(b, 1)
                    for group in range(GROUPS):
                        half = group % 2
                        if group == 0:
                            pass
                        else:
                            sp.wait_ge(scored, b * PER + (group - 1) * STEPS + 1)
                        for i in range(PIECES):
                            for j in range(PIECES):
                                rows = slice((i * PIECES + j) * DH, (i * PIECES + j + 1) * DH)
                                for pack, of, n in ((q_pack, scratch.q, i), (k_pack, scratch.k, j)):
                                    sp.dma_start(
                                        pack[rows, half], of[one, n, group * 32 : group * 32 + 32].rearrange("b (h d) t -> d (b h) t", d=DH)
                                    ).then_inc(packs_loaded[half], 16)
                        sp.dma_start(
                            q_pack[SHIFT_ROW:PACK_ROWS, half], scratch.shift[one, :, group * 4 : group * 4 + 4].rearrange("b i h t -> (b i) h t")
                        ).then_inc(packs_loaded[half], 16)
                        for n in range(2):
                            tile = group * 2 + n
                            if group > 0:
                                sp.wait_ge(misc_made, use(b, group - 1, n))
                            sp.dma_start(
                                sq[0:RQ, n, :], scratch.sparse_q[one, :, tile * P : tile * P + P].rearrange("b r t -> (b r) t")
                            ).then_inc(sq_loaded[n], 16)
                        for n in range(2):
                            tile = group * 2 + n - 2
                            if tile >= 0:
                                store_sparse(sp, b, tile)
                    for n in range(2):
                        store_sparse(sp, b, NT - 2 + n)
                    sp.wait_ge(scored, b * PER + PER + 1)
                    for n in range(2):
                        sp.wait_ge(so_stored[n], 16 * (b + 1) * GROUPS)
                    sp.sem_inc(sp_rounds, 1)

            @block.gpsimd
            def _(pool):
                pool.memset(v_pad[:], 0.0).then_inc(const_ready, 1)
                pool.wait_ge(const_ready, 1)
                pool.memset(q_pack[64:128], 0.0).then_inc(const_ready, 1)
                pool.wait_ge(const_ready, 2)
                pool.memset(k_pack[64:128], 1.0).then_inc(const_ready, 1)
                pool.wait_ge(const_ready, 3)
                pool.memset(sq[RQ:P], 0.0).then_inc(const_ready, 1)
                pool.wait_ge(const_ready, 4)
                pool.iota(order[:], pattern=[[1, 8]], base=1, channel_multiplier=0, allow_small_or_imprecise_dtypes=True).then_inc(const_ready, 1)
                pool.wait_ge(const_ready, 5)
                pool.memset(v_pad[:, :, :, :, DH : DH + 1], 1.0).then_inc(const_ready, 1)
                pool.wait_ge(const_ready, 6)
                with pool.Fori(0, B) as b:
                    for group in range(GROUPS):
                        if group >= 2:
                            pool.wait_ge(pv_done, (b * GROUPS + group - 1) * NT)
                        pool.tensor_copy(
                            v_pad[:, group % 2, :, :, 0:DH],
                            f.v[:, bass.ds(b * NT, NT), group * 32 : group * 32 + 32].rearrange("p n (h d) -> p n h d", d=DH),
                        ).then_inc(v_staged, 1)
                    pool.wait_ge(pv_done, (b + 1) * GROUPS * NT)

            @block.scalar
            def _(act):
                with act.Fori(0, B) as b:
                    for group in range(GROUPS):
                        for n in range(STEPS):
                            kt, j = n // 4, n % 4
                            act.wait_ge(scored, b * PER + group * STEPS + n + 2)
                            if j == 0 and group * NT + kt >= 2:
                                act.wait_ge(pv_done, b * GROUPS * NT + group * NT + kt - 1)
                            act.activation(probs[:, kt % 2, j, :], scores_ps[n % 2][:], ACT.Exp, scale=SCALE1).then_inc(exp_done, 1)
                            if n in (18, 26):
                                t = (n - 18) // 8
                                if group >= 1:
                                    act.wait_ge(misc_made, use(b, group - 1, 3 + 2 * t))
                                act.wait_ge(max_ready, (b * GROUPS + group) * 2 + t + 1)
                                act.activation(e[:, t, :], s[:, t, :], ACT.Exp, bias=nmax[:, t : t + 1], accum_out=z[:, t : t + 1]).then_inc(sparse_exp, 1)
                    act.wait_ge(pv_done, (b + 1) * GROUPS * NT)

            @block.tensor
            def _(pe):
                pe.wait_ge(const_ready, 6)
                pe.sem_inc(scored, 1)
                with pe.Fori(0, B) as b:
                    key_cols = lambda n: f.sparse_k[:, bass.ds(b * T + n * 512, 512)]

                    def score(group, n):
                        kt, j = n // 4, n % 4
                        if n == 0:
                            pe.wait_ge(packs_loaded[group % 2], 16 * 19 * (b * 2 + group // 2 + 1))
                        if group * STEPS + n >= 2:
                            pe.wait_ge(exp_done, b * PER + group * STEPS + n - 1)
                        for c in range(2):
                            ins = pe.matmul(
                                scores_ps[n % 2][:, c * 512 : c * 512 + 512],
                                k_pack[:, group % 2, j, kt * P : kt * P + P],
                                q_pack[:, group % 2, j, c * 512 : c * 512 + 512],
                                start=True,
                                stop=True,
                            )
                        ins.then_inc(scored, 1)

                    def values(group, kt, c):
                        if c == 0:
                            pe.wait_ge(exp_done, b * PER + group * STEPS + kt * 4 + 4)
                            if kt == 0:
                                pe.wait_ge(v_staged, b * GROUPS + group + 1)
                                if group >= 1:
                                    pe.wait_ge(pv_kept, b * GROUPS + group)
                        for j in range(4):
                            ins = pe.matmul(
                                pv_ps[32 * j : 32 * j + 32, c, :],
                                v_pad[:, group % 2, kt, j, :],
                                probs[:, kt % 2, j, c * 512 : c * 512 + 512],
                                start=(kt == 0),
                                stop=(kt == NT - 1),
                            )
                        if c == 1:
                            ins.then_inc(pv_done, 1)

                    def free(b, n):
                        if n > 0:
                            pe.wait_ge(misc_used, b * USES + n)

                    def sparse_scores(group, t):
                        free(b, use(0, group, t) - 1)
                        pe.wait_ge(sq_loaded[t], 16 * (b * GROUPS + group + 1))
                        for c in range(2):
                            ins = pe.matmul(misc[:, c * 512 : c * 512 + 512], sq[:, t, :], key_cols(c), start=True, stop=True)
                        ins.then_inc(misc_made, 1)

                    def turn_out(group):
                        free(b, use(0, group, 2) - 1)
                        pe.wait_ge(pv_kept, b * GROUPS + group + 1)
                        for n in range(NT):
                            ins = pe.transpose(misc[:, n * P : n * P + P], pv[:, n * P : n * P + P], g.ident[:])
                        ins.then_inc(misc_made, 1)

                    def turn_weights(group, t):
                        free(b, use(0, group, 3 + 2 * t) - 1)
                        pe.wait_ge(w_ready, (b * GROUPS + group) * 2 + t + 1)
                        for n in range(NT):
                            ins = pe.transpose(misc[:, n * P : n * P + P], e[:, t, n * P : n * P + P], g.ident[:])
                        ins.then_inc(misc_made, 1)

                    def sparse_values(group, t):
                        free(b, use(0, group, 4 + 2 * t) - 1)
                        pe.wait_ge(w_t_ready, (b * GROUPS + group) * 2 + t + 1)
                        for n in range(NT):
                            ins = pe.matmul(
                                misc[:, 0:C],
                                w_t[:, n, :],
                                f.sparse_v[:, bass.ds(b * NT + n, 1), :].rearrange("p n c -> p (n c)"),
                                start=(n == 0),
                                stop=(n == NT - 1),
                            )
                        ins.then_inc(misc_made, 1)

                    for group in range(GROUPS):
                        last = group - 1
                        side = {0: lambda: sparse_scores(group, 0), 3: lambda: sparse_scores(group, 1)}
                        if group > 0:
                            side |= {
                                6: lambda: turn_out(last),
                                9: lambda: turn_weights(last, 0),
                                12: lambda: sparse_values(last, 0),
                                15: lambda: turn_weights(last, 1),
                                18: lambda: sparse_values(last, 1),
                            }
                        for n in range(STEPS):
                            score(group, n)
                            if n % 4 in (1, 2):
                                if n >= 4:
                                    values(group, n // 4 - 1, n % 4 - 1)
                                elif group > 0:
                                    values(last, NT - 1, n % 4 - 1)
                            if n in side:
                                side[n]()
                    last = GROUPS - 1
                    values(last, NT - 1, 0)
                    values(last, NT - 1, 1)
                    turn_out(last)
                    for t in range(2):
                        turn_weights(last, t)
                        sparse_values(last, t)
                    pe.wait_ge(misc_used, b * USES + USES)

            @block.vector
            def _(dve):
                dve.wait_ge(const_ready, 6)
                step = Steps(dve, vec)
                step(dve.memset(f.doubt[:], 0.0))
                step.again()
                with dve.Fori(0, B) as b:
                    step = Steps(dve, vec)

                    def keep_pv(group):
                        dve.wait_ge(pv_done, (b * GROUPS + group + 1) * NT)
                        dve.tensor_copy(pv[:], pv_ps[:].rearrange("p c t -> p (c t)")).then_inc(pv_kept, 1)

                    def heads_out(group):
                        dve.wait_ge(misc_made, use(b, group, 2))
                        turned = misc[:].rearrange("p (n j c) -> p n j c", n=NT, j=4)
                        step(dve.reciprocal(inv[:, group], turned[:, :, :, DH]))
                        step.settle()
                        for n in range(NT):
                            ins = dve.tensor_tensor(
                                f.v[:, bass.ds(b * NT + n, 1), group * 32 : group * 32 + 32].rearrange("p n (j d) -> p (n j) d", d=DH),
                                turned[:, n, :, 0:DH],
                                inv[:, group, n, :].unsqueeze(2).to_broadcast([P, 4, DH]),
                                ALU.mult,
                            )
                            step(ins) if n < NT - 1 else ins.then_inc(misc_used, 1)

                    def keep_scores(group, t):
                        dve.wait_ge(misc_made, use(b, group, t))
                        dve.tensor_scalar(s[:, t, :], misc[:], 1.0, None, ALU.mult, ALU.add, accum_out=total[:, t : t + 1]).then_inc(misc_used, 1)
                        dve.wait_ge(misc_used, use(b, group, t))

                    def row_max(group, t):
                        dve.tensor_reduce(nmax[:, t : t + 1], s[:, t, :], AX.X, ALU.max, negate=True).then_inc(max_ready, 1)

                    def keep_turned(group, t):
                        dve.wait_ge(misc_made, use(b, group, 3 + 2 * t))
                        dve.tensor_copy(w_t[:], misc[:].rearrange("p (n c) -> p n c", n=NT)).then_inc(w_t_ready, 1)
                        dve.wait_ge(w_t_ready, (b * GROUPS + group) * 2 + t + 1)
                        dve.sem_inc(misc_used, 1)

                    def keep_out(group, t):
                        dve.wait_ge(misc_made, use(b, group, 4 + 2 * t))
                        if group >= 1:
                            dve.wait_ge(so_stored[t], 16 * (b * GROUPS + group))
                        dve.tensor_scalar(so[:, t, :], misc[:, 0:C], w_sum[:, t : t + 1], None, ALU.mult).then_inc(out_ready, 1)
                        dve.wait_ge(out_ready, b * NT + group * 2 + t + 1)
                        dve.sem_inc(misc_used, 1)

                    def start_search():
                        step(dve.tensor_scalar(mean[:], total[:], 1.0 / T, None, ALU.mult))
                        step.settle()
                        for t in range(2):
                            step(
                                dve.tensor_scalar(junk[:], s[:, t, :], mean[:, t : t + 1], None, ALU.max, ALU.add, accum_out=excess[:, t : t + 1])
                            )
                            step.settle()
                        step(dve.scalar_tensor_tensor(out=sigma[:], in0=excess[:], scalar=1.0 / T, in1=mean[:], op0=ALU.mult, op1=ALU.subtract))
                        step.settle()
                        step(dve.scalar_tensor_tensor(out=at[:, :, 0], in0=sigma[:], scalar=Z_TOP / MEAN_EXCESS, in1=mean[:], op0=ALU.mult, op1=ALU.add))
                        step.settle()
                        for bracket, z0, count in ((low, -Z_WIDE, N_LOW), (high, Z_WIDE, N_HIGH)):
                            step(dve.scalar_tensor_tensor(out=bracket[:, :, 0], in0=sigma[:], scalar=z0 / MEAN_EXCESS, in1=at[:, :, 0], op0=ALU.mult, op1=ALU.add))
                            step(dve.memset(bracket[:, :, 1], count))

                    def search(group, last):
                        for t in range(2):
                            step(dve.tensor_scalar(junk[:], s[:, t, :], at[:, t, 0:1], None, ALU.is_ge, ALU.add, accum_out=count[:, 2 * group + t : 2 * group + t + 1] if last else at[:, t, 1:2]))
                            step.settle()
                        if last:
                            return
                        step(dve.tensor_scalar(above[:], at[:, :, 1], float(IN_MAX), None, ALU.is_gt))
                        step(dve.tensor_scalar(below[:], at[:, :, 1], float(IN_MIN), None, ALU.is_lt))
                        step.settle()
                        step(dve.copy_predicated(low[:], above[:].unsqueeze(2).to_broadcast([P, 2, 2]), at[:]))
                        step(dve.copy_predicated(high[:], below[:].unsqueeze(2).to_broadcast([P, 2, 2]), at[:]))
                        step.settle()
                        step(dve.tensor_tensor(fall[:], low[:, :, 1], high[:, :, 1], ALU.subtract))
                        step(dve.tensor_tensor(span[:], high[:, :, 0], low[:, :, 0], ALU.subtract))
                        step.settle()
                        step(dve.reciprocal(fall[:], fall[:]))
                        step(dve.scalar_tensor_tensor(out=span[:], in0=low[:, :, 1], scalar=-AIM, in1=span[:], op0=ALU.add, op1=ALU.mult))
                        step.settle()
                        step(dve.tensor_tensor(span[:], span[:], fall[:], ALU.mult))
                        step.settle()
                        step(dve.tensor_tensor(at[:, :, 0], low[:, :, 0], span[:], ALU.add))
                        step.settle()

                    def weigh(group):
                        two = slice(2 * group, 2 * group + 2)
                        step(dve.tensor_scalar(rank[:, two], count[:, two], -1.0, float(TOP), ALU.mult, ALU.add))
                        dve.wait_ge(sparse_exp, (b * GROUPS + group) * 2 + 2)
                        for t in range(2):
                            tile = slice(2 * group + t, 2 * group + t + 1)
                            step(dve.scalar_tensor_tensor(out=junk[:], in0=s[:, t, :], scalar=at[:, t, 0:1], in1=e[:, t, :], op0=ALU.is_lt, op1=ALU.mult))
                            step.settle()
                            step(dve.max(near[:, 2 * group + t, :], junk[:]))
                            step.settle()
                            step(
                                dve.scalar_tensor_tensor(
                                    out=pick[:], in0=order[:], scalar=rank[:, tile], in1=near[:, 2 * group + t, :], op0=ALU.is_equal, op1=ALU.mult, accum_out=cut[:, tile]
                                )
                            )
                            step.settle()
                            step(
                                dve.scalar_tensor_tensor(
                                    out=e[:, t, :], in0=e[:, t, :], scalar=cut[:, tile], in1=e[:, t, :], op0=ALU.is_ge, op1=ALU.mult, accum_out=w_sum[:, t : t + 1]
                                )
                            )
                            step.settle()
                            step(
                                dve.scalar_tensor_tensor(
                                    out=w_sum[:, t : t + 1], in0=z[:, t : t + 1], scalar=1e-9, in1=w_sum[:, t : t + 1], op0=ALU.mult, op1=ALU.add
                                )
                            )
                            step.settle()
                            dve.reciprocal(w_sum[:, t : t + 1], w_sum[:, t : t + 1]).then_inc(w_ready, 1)

                    def doubts():
                        step(dve.tensor_scalar(wrong[:], count[:], float(IN_MIN), None, ALU.is_lt))
                        step(dve.tensor_scalar(tied[:], rank[:], 1.0, None, ALU.add))
                        step.settle()
                        step(dve.scalar_tensor_tensor(out=wrong[:], in0=count[:], scalar=float(IN_MAX), in1=wrong[:], op0=ALU.is_gt, op1=ALU.max))
                        step(dve.tensor_tensor(nearer[:], bc(order[:], NT), tied[:].unsqueeze(2).to_broadcast([P, NT, 8]), ALU.is_equal))
                        step.settle()
                        step(dve.tensor_tensor(nearer[:], nearer[:], near[:], ALU.mult))
                        step.settle()
                        step(dve.reduce_max(tied[:], nearer[:], AX.X))
                        step.settle()
                        step(dve.tensor_tensor(tied[:], tied[:], cut[:], ALU.is_equal))
                        step.settle()
                        step(dve.scalar_tensor_tensor(out=tied[:], in0=cut[:], scalar=0.0, in1=tied[:], op0=ALU.is_gt, op1=ALU.mult))
                        step.settle()
                        step(dve.tensor_tensor(wrong[:], wrong[:], tied[:], ALU.max))
                        step(dve.tensor_scalar(inv[:], inv[:], float(np.exp(FLOOR)), None, ALU.is_gt))
                        step.settle()
                        step(dve.reduce_max(worst[:, 0:1], inv[:].rearrange("p g n j -> p (g n j)"), AX.X))
                        step(dve.reduce_max(worst[:, 1:2], wrong[:], AX.X))
                        step.settle()
                        step(dve.tensor_tensor(f.doubt[:], f.doubt[:], worst[:], ALU.max))

                    for group in range(GROUPS):
                        last = group - 1
                        if group > 0:
                            keep_pv(last)
                        keep_scores(group, 0)
                        keep_scores(group, 1)
                        if group > 0:
                            heads_out(last)
                            keep_turned(last, 0)
                            keep_out(last, 0)
                            keep_turned(last, 1)
                            keep_out(last, 1)
                        row_max(group, 0)
                        row_max(group, 1)
                        start_search()
                        for i in range(SEARCH):
                            search(group, i == SEARCH - 1)
                        weigh(group)
                    last = GROUPS - 1
                    keep_pv(last)
                    heads_out(last)
                    for t in range(2):
                        keep_turned(last, t)
                        keep_out(last, t)
                    doubts()
                    step.again()


def heads_again(nc, g, f, scratch):
    with ExitStack() as ctx:
        a = Alloc(nc, ctx, "_again")
        flag, flag_ready = doubt_flag(nc, g, f, a, 0)
        q_pack = a.sb("q_pack", [P, T], BF16)
        k_pack = a.sb("k_pack", [P, T], BF16)
        v = a.sb("v", [P, NT, DH])
        probs = a.sb("probs", [P, T])
        probs_t = a.sb("probs_t", [P, T])
        nmax = a.sb("minus_max", [P, 1])
        total = a.sb("total", [P, 1])
        scores_ps = a.ps("scores_ps", [P, T])
        turn_ps = a.ps("turn_ps", [P, T])
        out_ps = a.ps("out_ps", [P, 512])
        vec = a.sem("vec")
        cleared = a.sem("cleared")
        loaded = a.sem("loaded")
        scored = a.sem("scored")
        max_ready = a.sem("max_ready")
        probs_ready = a.sem("probs_ready")
        probs_turned = a.sem("probs_turned")
        probs_t_ready = a.sem("probs_t_ready")
        out_made = a.sem("out_made")
        done = a.sem("done")
        sp_rounds = a.sem("sp_rounds")
        LOADS = 2 * PIECES * PIECES + 1

        with nc.Block() as block:

            @block.sync
            def _(sp):
                sp.wait_ge(flag_ready, 1)
                with sp.If(sp.value_load(flag[0:1, 0:1], min_val=0, max_val=P) != 0):
                    sp.wait_ge(cleared, 2)
                    with sp.Fori(0, B) as b:
                        with sp.Fori(0, HEADS) as head:
                            at = bass.ds(b, 1)
                            dims = bass.ds(head * DH, DH)
                            for i in range(PIECES):
                                for j in range(PIECES):
                                    rows = slice((i * PIECES + j) * DH, (i * PIECES + j + 1) * DH)
                                    sp.dma_start(q_pack[rows, :], scratch.q[at, i, dims].rearrange("b d t -> (b d) t")).then_inc(loaded, 16)
                                    sp.dma_start(k_pack[rows, :], scratch.k[at, j, dims].rearrange("b d t -> (b d) t")).then_inc(loaded, 16)
                            sp.dma_start(v[:], scratch.v[at, :, :, dims].rearrange("b n p d -> p (b n) d")).then_inc(loaded, 16)
                            sp.wait_ge(done, (b * HEADS + head + 1) * NT)
                            sp.sem_inc(sp_rounds, 1)

            @block.vector
            def _(dve):
                dve.wait_ge(flag_ready, 1)
                with dve.If(dve.value_load(flag[0:1, 0:1], min_val=0, max_val=P) != 0):
                    dve.memset(q_pack[64:128], 0.0).then_inc(cleared, 1)
                    dve.memset(k_pack[64:128], 0.0).then_inc(cleared, 1)
                    with dve.Fori(0, B) as b:
                        with dve.Fori(0, HEADS) as head:
                            with dve.Fori(0, NT) as n:
                                step = Steps(dve, vec)
                                at = (b * HEADS + head) * NT + n
                                dve.wait_ge(scored, at + 1)
                                step(dve.tensor_reduce(nmax[:], scores_ps[:], AX.X, ALU.max, negate=True))
                                step.settle()
                                dve.tensor_scalar(nmax[:], nmax[:], SCALE1, None, ALU.mult).then_inc(max_ready, 1)
                                dve.wait_ge(out_made, at + 1)
                                step(dve.reciprocal(total[:], total[:]))
                                step.settle()
                                dve.tensor_scalar(
                                    f.v[:, bass.ds(b * NT + n, 1), bass.ds(head * DH, DH)].rearrange("p n d -> p (n d)"), out_ps[:, 0:DH], total[:, 0:1], None, ALU.mult
                                ).then_inc(done, 1)
                                step.again()

            @block.scalar
            def _(act):
                act.wait_ge(flag_ready, 1)
                with act.If(act.value_load(flag[0:1, 0:1], min_val=0, max_val=P) != 0):
                    with act.Fori(0, B * HEADS * NT) as at:
                        act.wait_ge(max_ready, at + 1)
                        act.activation(probs[:], scores_ps[:], ACT.Exp, bias=nmax[:, 0:1], scale=SCALE1, accum_out=total[:, 0:1]).then_inc(probs_ready, 1)
                        act.wait_ge(probs_turned, at + 1)
                        act.activation(probs_t[:], turn_ps[:], ACT.Copy).then_inc(probs_t_ready, 1)
                        act.wait_ge(done, at + 1)

            @block.tensor
            def _(pe):
                pe.wait_ge(flag_ready, 1)
                with pe.If(pe.value_load(flag[0:1, 0:1], min_val=0, max_val=P) != 0):
                    with pe.Fori(0, B * HEADS) as head:
                        with pe.Fori(0, NT) as n:
                            pe.wait_ge(loaded, head * (16 * LOADS) + 16 * LOADS)
                            at = head * NT + n
                            for c in range(2):
                                cols = slice(c * 512, c * 512 + 512)
                                ins = pe.matmul(scores_ps[:, cols], q_pack[:, bass.ds(n * P, P)], k_pack[:, cols], start=True, stop=True)
                            ins.then_inc(scored, 1)
                            pe.wait_ge(probs_ready, at + 1)
                            for m in range(NT):
                                ins = pe.transpose(turn_ps[:, m * P : m * P + P], probs[:, m * P : m * P + P], g.ident[:])
                            ins.then_inc(probs_turned, 1)
                            pe.wait_ge(probs_t_ready, at + 1)
                            for m in range(NT):
                                ins = pe.matmul(out_ps[:, 0:DH], probs_t[:, m * P : m * P + P], v[:, m, :], start=(m == 0), stop=(m == NT - 1))
                            ins.then_inc(out_made, 1)
                            pe.wait_ge(done, at + 1)


def sparse_again(nc, g, f, scratch):
    with ExitStack() as ctx:
        a = Alloc(nc, ctx, "_sparse_again")
        flag, flag_ready = doubt_flag(nc, g, f, a, 1)
        sq = a.sb("sq", [P, P])
        e = a.sb("e", [P, T])
        left = a.sb("left", [P, T])
        w_t = a.sb("w_t", [P, T])
        so = a.sb("so", [P, C])
        best = a.sb("best", [P, 8])
        nmax = a.sb("minus_max", [P, 1])
        z = a.sb("z", [P, 1])
        w_sum = a.sb("w_sum", [P, 1])
        scores_ps = a.ps("scores_ps", [P, T])
        turn_ps = a.ps("turn_ps", [P, T])
        out_ps = a.ps("out_ps", [P, 512])
        vec = a.sem("vec")
        cleared = a.sem("cleared")
        loaded = a.sem("loaded")
        scored = a.sem("scored")
        max_ready = a.sem("max_ready")
        exp_ready = a.sem("exp_ready")
        w_ready = a.sem("w_ready")
        w_turned = a.sem("w_turned")
        w_t_ready = a.sem("w_t_ready")
        out_made = a.sem("out_made")
        out_ready = a.sem("out_ready")
        stored = a.sem("stored")
        sp_rounds = a.sem("sp_rounds")
        ROUNDS, LAST = TOP // 8, TOP % 8

        with nc.Block() as block:

            @block.sync
            def _(sp):
                sp.wait_ge(flag_ready, 1)
                with sp.If(sp.value_load(flag[0:1, 0:1], min_val=0, max_val=P) != 0):
                    sp.wait_ge(cleared, 1)
                    with sp.Fori(0, B) as b:
                        with sp.Fori(0, NT) as n:
                            sp.dma_start(sq[0:RQ, :], scratch.sparse_q[bass.ds(b, 1), :, bass.ds(n * P, P)].rearrange("b r t -> (b r) t")).then_inc(loaded, 16)
                            sp.wait_ge(out_ready, b * NT + n + 1)
                            sp.dma_start(scratch.sparse_out[bass.ds(b, 1), bass.ds(n, 1)].rearrange("b n p c -> (b n p) c"), so[:]).then_inc(stored, 16)
                            sp.wait_ge(stored, (b * NT + n) * 16 + 16)
                            sp.sem_inc(sp_rounds, 1)

            @block.vector
            def _(dve):
                dve.wait_ge(flag_ready, 1)
                with dve.If(dve.value_load(flag[0:1, 0:1], min_val=0, max_val=P) != 0):
                    dve.memset(sq[RQ:P], 0.0).then_inc(cleared, 1)
                    with dve.Fori(0, TILES) as at:
                        step = Steps(dve, vec)
                        dve.wait_ge(scored, at + 1)
                        dve.tensor_reduce(nmax[:], scores_ps[:], AX.X, ALU.max, negate=True).then_inc(max_ready, 1)
                        dve.wait_ge(exp_ready, at + 1)
                        step(dve.tensor_copy(left[:], e[:]))
                        step.again()
                        with dve.Fori(0, ROUNDS) as _:
                            step = Steps(dve, vec)
                            step(dve.max(best[:], left[:]))
                            step.settle()
                            step(dve.match_replace(left[:], best[:], left[:], -1.0))
                            step.again()
                        step = Steps(dve, vec)
                        if LAST:
                            step(dve.max(best[:], left[:]))
                            step.settle()
                            step(dve.memset(best[:, LAST:8], 2.0))
                            step.settle()
                            step(dve.match_replace(left[:], best[:], left[:], -1.0))
                            step.settle()
                        step(dve.scalar_tensor_tensor(out=left[:], in0=left[:], scalar=0.0, in1=e[:], op0=ALU.is_lt, op1=ALU.mult, accum_out=w_sum[:]))
                        step.settle()
                        step(dve.scalar_tensor_tensor(out=w_sum[:], in0=z[:], scalar=1e-9, in1=w_sum[:], op0=ALU.mult, op1=ALU.add))
                        step.settle()
                        dve.reciprocal(w_sum[:], w_sum[:]).then_inc(w_ready, 1)
                        dve.wait_ge(out_made, at + 1)
                        dve.wait_ge(w_ready, at + 1)
                        dve.tensor_scalar(so[:], out_ps[:, 0:C], w_sum[:, 0:1], None, ALU.mult).then_inc(out_ready, 1)
                        step.again()

            @block.scalar
            def _(act):
                act.wait_ge(flag_ready, 1)
                with act.If(act.value_load(flag[0:1, 0:1], min_val=0, max_val=P) != 0):
                    with act.Fori(0, TILES) as at:
                        act.wait_ge(max_ready, at + 1)
                        act.activation(e[:], scores_ps[:], ACT.Exp, bias=nmax[:, 0:1], accum_out=z[:, 0:1]).then_inc(exp_ready, 1)
                        act.wait_ge(w_turned, at + 1)
                        act.activation(w_t[:], turn_ps[:], ACT.Copy).then_inc(w_t_ready, 1)

            @block.tensor
            def _(pe):
                pe.wait_ge(flag_ready, 1)
                with pe.If(pe.value_load(flag[0:1, 0:1], min_val=0, max_val=P) != 0):
                    with pe.Fori(0, B) as b:
                        with pe.Fori(0, NT) as n:
                            at = b * NT + n
                            pe.wait_ge(loaded, at * 16 + 16)
                            for c in range(2):
                                ins = pe.matmul(scores_ps[:, c * 512 : c * 512 + 512], sq[:], f.sparse_k[:, bass.ds(b * T + c * 512, 512)], start=True, stop=True)
                            ins.then_inc(scored, 1)
                            pe.wait_ge(w_ready, at + 1)
                            for m in range(NT):
                                ins = pe.transpose(turn_ps[:, m * P : m * P + P], left[:, m * P : m * P + P], g.ident[:])
                            ins.then_inc(w_turned, 1)
                            pe.wait_ge(w_t_ready, at + 1)
                            for m in range(NT):
                                ins = pe.matmul(
                                    out_ps[:, 0:C],
                                    w_t[:, m * P : m * P + P],
                                    f.sparse_v[:, bass.ds(b * NT + m, 1), :].rearrange("p n c -> p (n c)"),
                                    start=(m == 0),
                                    stop=(m == NT - 1),
                                )
                            ins.then_inc(out_made, 1)


def doubt_flag(nc, g, f, a, kind):
    flag = a.sb("flag", [P, 1], I32)
    doubt = a.sb("doubt_bf16", [P, 1], BF16)
    flag_ps = a.ps("flag_ps", [P, 1])
    doubt_ready = a.sem("doubt_ready")
    counted = a.sem("doubt_counted")
    flag_ready = a.sem("flag_ready")
    with nc.Block() as block:

        @block.vector
        def _(dve):
            dve.tensor_copy(doubt[:], f.doubt[:, kind : kind + 1]).then_inc(doubt_ready, 1)
            dve.wait_ge(counted, 1)
            dve.tensor_copy(flag[:], flag_ps[:]).then_inc(flag_ready, 1)

        @block.tensor
        def _(pe):
            pe.wait_ge(doubt_ready, 1)
            pe.matmul(flag_ps[:], g.ones_b[:], doubt[:], start=True, stop=True).then_inc(counted, 1)

    return flag, flag_ready


def finish_attention(nc, g, f, scratch):
    with ExitStack() as ctx:
        a = Alloc(nc, ctx)
        norm = Norm(a, "ln_post", g.minus_half)
        h = a.sb("h1_again", [P, NT, C])
        sparse = a.sb("sparse_in", [P, NT, C])
        ctx_rows = a.sb("ctx1_rows", [P, NT, C])
        ctx_t = a.sb("ctx1_t", [P, T])
        y = a.sb("y1", [P, NT, C])
        y_t = a.sb("y1_t", [P, T])
        ff = a.sb("ff1", [P, FC, T])
        lam_e = a.sb("lam_exp", [P, 1])
        sig = a.sb("sigmoid_lam", [P, 1])
        cosig = a.sb("one_minus_sigmoid", [P, 1])
        turn_ps = a.ps("post_turn_ps", [P, T])
        out_ps = a.ps("post_out_ps", [P, T])
        ff_ps = [a.ps(f"post_ff_ps{i}", [P, 512]) for i in range(4)]
        vec = a.sem("post_vec")
        lam_ready = a.sem("lam_exp_ready")
        sparse_loaded = a.sem("sparse_loaded")
        rows_ready = a.sem("ctx1_rows_ready")
        ctx_turned = a.sem("ctx1_turned")
        ctx_t_ready = a.sem("ctx1_t_ready")
        dense_made = a.sem("dense_made")
        y_ready = a.sem("y1_ready")
        y_turned = a.sem("y1_turned")
        y_t_ready = a.sem("y1_t_ready")
        ff_made = a.sem("ff1_made")
        ff_act = a.sem("ff1_kept_act")
        down_made = a.sem("ff2_made")
        done = a.sem("post_done")
        sp_rounds = a.sem("post_sp_rounds")

        with nc.Block() as block:

            @block.sync
            def _(sp):
                with sp.Fori(0, B) as b:
                    sp.dma_start(sparse[:], scratch.sparse_out[bass.ds(b, 1)].rearrange("b n p c -> p (b n) c")).then_inc(sparse_loaded, 16)
                    sp.wait_ge(done, b + 1)
                    sp.sem_inc(sp_rounds, 1)

            @block.gpsimd
            def _(pool):
                with pool.Fori(0, B) as b:
                    pool.tensor_copy(ctx_rows[:], f.v[:, bass.ds(b * NT, NT), :]).then_inc(rows_ready, 1)
                    for n in range(3):
                        norm.pool(pool, 3 * b + n + 1)

            @block.vector
            def _(dve):
                step = Steps(dve, vec)
                dve.wait_ge(lam_ready, 1)
                step(dve.tensor_scalar(lam_e[:], lam_e[:], 1.0, None, ALU.add))
                step.settle()
                step(dve.reciprocal(sig[:], lam_e[:]))
                step.settle()
                step(dve.tensor_scalar(cosig[:], sig[:], -1.0, 1.0, ALU.mult, ALU.add))
                step.again()
                flat = lambda t: t[:].rearrange("p n c -> p (n c)")
                with dve.Fori(0, B) as b:
                    step = Steps(dve, vec)
                    rows = g.x[:, bass.ds(b * NT, NT), :]
                    layer_norm(dve, step, norm, rows, h[:], g.mod_row(1, b, CA), lambda: dve.wait_ge(norm.rstd_ready, 3 * b + 1))
                    step(dve.tensor_tensor(h[:], h[:], g.mod_row(1, b, SA), ALU.add))
                    dve.wait_ge(sparse_loaded, 16 * (b + 1))
                    step.settle()
                    step(dve.scalar_tensor_tensor(out=flat(h), in0=flat(sparse), scalar=cosig[:, 0:1], in1=flat(h), op0=ALU.mult, op1=ALU.add))
                    dve.wait_ge(dense_made, b + 1)
                    step(dve.tensor_tensor(y[:], out_ps[:].rearrange("p (n c) -> p n c", c=C), bc(g.row("L1_attn_out_proj_b"), NT), ALU.add))
                    step.settle()
                    step(dve.scalar_tensor_tensor(out=flat(h), in0=flat(y), scalar=sig[:, 0:1], in1=flat(h), op0=ALU.mult, op1=ALU.add))
                    step.settle()
                    layer_norm(dve, step, norm, h, y[:], bc(g.row("L1_attn_ln1_g"), NT), lambda: dve.wait_ge(norm.rstd_ready, 3 * b + 2))
                    dve.tensor_tensor(y[:], y[:], bc(g.row("L1_attn_ln1_b"), NT), ALU.add).then_inc(y_ready, 1)
                    dve.wait_ge(y_ready, b + 1)
                    dve.wait_ge(down_made, b + 1)
                    step(dve.tensor_tensor(h[:], out_ps[:].rearrange("p (n c) -> p n c", c=C), bc(g.row("L1_attn_ff2_b"), NT), ALU.add))
                    step.settle()
                    step(dve.tensor_tensor(h[:], h[:], y[:], ALU.add))
                    step.settle()
                    layer_norm(dve, step, norm, h, y[:], bc(g.row("L1_attn_ln2_g"), NT), lambda: dve.wait_ge(norm.rstd_ready, 3 * b + 3))
                    step(dve.tensor_tensor(y[:], y[:], bc(g.row("L1_attn_ln2_b"), NT), ALU.add))
                    step.settle()
                    step(dve.tensor_tensor(y[:], y[:], g.mod_row(1, b, GA), ALU.mult))
                    step.settle()
                    step(dve.tensor_tensor(rows, rows, y[:], ALU.add))
                    step.settle()
                    dve.sem_inc(done, 1)
                    step.again()

            @block.scalar
            def _(act):
                act.activation(lam_e[:], g.lam[:], ACT.Exp, scale=-1.0).then_inc(lam_ready, 1)
                with act.Fori(0, B) as b:
                    for n in range(2):
                        act.wait_ge(ctx_turned, 2 * b + n + 1)
                        act.activation(ctx_t[:, n * 512 : n * 512 + 512], turn_ps[:, n * 512 : n * 512 + 512], ACT.Copy).then_inc(ctx_t_ready, 1)
                    for n in range(2):
                        act.wait_ge(y_turned, 2 * b + n + 1)
                        act.activation(y_t[:, n * 512 : n * 512 + 512], turn_ps[:, n * 512 : n * 512 + 512], ACT.Copy).then_inc(y_t_ready, 1)
                    for n in range(2):
                        for k in range(FC):
                            act.wait_ge(ff_made, b * 2 * FC + n * FC + k + 1)
                            act.activation(ff[:, k, n * 512 : n * 512 + 512], ff_ps[k][:], ACT.Relu, bias=g.bias(B_FF1 + k)).then_inc(ff_act, 1)

            @block.tensor
            def _(pe):
                with pe.Fori(0, B) as b:

                    def turn(of, made):
                        for n in range(NT):
                            ins = pe.transpose(turn_ps[:, n * P : n * P + P], of[:, n, :], g.ident[:])
                            if n % 4 == 3:
                                ins.then_inc(made, 1)

                    pe.wait_ge(rows_ready, b + 1)
                    turn(ctx_rows, ctx_turned)
                    pe.wait_ge(ctx_t_ready, 2 * b + 2)
                    for n in range(NT):
                        ins = pe.matmul(out_ps[:, n * C : n * C + C], ctx_t[:, n * P : n * P + P], g.weights(W_OUT1), start=True, stop=True)
                    ins.then_inc(dense_made, 1)
                    pe.wait_ge(y_ready, b + 1)
                    turn(y, y_turned)
                    for n in range(2):
                        pe.wait_ge(y_t_ready, 2 * b + n + 1)
                        for k in range(FC):
                            if n == 1:
                                pe.wait_ge(ff_act, b * 2 * FC + k + 1)
                            pe.matmul(ff_ps[k][:], g.weights(W_FF1 + k), y_t[:, n * 512 : n * 512 + 512], start=True, stop=True).then_inc(ff_made, 1)
                    for n in range(2):
                        pe.wait_ge(ff_act, b * 2 * FC + (n + 1) * FC)
                        for m in range(4 * n, 4 * n + 4):
                            for k in range(FC):
                                ins = pe.matmul(out_ps[:, m * C : m * C + C], ff[:, k, m * P : m * P + P], g.weights(W_FF2 + k), start=(k == 0), stop=(k == FC - 1))
                    ins.then_inc(down_made, 1)


def fused_attention(nc, g, dram):
    with ExitStack() as ctx:
        f = Fused(Alloc(nc, ctx))
        scratch = Scratch(nc)
        prepare(nc, g, f, scratch, dram)
        attend(nc, g, f, scratch)
        heads_again(nc, g, f, scratch)
        sparse_again(nc, g, f, scratch)
        finish_attention(nc, g, f, scratch)


class Moe:

    def __init__(self, g, a, layer):
        self.gates = a.sb(f"gates{layer}", [P, TILES, E])
        self.h_t = a.sb(f"moe_h_t{layer}", [C, B * T])
        self.b2 = a.sb(f"down_bias{layer}", [P, E, C])
        if layer == 1:
            self.up = a.sb("up1", [C, E, FF])
            self.down = a.sb("down1", [P, E * FC, C])
        self.g, self.layer = g, layer

    def loads(self, dram):
        if self.layer == 0:
            return [(self.b2[:], dram["L0_ffn_expert_b2"].partition_broadcast(P))]
        return [
            (self.b2[:], dram["L1_ffn_b2"].partition_broadcast(P)),
            (self.up[:], dram["L1_ffn_W1"].rearrange("e c h -> c e h")),
            (self.down[:], dram["L1_ffn_W2"].rearrange("e (k p) c -> p (e k) c", p=P)),
        ]

    def up_weights(self, e, k):
        return self.g.weights(W_UP0 + e * FC + k) if self.layer == 0 else self.up[:, e, k * P : k * P + P]

    def down_weights(self, e, k):
        return self.g.weights(W_DOWN0 + e * FC + k) if self.layer == 0 else self.down[:, e * FC + k, :]


def adaln_program(nc, dram, out):
    with ExitStack() as whole:
        g = Shared(Alloc(nc, whole))
        with ExitStack() as layer0:
            a = Alloc(nc, layer0)
            g.wt0 = a.sb("weights0_t", [P, W_SLOTS_L0, P])
            setup(nc, g, dram)
            causal_attention(nc, g, dram)
            moe = Moe(g, a, 0)
            route(nc, g, moe, dram, 0)
            experts(nc, g, moe, 0)
        with ExitStack() as attn1:
            fused_attention(nc, g, dram)
        with ExitStack() as ffn1:
            moe = Moe(g, Alloc(nc, ffn1), 1)
            route(nc, g, moe, dram, 1)
            experts(nc, g, moe, 1)
        store(nc, g, out)


_INS = [
    "L0_attn_x",
    "L0_attn_qkv_w",
    "L0_attn_out_w",
    "L0_attn_out_b",
    "L0_ffn_router_w",
    "L0_ffn_expert_w1",
    "L0_ffn_expert_b1",
    "L0_ffn_expert_w2",
    "L0_ffn_expert_b2",
    "L0_c",
    "L0_wmod",
    "L1_attn_in_proj_w",
    "L1_attn_in_proj_b",
    "L1_attn_out_proj_w",
    "L1_attn_out_proj_b",
    "L1_attn_Qp_w",
    "L1_attn_Qp_b",
    "L1_attn_Kp_w",
    "L1_attn_Kp_b",
    "L1_attn_Vp_w",
    "L1_attn_Vp_b",
    "L1_attn_lam",
    "L1_attn_ff1_w",
    "L1_attn_ff1_b",
    "L1_attn_ff2_w",
    "L1_attn_ff2_b",
    "L1_attn_ln1_g",
    "L1_attn_ln1_b",
    "L1_attn_ln2_g",
    "L1_attn_ln2_b",
    "L1_ffn_Wr",
    "L1_ffn_W1",
    "L1_ffn_b1",
    "L1_ffn_W2",
    "L1_ffn_b2",
    "L1_c",
    "L1_wmod",
]
_OUT = (B, T, C)


def kernel(**inputs):
    import numpy as _np
    import concourse.bacc as _bacc
    from concourse import mybir as _mybir
    from concourse.bass_utils import run_bass_kernel_spmd as _run

    nc = _bacc.Bacc("TRN2", target_bir_lowering=False, num_devices=1)
    arrays, dram = {}, {}
    for name in _INS:
        a = _np.ascontiguousarray(inputs[name])
        if a.ndim == 0:
            a = a.reshape(1)
        arrays[f"in_{name}_dram"] = a
        dram[name] = nc.dram_tensor(f"in_{name}_dram", a.shape, _mybir.dt.from_np(a.dtype), kind="ExternalInput").ap()
    out = nc.dram_tensor("out_dram", _OUT, F32, kind="ExternalOutput").ap()
    adaln_program(nc, dram, out)
    r = _run(nc, [arrays], core_ids=[0])
    return r.results[0]["out_dram"]
```

```python
from contextlib import ExitStack

import numpy as np

import concourse.bass as bass
from concourse import mybir

ALU = mybir.AluOpType
ACT = mybir.ActivationFunctionType
AX = mybir.AxisListType
F32 = mybir.dt.float32
BF16 = mybir.dt.bfloat16
I32 = mybir.dt.int32

P = 128
B, T, C = 4, 1024, 128
NT = T // P
TILES = B * NT
E, FF = 8, 512
RQ = 64
FC = FF // P
LN_EPS = 1e-5

W_QKV0, W_OUT0 = 0, 3
W_UP0 = 4
W_DOWN0 = W_UP0 + E * FC
W_QKV1 = W_DOWN0 + E * FC
W_OUT1 = W_QKV1 + 3
W_QK1 = W_OUT1 + 1
W_ROUTER0 = W_QK1 + 1
W_V1 = W_ROUTER0 + 1
W_FF1 = W_V1 + 1
W_FF2 = W_FF1 + FC
W_BIAS = W_FF2 + FC
W_SLOTS = W_BIAS + 1
W_SLOTS_L0 = W_QKV1

B_UP1 = 0
B_FF1 = B_UP1 + E * FC
B_Q1 = B_FF1 + FC
B_K1, B_SQ1, B_SK1, B_DOWN1 = B_Q1 + 1, B_Q1 + 2, B_Q1 + 3, B_Q1 + 4
CAPACITY = int(T / E * 1.25)

SA, CA, GA, SB, CB, GB = range(6)


class Alloc:

    def __init__(self, nc, ctx, tag=""):
        self.nc, self.ctx, self.tag = nc, ctx, tag
        self.sems = []

    def sb(self, name, shape, dt=F32):
        return self.ctx.enter_context(self.nc.sbuf_tensor(name + self.tag, shape, dt))

    def ps(self, name, shape, dt=F32):
        return self.ctx.enter_context(self.nc.psum_tensor(name + self.tag, shape, dt))

    def sem(self, name):
        self.sems.append(self.ctx.enter_context(self.nc.semaphore(name + self.tag)))
        return self.sems[-1]

    def clear_sems(self):
        nums = sorted(s.num for s in self.sems)
        firsts = [n for n in nums if n - 1 not in nums]
        lasts = [n for n in nums if n + 1 not in nums]
        with self.nc.Block() as block:

            @block.gpsimd
            def _(pool):
                for first, last in zip(firsts, lasts):
                    pool.sem_clear(range(first, last + 1))


class Steps:

    def __init__(self, eng, sem):
        self.eng, self.sem, self.n = eng, sem, 0

    def __call__(self, ins):
        self.n += 1
        return ins.then_inc(self.sem, 1)

    def settle(self):
        self.eng.wait_ge(self.sem, self.n)

    def again(self):
        self.settle()
        self.eng.sem_clear(self.sem)


def bc(ap, n):
    return ap.unsqueeze(1).to_broadcast([ap.shape[0], n, ap.shape[1]])


def setup(nc, g, dram):
    with ExitStack() as ctx:
        a = Alloc(nc, ctx)
        nat = a.sb("weights_natural", [P, W_SLOTS, P])
        wmod = a.sb("wmod", [P, 2, 6 * C])
        cond = a.sb("cond", [2 * B, C])
        cond_t = a.sb("cond_t", [P, 2 * B])
        cond_e = a.sb("cond_e", [P, 2 * B])
        silu = a.sb("silu", [P, 2 * B])
        silu_b = a.sb("silu_b", [P, 2 * B, P])
        gate_sign = a.sb("gate_sign", [P, 4, B, C])
        weight_ps = [a.ps(f"weight_ps{i}", [P, 4, P]) for i in range(4)]
        mod_ps = [a.ps(f"mod_ps{i}", [P, 512]) for i in range(4)]
        cond_loaded = a.sem("cond_loaded")
        w0_loaded = a.sem("w0_loaded")
        w1_loaded = a.sem("w1_loaded")
        x_loaded = a.sem("x_loaded")
        rows_loaded = a.sem("rows_loaded")
        zeroed = a.sem("zeroed")
        ident_ready = a.sem("ident_ready")
        turned = a.sem("turned")
        kept_act = a.sem("kept_act")
        kept_dve = a.sem("kept_dve")
        cond_turned = a.sem("cond_turned")
        cond_kept = a.sem("cond_kept")
        cond_exp = a.sem("cond_exp")
        silu_ready = a.sem("silu_ready")
        mod_ready = a.sem("mod_ready")
        mod_kept = a.sem("mod_kept")
        vec = a.sem("setup_vec")
        GROUPS = -(-W_SLOTS // 4)
        W0_GROUPS = W_SLOTS_L0 // 4
        MODS = 2 * B * 2
        HALF = 3 * C

        def group(i):
            return 4 * i, min(4, W_SLOTS - 4 * i)

        with nc.Block() as block:

            @block.sync
            def _(sp):
                for half in range(2):
                    sp.dma_start(cond[half * B : half * B + B, :], dram[f"L{half}_c"]).then_inc(cond_loaded, 16)
                sp.dma_start(nat[:, W_QKV0 : W_QKV0 + 3, :], dram["L0_attn_qkv_w"].rearrange("(n p) c -> p n c", p=P)).then_inc(w0_loaded, 16)
                sp.dma_start(nat[:, W_OUT0, :], dram["L0_attn_out_w"]).then_inc(w0_loaded, 16)
                sp.dma_start(
                    nat[:, W_UP0 : W_UP0 + E * FC, :], dram["L0_ffn_expert_w1"].rearrange("e (k p) c -> p (e k) c", p=P)
                ).then_inc(w0_loaded, 16)
                sp.dma_start(
                    nat[:, W_DOWN0 : W_DOWN0 + E * FC, :].rearrange("p (e k) f -> p e (k f)", e=E),
                    dram["L0_ffn_expert_w2"].rearrange("e c f -> c e f"),
                ).then_inc(w0_loaded, 16)
                for half in range(2):
                    sp.dma_start(wmod[:, half, :], dram[f"L{half}_wmod"]).then_inc(cond_loaded, 16)
                sp.dma_start(g.x[:], dram["L0_attn_x"].rearrange("b (n p) c -> p (b n) c", p=P)).then_inc(x_loaded, 16)
                sp.wait_ge(x_loaded, 16)

            @block.gpsimd
            def _(pool):
                pool.memset(nat[:, W_ROUTER0, :], 0.0).then_inc(zeroed, 1)
                pool.memset(nat[:, W_BIAS, :], 0.0).then_inc(zeroed, 1)
                pool.memset(g.ident[:], 0.0).then_inc(zeroed, 1)
                pool.memset(g.causal[:], 0.0).then_inc(zeroed, 1)
                pool.memset(g.minus_half[:], -0.5)
                pool.memset(g.zeros[:], 0.0)
                for e in range(E):
                    pool.memset(g.expert_rank[:, e : e + 1], float(E - e))
                pool.memset(g.ones_b[:], 1.0).then_inc(zeroed, 1)
                pool.wait_ge(zeroed, 5)
                pool.affine_select(
                    out=g.ident[:], in_=g.ident[:], compare_op=ALU.not_equal, fill=1.0, base=0, pattern=[[-1, P]], channel_multiplier=1
                ).then_inc(ident_ready, 1)
                pool.affine_select(
                    out=g.causal[:], in_=g.causal[:], compare_op=ALU.is_ge, fill=-1e30, base=0, pattern=[[-1, P]], channel_multiplier=1
                )
                pool.affine_select(
                    out=g.before[:], in_=g.ones_b[:], compare_op=ALU.is_gt, fill=0.0, base=0, pattern=[[1, P]], channel_multiplier=-1
                )

            @block.scalar
            def _(act):
                act.wait_ge(zeroed, 2)
                act.dma_start(nat[0:E, W_ROUTER0, :], dram["L0_ffn_router_w"]).then_inc(w1_loaded, 16)
                act.dma_start(nat[:, W_QKV1 : W_QKV1 + 3, :], dram["L1_attn_in_proj_w"].rearrange("(n p) c -> p n c", p=P)).then_inc(w1_loaded, 16)
                act.dma_start(nat[:, W_OUT1, :], dram["L1_attn_out_proj_w"]).then_inc(w1_loaded, 16)
                act.dma_start(nat[0:RQ, W_QK1, :], dram["L1_attn_Qp_w"]).then_inc(w1_loaded, 16)
                act.dma_start(nat[RQ : 2 * RQ, W_QK1, :], dram["L1_attn_Kp_w"]).then_inc(w1_loaded, 16)
                act.dma_start(nat[:, W_V1, :], dram["L1_attn_Vp_w"]).then_inc(w1_loaded, 16)
                act.dma_start(nat[:, W_FF1 : W_FF1 + FC, :], dram["L1_attn_ff1_w"].rearrange("(k p) c -> p k c", p=P)).then_inc(w1_loaded, 16)
                act.dma_start(nat[:, W_FF2 : W_FF2 + FC, :].rearrange("p k f -> p (k f)"), dram["L1_attn_ff2_w"]).then_inc(w1_loaded, 16)
                bias = nat[:, W_BIAS, :]
                act.dma_start(bias[B_DOWN1 : B_DOWN1 + E, :], dram["L1_ffn_b2"]).then_inc(w1_loaded, 16)
                act.dma_start(bias[B_UP1 : B_UP1 + E * FC, :], dram["L1_ffn_b1"].rearrange("e (k p) -> (e k) p", p=P)).then_inc(w1_loaded, 16)
                act.dma_start(bias[B_FF1 : B_FF1 + FC, :], dram["L1_attn_ff1_b"].rearrange("(k p) -> k p", p=P)).then_inc(w1_loaded, 16)
                act.dma_start(bias[B_Q1 : B_Q1 + 2, :], dram["L1_attn_in_proj_b"][0 : 2 * C].rearrange("(k p) -> k p", p=P)).then_inc(w1_loaded, 16)
                act.dma_start(bias[B_SQ1 : B_SQ1 + 1, 0:RQ], dram["L1_attn_Qp_b"].rearrange("(a r) -> a r", a=1)).then_inc(w1_loaded, 16)
                act.dma_start(bias[B_SK1 : B_SK1 + 1, 0:RQ], dram["L1_attn_Kp_b"].rearrange("(a r) -> a r", a=1)).then_inc(w1_loaded, 16)
                for dst, src in g.small_loads(dram):
                    act.dma_start(dst, src).then_inc(rows_loaded, 16)
                act.wait_ge(cond_kept, 1)
                act.activation(cond_e[:], cond_t[:], ACT.Exp, scale=-1.0).then_inc(cond_exp, 1)
                for i in range(0, GROUPS, 2):
                    first, n = group(i)
                    act.wait_ge(turned, i + 1)
                    act.activation(g.weights(first, n), weight_ps[i % 4][:, 0:n, :], ACT.Copy).then_inc(kept_act, 1)
                for i in range(MODS):
                    col, part = i // 2, i % 2
                    act.wait_ge(mod_ready, i + 1)
                    act.activation(g.mods[col // B][:, col % B, part * HALF : part * HALF + HALF], mod_ps[i % 4][:, 0:HALF], ACT.Copy).then_inc(mod_kept, 1)
                act.wait_ge(rows_loaded, 16 * len(g.small_loads(dram)))

            @block.vector
            def _(dve):
                step = Steps(dve, vec)
                dve.wait_ge(cond_turned, 1)
                step(dve.tensor_copy(cond_t[:], mod_ps[0][:, 0 : 2 * B]))
                step.settle()
                dve.tensor_copy(cond_t[:], cond_t[:]).then_inc(cond_kept, 1)
                dve.wait_ge(cond_exp, 1)
                step(dve.tensor_scalar(cond_e[:], cond_e[:], 1.0, None, ALU.add))
                step.settle()
                step(dve.reciprocal(cond_e[:], cond_e[:]))
                step.settle()
                step(dve.tensor_tensor(silu[:], cond_t[:], cond_e[:], ALU.mult))
                step.settle()
                dve.tensor_copy(silu_b[:], silu[:].unsqueeze(2).to_broadcast([P, 2 * B, P])).then_inc(silu_ready, 1)
                for i in range(1, GROUPS, 2):
                    first, n = group(i)
                    dve.wait_ge(turned, i + 1)
                    dve.tensor_copy(g.weights(first, n), weight_ps[i % 4][:, 0:n, :]).then_inc(kept_dve, 1)
                dve.wait_ge(mod_kept, MODS)
                for mod in g.mods:
                    for part in (CA, CB):
                        v = mod[:, :, part * C : part * C + C]
                        step(dve.tensor_scalar(v, v, 1.0, None, ALU.add))
                for layer, part in ((0, GA), (0, GB), (1, GA), (1, GB)):
                    v, s = g.mods[layer][:, :, part * C : part * C + C], gate_sign[:, 2 * layer + (part == GB)]
                    step(dve.tensor_scalar(s, v, 0.0, 2.0, ALU.is_ge, ALU.mult))
                    step.settle()
                    step(dve.tensor_scalar(s, s, -1.0, None, ALU.add))
                    step.settle()
                    step(dve.tensor_tensor(v, v, s, ALU.mult))
                    step.settle()
                    step(dve.scalar_tensor_tensor(out=v, in0=v, scalar=0.25, in1=s, op0=ALU.max, op1=ALU.mult))

            @block.tensor
            def _(pe):
                pe.wait_ge(ident_ready, 1)
                pe.wait_ge(cond_loaded, 64)
                pe.transpose(mod_ps[0][:, 0 : 2 * B], cond[:], g.ident[0 : 2 * B, 0 : 2 * B]).then_inc(cond_turned, 1)
                for i in range(GROUPS):
                    if i == 0:
                        pe.wait_ge(w0_loaded, 64)
                    if i == W0_GROUPS:
                        pe.wait_ge(w1_loaded, 224)
                    if i >= 4:
                        pe.wait_ge(kept_dve if i % 2 else kept_act, (i - 4) // 2 + 1)
                    first, n = group(i)
                    for k in range(n):
                        ins = pe.transpose(weight_ps[i % 4][:, k, :], nat[:, first + k, :], g.ident[:])
                    ins.then_inc(turned, 1)
                pe.wait_ge(silu_ready, 1)
                for i in range(MODS):
                    col, part = i // 2, i % 2
                    if i >= 4:
                        pe.wait_ge(mod_kept, i - 3)
                    pe.matmul(
                        mod_ps[i % 4][:, 0:HALF], silu_b[:, col, :], wmod[:, col // B, part * HALF : part * HALF + HALF], start=True, stop=True
                    ).then_inc(mod_ready, 1)
        a.clear_sems()


def layer_norm(dve, step, st, rows, out, scale, rstd_wait):
    for n in range(NT):
        step(dve.bn_stats(st.stats[:, n, :], rows[:, n, :]))
    step.settle()
    for n in range(NT):
        step(dve.bn_aggr(st.mean_var[:, n, :], st.stats[:, n, :]))
    step.settle()
    dve.tensor_scalar(st.var_eps[:], st.mean_var[:, :, 1], LN_EPS, None, ALU.add).then_inc(st.var_ready, 1)
    rstd_wait()
    for n in range(NT):
        step(
            dve.tensor_scalar(
                out[:, n, :], rows[:, n, :], st.mean_var[:, n, 0:1], st.rstd[:, n : n + 1], ALU.subtract, ALU.mult
            )
        )
    step.settle()
    step(dve.tensor_tensor(out, out, scale, ALU.mult))
    step.settle()


class Norm:

    def __init__(self, a, name, minus_half):
        self.stats = a.sb(f"{name}_stats", [P, NT, 6])
        self.mean_var = a.sb(f"{name}_mean_var", [P, NT, 2])
        self.var_eps = a.sb(f"{name}_var_eps", [P, NT])
        self.rstd = a.sb(f"{name}_rstd", [P, NT])
        self.var_ready = a.sem(f"{name}_var_ready")
        self.rstd_ready = a.sem(f"{name}_rstd_ready")
        self.minus_half = minus_half

    def pool(self, pool, n):
        pool.wait_ge(self.var_ready, n)
        pool.tensor_tensor(self.rstd[:], self.var_eps[:], self.minus_half[:, 0:NT], ALU.pow).then_inc(self.rstd_ready, 1)


def causal_attention(nc, g, rows):
    SCALE = float(C) ** -0.5
    with ExitStack() as ctx:
        a = Alloc(nc, ctx)
        norm = Norm(a, "ln0", g.minus_half)
        h = a.sb("h0", [P, NT, C])
        h_t = a.sb("h0_t", [P, T])
        q_t = a.sb("q0_t", [P, T])
        k_t = a.sb("k0_t", [P, T])
        v = a.sb("v0", [P, NT, C])
        probs = a.sb("probs0", [P, 2, T])
        probs_t = a.sb("probs0_t", [P, NT, P])
        ctx_t = a.sb("ctx0_t", [P, 2, P])
        mx = a.sb("max0", [P, 2])
        nmx = a.sb("minus_max0", [P, 2])
        total = a.sb("total0", [P, NT])
        inv = a.sb("inv0", [P, 2])
        o = a.sb("o0", [P, 2, C])
        scores_ps = [a.ps(f"scores0_ps{i}", [P, T]) for i in range(2)]
        turn_ps = a.ps("turn0_ps", [P, T])
        ctx_ps = a.ps("ctx0_ps", [P, 512])
        out_ps = a.ps("out0_ps", [P, 512])
        vec = a.sem("attn0_vec")
        h_ready = a.sem("h0_ready")
        h_turned = a.sem("h0_turned")
        h_t_ready = a.sem("h0_t_ready")
        q_made = a.sem("q0_made")
        k_made = a.sem("k0_made")
        v_made = a.sem("v0_made")
        q_ready = a.sem("q0_ready")
        k_ready = a.sem("k0_ready")
        v_ready = a.sem("v0_ready")
        scored = a.sem("scored0")
        max_ready = a.sem("max0_ready")
        probs_ready = a.sem("probs0_ready")
        probs_turned = a.sem("probs0_turned")
        probs_t_act = a.sem("probs0_t_act")
        probs_t_dve = a.sem("probs0_t_dve")
        ctx_made = a.sem("ctx0_made")
        ctx_ready = a.sem("ctx0_ready")
        out_made = a.sem("out0_made")
        out_used = a.sem("out0_used")
        cleared = a.sem("rows_cleared")
        H = NT // 2

        with nc.Block() as block:

            @block.sync
            def _(sp):
                for of in rows:
                    of.clear(sp, g.zeros[:], cleared)
                sp.wait_ge(cleared, 16 * len(rows))

            @block.gpsimd
            def _(pool):
                with pool.Fori(0, B) as b:
                    norm.pool(pool, b + 1)

            @block.vector
            def _(dve):
                with dve.Fori(0, B) as b:
                    step = Steps(dve, vec)
                    rows = g.x[:, bass.ds(b * NT, NT), :]
                    layer_norm(dve, step, norm, rows, h[:], g.mod_row(0, b, CA), lambda: dve.wait_ge(norm.rstd_ready, b + 1))
                    dve.tensor_tensor(h[:], h[:], g.mod_row(0, b, SA), ALU.add).then_inc(h_ready, 1)
                    dve.wait_ge(k_made, b + 1)
                    dve.tensor_copy(k_t[:], scores_ps[1][:]).then_inc(k_ready, 1)

                    def row_max(i):
                        n = (i + 1) * P
                        s = scores_ps[i % 2]
                        dve.wait_ge(scored, b * NT + i + 1)
                        step(dve.tensor_tensor(s[:, n - P : n], s[:, n - P : n], g.causal[:], ALU.add))
                        step.settle()
                        step(dve.reduce_max(mx[:, i % 2 : i % 2 + 1], s[:, 0:n], AX.X))
                        step.settle()
                        dve.tensor_scalar(nmx[:, i % 2 : i % 2 + 1], mx[:, i % 2 : i % 2 + 1], -SCALE, None, ALU.mult).then_inc(max_ready, 1)

                    def keep_probs(i):
                        if i >= H:
                            dve.wait_ge(probs_turned, b * NT + i + 1)
                            dve.tensor_copy(
                                probs_t[:, H : i + 1, :], turn_ps[:, H * P : (i + 1) * P].rearrange("p (n c) -> p n c", c=P)
                            ).then_inc(probs_t_dve, 1)

                    def residual(i):
                        one = slice(i % 2, i % 2 + 1)
                        dve.wait_ge(out_made, b * NT + i + 1)
                        step(dve.reciprocal(inv[:, one], total[:, i : i + 1]))
                        step.settle()
                        dve.scalar_tensor_tensor(
                            out=o[:, i % 2, :], in0=out_ps[:, 0:C], scalar=inv[:, one], in1=g.row("L0_attn_out_b"), op0=ALU.mult, op1=ALU.add
                        ).then_inc(out_used, 1)
                        dve.wait_ge(out_used, b * NT + i + 1)
                        step(dve.tensor_tensor(o[:, i % 2, :], o[:, i % 2, :], g.mod_part(0, b, GA), ALU.mult))
                        step.settle()
                        xr = g.x[:, bass.ds(b * NT + i, 1), :].rearrange("p n c -> p (n c)")
                        step(dve.tensor_tensor(xr, xr, o[:, i % 2, :], ALU.add))

                    row_max(0)
                    for i in range(NT):
                        if i + 1 < NT:
                            row_max(i + 1)
                        keep_probs(i)
                        if i >= 1:
                            residual(i - 1)
                    residual(NT - 1)
                    step.again()

            @block.scalar
            def _(act):
                with act.Fori(0, B) as b:
                    for k in range(2):
                        act.wait_ge(h_turned, b * 2 + k + 1)
                        act.activation(h_t[:, k * 512 : k * 512 + 512], turn_ps[:, k * 512 : k * 512 + 512], ACT.Copy).then_inc(h_t_ready, 1)
                    act.wait_ge(q_made, b + 1)
                    act.activation(q_t[:], scores_ps[0][:], ACT.Copy).then_inc(q_ready, 1)
                    act.wait_ge(v_made, b + 1)
                    act.activation(v[:], turn_ps[:].rearrange("p (n c) -> p n c", c=C), ACT.Copy).then_inc(v_ready, 1)

                    def exp(i):
                        one = slice(i % 2, i % 2 + 1)
                        n = (i + 1) * P
                        act.wait_ge(max_ready, b * NT + i + 1)
                        act.activation(
                            probs[:, i % 2, 0:n], scores_ps[i % 2][:, 0:n], ACT.Exp, bias=nmx[:, one], scale=SCALE, accum_out=total[:, i : i + 1]
                        ).then_inc(probs_ready, 1)

                    exp(0)
                    for i in range(NT):
                        m = min(i + 1, H)
                        act.wait_ge(probs_turned, b * NT + i + 1)
                        act.activation(probs_t[:, 0:m, :], turn_ps[:, 0 : m * P].rearrange("p (n c) -> p n c", c=P), ACT.Copy).then_inc(probs_t_act, 1)
                        if i + 1 < NT:
                            exp(i + 1)
                        act.wait_ge(ctx_made, b * NT + i + 1)
                        act.activation(ctx_t[:, i % 2, :], ctx_ps[:, 0:P], ACT.Copy).then_inc(ctx_ready, 1)

            @block.tensor
            def _(pe):
                with pe.Fori(0, B) as b:
                    pe.wait_ge(h_ready, b + 1)
                    for n in range(NT):
                        ins = pe.transpose(turn_ps[:, n * P : n * P + P], h[:, n, :], g.ident[:])
                        if n % H == H - 1:
                            ins.then_inc(h_turned, 1)
                    for k in range(2):
                        cols = slice(k * 512, k * 512 + 512)
                        pe.wait_ge(h_t_ready, b * 2 + k + 1)
                        q_ins = pe.matmul(scores_ps[0][:, cols], g.weights(W_QKV0), h_t[:, cols], start=True, stop=True)
                        if k == 1:
                            q_ins.then_inc(q_made, 1)
                        k_ins = pe.matmul(scores_ps[1][:, cols], g.weights(W_QKV0 + 1), h_t[:, cols], start=True, stop=True)
                        if k == 1:
                            k_ins.then_inc(k_made, 1)
                    for n in range(NT):
                        ins = pe.matmul(turn_ps[:, n * P : n * P + P], h_t[:, n * P : n * P + P], g.weights(W_QKV0 + 2), start=True, stop=True)
                    ins.then_inc(v_made, 1)
                    pe.wait_ge(q_ready, b + 1)
                    pe.wait_ge(k_ready, b + 1)

                    def score(i):
                        n = (i + 1) * P
                        if i >= 2:
                            pe.wait_ge(probs_ready, b * NT + i - 1)
                        for c0 in range(0, n, 512):
                            c1 = min(n, c0 + 512)
                            ins = pe.matmul(scores_ps[i % 2][:, c0:c1], q_t[:, i * P : i * P + P], k_t[:, c0:c1], start=True, stop=True)
                        ins.then_inc(scored, 1)

                    def project(i):
                        pe.wait_ge(ctx_ready, b * NT + i + 1)
                        if i >= 1:
                            pe.wait_ge(out_used, b * NT + i)
                        pe.matmul(out_ps[:, 0:C], ctx_t[:, i % 2, :], g.weights(W_OUT0), start=True, stop=True).then_inc(out_made, 1)

                    score(0)
                    pe.wait_ge(v_ready, b + 1)
                    for i in range(NT):
                        if i + 1 < NT:
                            score(i + 1)
                        pe.wait_ge(probs_ready, b * NT + i + 1)
                        for n in range(i + 1):
                            ins = pe.transpose(turn_ps[:, n * P : n * P + P], probs[:, i % 2, n * P : n * P + P], g.ident[:])
                        ins.then_inc(probs_turned, 1)
                        if i >= 1:
                            project(i - 1)
                        pe.wait_ge(probs_t_act, b * NT + i + 1)
                        if i >= H:
                            pe.wait_ge(probs_t_dve, b * H + i - H + 1)
                        for n in range(i + 1):
                            ins = pe.matmul(ctx_ps[:, 0:P], v[:, n, :], probs_t[:, n, :], start=(n == 0), stop=(n == i))
                        ins.then_inc(ctx_made, 1)
                    project(NT - 1)
        a.clear_sems()


BATCH_TILES = (2 * T // P + E - 1, E * CAPACITY // P)
UNROLL = 4


class ExpertRows:

    def __init__(self, nc, layer):
        self.tiles = BATCH_TILES[layer]
        self.trash = B * self.tiles * P
        self.total = self.trash + (2 * UNROLL if layer == 0 else 2 * NT) * P
        self.rows = nc.dram_tensor(f"expert_rows{layer}_dram", [self.total, C], F32, kind="Internal").ap()

    def clear(self, eng, zeros, sem):
        n = self.total // P
        eng.dma_start(self.rows.rearrange("(p n) c -> p n c", n=n), zeros.unsqueeze(1).to_broadcast([P, n, C])).then_inc(sem, 16)


class Moe:

    def __init__(self, a, rows, layer):
        self.layer, self.tiles, self.slots, self.trash = layer, rows.tiles, rows.tiles * P, rows.trash
        self.rows = rows.rows
        self.gates = a.sb(f"gates{layer}", [P, B, 2, NT])
        self.pick = a.sb(f"pick{layer}", [P, B, 2, NT], I32)
        if layer == 0:
            self.tile_expert = a.sb("tile_expert", [P, B * self.tiles + UNROLL], I32)
            self.b1 = a.sb("up_bias0", [P, E, FF])
            self.b2 = a.sb("down_bias0", [P, E, C])
        else:
            self.up = a.sb("up1", [C, E, FF])
            self.down = a.sb("down1", [P, E * FC, C])

    def loads(self, dram):
        if self.layer == 0:
            return [
                (self.b1[:].rearrange("p e f -> p (e f)"), dram["L0_ffn_expert_b1"].rearrange("e f -> (e f)").partition_broadcast(P)),
                (self.b2[:].rearrange("p e c -> p (e c)"), dram["L0_ffn_expert_b2"].rearrange("e c -> (e c)").partition_broadcast(P)),
            ]
        return [
            (self.up[:], dram["L1_ffn_W1"].rearrange("e c h -> c e h")),
            (self.down[:], dram["L1_ffn_W2"].rearrange("e (k p) c -> p (e k) c", p=P)),
        ]


def route(nc, g, moe, dram, layer):
    with ExitStack() as ctx:
        a = Alloc(nc, ctx, f"_route{layer}")
        stats = a.sb("stats", [P, NT, 6])
        mean_var = a.sb("mean_var", [P, NT, 2])
        mean = a.sb("mean", [P, TILES])
        var_eps = a.sb("var_eps", [P, TILES])
        rstd = a.sb("rstd", [P, TILES])
        halves = a.sb("minus_halves", [P, TILES])
        h = a.sb("h", [P, NT, C])
        h_rows = a.sb("h_rows", [P, NT, C])
        h_t = a.sb("h_t", [P, T])
        logits = a.sb("logits", [P, NT, E])
        expl = a.sb("exp_logits", [P, NT, E])
        best = a.sb("two_best", [P, 2, NT, E])
        masked = a.sb("masked", [P, NT, E])
        sel_b = a.sb("selected_bf16", [P, NT, E], BF16)
        slot = a.sb("slot", [P, NT, E])
        kept = a.sb("kept", [P, NT, E])
        of_best = a.sb("of_best", [P, 2, NT, E])
        row = a.sb("row", [P, 2, NT])
        keep = a.sb("keep", [P, 2, NT])
        send = a.sb("send", [P, 2, NT], I32)
        base = a.sb("base", [P, 1])
        to = a.sb("to", [P, 2, NT])
        trash = a.sb("trash", [P, 2, NT])
        m1 = a.sb("best_logit", [P, NT])
        m2 = a.sb("next_logit", [P, NT])
        rank = a.sb("best_rank", [P, NT])
        total = a.sb("total_exp", [P, NT])
        e2 = a.sb("next_exp", [P, NT])
        share = a.sb("share", [P, NT])
        expert_slot = a.sb("expert_slot", [P, E])
        full_tiles = a.sb("full_tiles", [P, NT])
        earlier = a.sb("earlier", [P, E, E])
        more = a.sb("more", [P, E, NT])
        tiles = a.sb("tiles", [P, E])
        ahead = a.sb("ahead", [P, E, E])
        start = a.sb("start", [P, E])
        tile_no = a.sb("tile_no", [P, moe.tiles])
        begun = a.sb("begun", [P, moe.tiles, E])
        expert = a.sb("expert", [P, moe.tiles])
        turn_ps = a.ps("turn_ps", [P, T])
        logits_ps = a.ps("logits_ps", [P, 512])
        pos_ps = a.ps("pos_ps", [P, 512])
        count_ps = a.ps("count_ps", [P, 512])
        vec = a.sem("vec")
        const_ready = a.sem("const_ready")
        var_ready = a.sem("var_ready")
        rstd_ready = a.sem("rstd_ready")
        h_ready = a.sem("h_ready")
        h_turned = a.sem("h_turned")
        h_t_ready = a.sem("h_t_ready")
        rows_ready = a.sem("rows_ready")
        rows_free = a.sem("rows_free")
        scored = a.sem("logits_made")
        shifted = a.sem("logits_shifted")
        exp_ready = a.sem("logits_exp")
        sel_ready = a.sem("selected_ready")
        pos_made = a.sem("pos_made")
        send_ready = a.sem("send_ready")
        sends = a.sem("pool_rounds")
        sent, sent_before = g.rows_sent, layer * B * 2 * NT * 16
        loaded = a.sem("loaded")
        H = NT // 2

        def tall(ap):
            return ap.unsqueeze(2).to_broadcast([P, NT, E])

        with nc.Block() as block:

            @block.sync
            def _(sp):
                for dst, src in moe.loads(dram):
                    sp.dma_start(dst, src).then_inc(loaded, 16)
                sp.wait_ge(loaded, 16 * len(moe.loads(dram)))

            @block.gpsimd
            def _(pool):
                pool.memset(halves[:], -0.5).then_inc(const_ready, 1)
                if layer == 0:
                    for n in range(NT):
                        pool.memset(full_tiles[:, n : n + 1], float(n * P)).then_inc(const_ready, 1)
                    for e in range(E):
                        pool.memset(earlier[:, e, e:E], 0.0).then_inc(const_ready, 1)
                        if e > 0:
                            pool.memset(earlier[:, e, 0:e], 1.0).then_inc(const_ready, 1)
                    pool.memset(moe.tile_expert[:], 0).then_inc(const_ready, 1)
                    pool.iota(tile_no[:], pattern=[[1, moe.tiles]], base=0, channel_multiplier=0, allow_small_or_imprecise_dtypes=True).then_inc(const_ready, 1)
                else:
                    for e in range(E):
                        pool.memset(expert_slot[:, e : e + 1], float(e * CAPACITY)).then_inc(const_ready, 1)
                    pool.iota(trash[:].rearrange("p k n -> p (k n)"), pattern=[[P, 2 * NT]], base=moe.trash, channel_multiplier=1, allow_small_or_imprecise_dtypes=True).then_inc(const_ready, 1)
                consts = 1 + (NT + 2 * E - 1 + 2 if layer == 0 else E + 1)
                pool.wait_ge(const_ready, consts)
                pool.wait_ge(var_ready, 1)
                pool.tensor_tensor(rstd[:], var_eps[:], halves[:], ALU.pow).then_inc(rstd_ready, 1)
                pool.sem_inc(rows_free, 1)
                with pool.Fori(0, B) as b:
                    pool.wait_ge(rows_ready, b + 1)
                    pool.wait_ge(send_ready, b + 1)
                    pool.sem_inc(sends, 1)
                    for k in range(2):
                        for n in range(NT):
                            pool.indirect_dma_start(
                                moe.rows, bass.IndirectOffsetOnAxis(ap=send[:, k, n : n + 1], axis=0), h_rows[:, n, :], None
                            ).then_inc(sent, 16)
                    pool.wait_ge(sent, b * (16 * 2 * NT) + (sent_before + 16 * 2 * NT))
                    pool.sem_inc(rows_free, 1)

            @block.vector
            def _(dve):
                with dve.Fori(0, B) as b:
                    step = Steps(dve, vec)
                    for n in range(NT):
                        step(dve.bn_stats(stats[:, n, :], g.x[:, bass.ds(b * NT + n, 1), :].rearrange("p n c -> p (n c)")))
                    step.settle()
                    for n in range(NT):
                        step(dve.bn_aggr(mean_var[:, n, :], stats[:, n, :]))
                    step.settle()
                    step(dve.tensor_scalar(var_eps[:, bass.ds(b * NT, NT)], mean_var[:, :, 1], LN_EPS, None, ALU.add))
                    step(dve.tensor_copy(mean[:, bass.ds(b * NT, NT)], mean_var[:, :, 0]))
                    step.again()
                step = Steps(dve, vec)
                step(dve.memset(base[:], 0.0))
                step.again()
                dve.sem_inc(var_ready, 1)
                dve.wait_ge(rstd_ready, 1)
                with dve.Fori(0, B) as b:
                    step = Steps(dve, vec)
                    for n in range(NT):
                        at = bass.ds(b * NT + n, 1)
                        step(dve.tensor_scalar(h[:, n, :], g.x[:, at, :].rearrange("p n c -> p (n c)"), mean[:, at], rstd[:, at], ALU.subtract, ALU.mult))
                    step.settle()
                    step(dve.tensor_tensor(h[:], h[:], g.mod_row(layer, b, CB), ALU.mult))
                    step.settle()
                    dve.tensor_tensor(h[:], h[:], g.mod_row(layer, b, SB), ALU.add).then_inc(h_ready, 1)
                    dve.wait_ge(scored, b + 1)
                    step(dve.tensor_copy(logits[:].rearrange("p n e -> p (n e)"), logits_ps[:, 0 : NT * E]))
                    step.settle()
                    step(dve.reduce_max(m1[:], logits[:], AX.X))
                    step.settle()
                    dve.tensor_tensor(expl[:], logits[:], tall(m1[:]), ALU.subtract).then_inc(shifted, 1)

                    def choose(chosen, of, top):
                        step(dve.tensor_tensor(chosen, of[:], tall(top[:]), ALU.is_equal))
                        step.settle()
                        step(dve.tensor_tensor(chosen, chosen, bc(g.expert_rank[:], NT), ALU.mult))
                        step.settle()
                        step(dve.reduce_max(rank[:], chosen, AX.X))
                        step.settle()
                        step(dve.tensor_tensor(chosen, chosen, tall(rank[:]), ALU.is_equal))
                        step.settle()

                    first, second = best[:, 0], best[:, 1]
                    choose(first, logits, m1)
                    step(dve.scalar_tensor_tensor(out=masked[:], in0=first, scalar=-1e30, in1=logits[:], op0=ALU.mult, op1=ALU.add))
                    step.settle()
                    step(dve.reduce_max(m2[:], masked[:], AX.X))
                    step.settle()
                    choose(second, masked, m2)
                    dve.tensor_tensor(sel_b[:], first, second, ALU.add).then_inc(sel_ready, 1)
                    dve.wait_ge(exp_ready, b + 1)
                    step(dve.reduce_sum(total[:], expl[:], AX.X))
                    step(dve.tensor_tensor(masked[:], expl[:], second, ALU.mult))
                    step.settle()
                    step(dve.reduce_sum(e2[:], masked[:], AX.X))
                    step.settle()
                    if layer == 0:
                        step(dve.scalar_tensor_tensor(out=total[:], in0=total[:], scalar=1e-9, in1=e2[:], op0=ALU.mult, op1=ALU.add))
                        step.settle()
                        step(dve.tensor_scalar(total[:], total[:], 1.0, None, ALU.add))
                        step.settle()
                    step(dve.reciprocal(share[:], total[:]))
                    step.settle()
                    step(dve.tensor_tensor(e2[:], e2[:], share[:], ALU.mult))
                    dve.wait_ge(pos_made, b + 1)
                    pos = pos_ps[:, 0 : NT * E].rearrange("p (n e) -> p n e", e=E)
                    if layer == 0:
                        step(dve.tensor_tensor(more[:], count_ps[:, 0:E].unsqueeze(2).to_broadcast([P, E, NT]), bc(full_tiles[:], E), ALU.is_gt))
                        step.settle()
                        step(dve.reduce_sum(tiles[:], more[:], AX.X))
                        step.settle()
                        step(dve.tensor_tensor(ahead[:], bc(tiles[:], E), earlier[:], ALU.mult))
                        step.settle()
                        step(dve.reduce_sum(start[:], ahead[:], AX.X))
                        step.settle()
                        step(dve.scalar_tensor_tensor(out=slot[:], in0=bc(start[:], NT), scalar=float(P), in1=pos, op0=ALU.mult, op1=ALU.add))
                        step(dve.tensor_tensor(begun[:], bc(start[:], moe.tiles), tile_no[:].unsqueeze(2).to_broadcast([P, moe.tiles, E]), ALU.is_le))
                        step.settle()
                        step(dve.reduce_sum(expert[:], begun[:], AX.X))
                        step.settle()
                        step(dve.tensor_scalar(moe.tile_expert[:, bass.ds(b * moe.tiles, moe.tiles)], expert[:], -1.0, None, ALU.add))
                    else:
                        step(dve.tensor_scalar(kept[:], pos, float(CAPACITY), None, ALU.is_lt))
                        step(dve.scalar_tensor_tensor(out=slot[:], in0=pos, scalar=float(CAPACITY - 1), in1=bc(expert_slot[:], NT), op0=ALU.min, op1=ALU.add))
                        step.settle()
                    both = lambda ap: ap.unsqueeze(1).to_broadcast([P, 2, NT, E])
                    step(dve.tensor_tensor(of_best[:], best[:], both(slot[:]), ALU.mult))
                    step.settle()
                    step(dve.reduce_sum(row[:], of_best[:], AX.X))
                    step.settle()
                    step(dve.tensor_scalar(row[:], row[:], base[:, 0:1], None, ALU.add))
                    one = bass.ds(b, 1)
                    gate = lambda k: moe.gates[:, one, k, :].rearrange("p b n -> p (b n)")
                    if layer == 0:
                        step.settle()
                        dve.wait_ge(rows_free, b + 1)
                        dve.tensor_copy(send[:], row[:]).then_inc(send_ready, 1)
                        step(dve.tensor_copy(gate(0), share[:]))
                        step(dve.tensor_copy(gate(1), e2[:]))
                    else:
                        step(dve.tensor_tensor(of_best[:], best[:], both(kept[:]), ALU.mult))
                        step.settle()
                        step(dve.reduce_sum(keep[:], of_best[:], AX.X))
                        step.settle()
                        step(dve.tensor_tensor(to[:], row[:], trash[:], ALU.subtract))
                        step.settle()
                        step(dve.tensor_tensor(to[:], to[:], keep[:], ALU.mult))
                        step.settle()
                        dve.wait_ge(rows_free, b + 1)
                        dve.tensor_tensor(send[:], to[:], trash[:], ALU.add).then_inc(send_ready, 1)
                        step(dve.tensor_tensor(gate(0), share[:], keep[:, 0], ALU.mult))
                        step(dve.tensor_tensor(gate(1), e2[:], keep[:, 1], ALU.mult))
                    step(dve.tensor_copy(moe.pick[:, one].rearrange("p b k n -> p (b k) n"), row[:]))
                    step(dve.tensor_scalar(base[:], base[:], float(moe.slots), None, ALU.add))
                    dve.wait_ge(rows_ready, b + 1)
                    dve.wait_ge(send_ready, b + 1)
                    dve.sem_inc(vec, 1)
                    step.n += 1
                    step.again()

            @block.scalar
            def _(act):
                with act.Fori(0, B) as b:
                    for k in range(2):
                        act.wait_ge(h_turned, b * 2 + k + 1)
                        act.activation(h_t[:, k * 512 : k * 512 + 512], turn_ps[:, k * 512 : k * 512 + 512], ACT.Copy).then_inc(h_t_ready, 1)
                    act.wait_ge(rows_free, b + 1)
                    act.activation(h_rows[:], h[:], ACT.Copy).then_inc(rows_ready, 1)
                    act.wait_ge(shifted, b + 1)
                    act.activation(expl[:], expl[:], ACT.Exp).then_inc(exp_ready, 1)

            @block.tensor
            def _(pe):
                router = g.weights(W_ROUTER0)[:, 0:E] if layer == 0 else g.wr1[:]
                with pe.Fori(0, B) as b:
                    pe.wait_ge(h_ready, b + 1)
                    for n in range(NT):
                        ins = pe.transpose(turn_ps[:, n * P : n * P + P], h[:, n, :], g.ident[:])
                        if n % H == H - 1:
                            ins.then_inc(h_turned, 1)
                    pe.wait_ge(h_t_ready, b * 2 + 2)
                    for n in range(NT):
                        ins = pe.matmul(logits_ps[:, n * E : n * E + E], h_t[:, n * P : n * P + P], router, start=True, stop=True)
                    ins.then_inc(scored, 1)
                    pe.wait_ge(sel_ready, b + 1)
                    if layer == 0:
                        for m in range(NT):
                            pe.matmul(count_ps[:, 0:E], g.ones_b[:], sel_b[:, m, :], start=(m == 0), stop=(m == NT - 1))
                    for n in range(NT):
                        for m in range(n + 1):
                            ins = pe.matmul(
                                pos_ps[:, n * E : n * E + E], g.before[:] if m == n else g.ones_b[:], sel_b[:, m, :], start=(m == 0), stop=(m == n)
                            )
                    ins.then_inc(pos_made, 1)
        a.clear_sems()


class Combine:

    def __init__(self, nc, g, moe, a):
        self.g, self.moe = g, moe
        self.pick = a.sb("pick_now", [P, 2, NT], I32)
        self.y = a.sb("picked", [P, 2, NT, C])
        self.vec = a.sem("combine_pool")
        self.picked, self.picked_before = g.rows_picked, moe.layer * B * 2 * NT * 16
        self.rounds = a.sem("combine_rounds")

    def batch(self, pool, b):
        g, moe, y = self.g, self.moe, self.y
        step = Steps(pool, self.vec)
        pool.sem_inc(self.rounds, 1)
        one = bass.ds(b, 1)
        step(pool.tensor_copy(self.pick[:], moe.pick[:, one].rearrange("p b k n -> p (b k) n")))
        step.settle()
        for k in range(2):
            for n in range(NT):
                pool.indirect_dma_start(y[:, k, n, :], None, moe.rows, bass.IndirectOffsetOnAxis(ap=self.pick[:, k, n : n + 1], axis=0)).then_inc(self.picked, 16)
        pool.wait_ge(self.picked, b * (16 * 2 * NT) + (self.picked_before + 16 * 2 * NT))
        rows = y[:].rearrange("p k n c -> p (k n) c")
        gates = moe.gates[:, one].rearrange("p b k n -> p (b k n)").unsqueeze(2).to_broadcast([P, 2 * NT, C])
        step(pool.tensor_tensor(rows, rows, gates, ALU.mult))
        step.settle()
        step(pool.tensor_tensor(y[:, 0], y[:, 0], y[:, 1], ALU.add))
        step.settle()
        step(pool.tensor_tensor(y[:, 0], y[:, 0], g.mod_row(moe.layer, b, GB), ALU.mult))
        step.settle()
        xr = g.x[:, bass.ds(b * NT, NT), :]
        step(pool.tensor_tensor(xr, xr, y[:, 0], ALU.add))
        step.settle()
        step.again()


def experts0(nc, g, moe):
    STEPS = B * moe.tiles // UNROLL
    AHEAD = -(-moe.tiles // UNROLL)
    HALF = UNROLL // 2
    with ExitStack() as ctx:
        a = Alloc(nc, ctx, "_experts0")
        combine = Combine(nc, g, moe, a)
        x_rows = a.sb("x_rows", [P, UNROLL, C])
        x_t = a.sb("x_t", [C, UNROLL, P])
        pre = a.sb("pre", [P, 2, FF])
        hidden = a.sb("hidden", [P, 2, FC, P])
        hidden_t = a.sb("hidden_t", [P, 2, FC, P])
        y_rows = a.sb("y_rows", [P, UNROLL, C])
        xt_ps = a.ps("xt_ps", [C, UNROLL, P])
        up_ps = [a.ps(f"up_ps{i}", [P, FF]) for i in range(2)]
        turn_ps = [a.ps(f"turn_ps{i}", [P, FC, P]) for i in range(2)]
        down_ps = [a.ps(f"down_ps{i}", [P, 512]) for i in range(2)]
        rows_loaded = a.sem("rows_loaded")
        x_turned = a.sem("x_turned")
        x_t_ready = a.sem("x_t_ready")
        up_made = a.sem("up_made")
        pre_ready = a.sem("pre_ready")
        hidden_ready = a.sem("hidden_ready")
        turned = a.sem("turned")
        hidden_t_ready = a.sem("hidden_t_ready")
        down_made = a.sem("down_made")
        y_ready = a.sem("y_ready")
        stored = a.sem("stored")
        y_free = a.sem("y_free")
        up_w = lambda e: g.wt0[:, bass.ds(e * FC + W_UP0, FC), :].rearrange("p k c -> p (k c)")
        down_w = lambda e, k: g.wt0[:, bass.ds(e * FC + (W_DOWN0 + k), 1), :].rearrange("p k c -> p (k c)")

        def expert_of(eng, tile):
            return eng.value_load(moe.tile_expert[0:1, tile : tile + 1] if isinstance(tile, int) else moe.tile_expert[0:1, bass.ds(tile, 1)], min_val=0, max_val=E - 1)

        with nc.Block() as block:

            @block.sync
            def _(sp):
                rows = lambda of, at: of[bass.ds(at * (UNROLL * P), UNROLL * P), :].rearrange("(n p) c -> p n c", p=P)
                sp.dma_start(x_rows[:], moe.rows[0 : UNROLL * P, :].rearrange("(n p) c -> p n c", p=P)).then_inc(rows_loaded, 16)
                sp.sem_inc(y_free, 1)
                sp.wait_ge(x_turned, 1)
                sp.dma_start(x_rows[:], moe.rows[UNROLL * P : 2 * UNROLL * P, :].rearrange("(n p) c -> p n c", p=P)).then_inc(rows_loaded, 16)
                with sp.Fori(0, STEPS) as i:
                    for k in range(2):
                        sp.wait_ge(y_ready, i * UNROLL + (HALF * (k + 1) + 2))
                        at = bass.ds(i * (UNROLL * P) + k * HALF * P, HALF * P)
                        sp.dma_start(moe.rows[at, :].rearrange("(n p) c -> p n c", p=P), y_rows[:, k * HALF : (k + 1) * HALF, :]).then_inc(stored, 16)
                        if k == 0:
                            sp.wait_ge(x_turned, i + 2)
                            sp.dma_start(x_rows[:], rows(moe.rows, i + 2)).then_inc(rows_loaded, 16)
                        sp.wait_ge(stored, i * 32 + (k + 1) * 16)
                        sp.sem_inc(y_free, 1)
                sp.wait_ge(rows_loaded, (STEPS + 2) * 16)
                sp.sem_inc(y_free, 2 * (AHEAD * B - STEPS))

            @block.gpsimd
            def _(pool):
                with pool.Fori(0, B) as b:
                    pool.wait_ge(y_free, b * (2 * AHEAD) + (2 * AHEAD + 1))
                    combine.batch(pool, b)

            @block.vector
            def _(dve):

                def add_bias(tile, k):
                    e = expert_of(dve, tile)
                    dve.wait_ge(up_made, tile + 1)
                    dve.tensor_tensor(
                        pre[:, k % 2, :], up_ps[k % 2][:], moe.b1[:, bass.ds(e, 1), :].rearrange("p e f -> p (e f)"), ALU.add
                    ).then_inc(pre_ready, 1)

                def add_down_bias(i, tile, k):
                    e = expert_of(dve, tile)
                    if k % HALF == 0:
                        dve.wait_ge(y_free, i * 2 + (k // HALF + 1))
                    dve.wait_ge(down_made, tile + 1)
                    dve.tensor_tensor(
                        y_rows[:, k, :], down_ps[k % 2][:, 0:C], moe.b2[:, bass.ds(e, 1), :].rearrange("p e c -> p (e c)"), ALU.add
                    ).then_inc(y_ready, 1)

                dve.sem_inc(y_ready, 2)
                for k in range(2):
                    add_bias(k, k)
                with dve.Fori(0, STEPS) as i:
                    for k in range(UNROLL):
                        add_bias(i * UNROLL + (k + 2), k)
                        add_down_bias(i, i * UNROLL + k, k)

            @block.scalar
            def _(act):

                def keep_x(i):
                    act.wait_ge(x_turned, i + 1)
                    act.activation(x_t[:], xt_ps[:], ACT.Copy).then_inc(x_t_ready, 1)

                def gelu(tile, k):
                    act.wait_ge(pre_ready, tile + 1)
                    act.activation(hidden[:, k % 2].rearrange("p k c -> p (k c)"), pre[:, k % 2, :], ACT.Gelu).then_inc(hidden_ready, 1)

                def keep_turned(tile, k):
                    act.wait_ge(turned, tile + 1)
                    act.activation(hidden_t[:, k % 2], turn_ps[k % 2][:], ACT.Copy).then_inc(hidden_t_ready, 1)

                keep_x(0)
                for k in range(2):
                    gelu(k, k)
                with act.Fori(0, STEPS) as i:
                    for k in range(UNROLL):
                        keep_turned(i * UNROLL + k, k)
                        if k == 1:
                            keep_x(i + 1)
                        gelu(i * UNROLL + (k + 2), k)

            @block.tensor
            def _(pe):

                def turn_x():
                    for k in range(UNROLL):
                        ins = pe.transpose(xt_ps[:, k, :], x_rows[:, k, :], g.ident[:])
                    ins.then_inc(x_turned, 1)

                def go_up(tile, k):
                    e = expert_of(pe, tile)
                    pe.matmul(up_ps[k % 2][:], x_t[:, k % UNROLL, :], up_w(e), start=True, stop=True).then_inc(up_made, 1)

                def turn_hidden(tile, k):
                    pe.wait_ge(hidden_ready, tile + 1)
                    for c in range(FC):
                        ins = pe.transpose(turn_ps[k % 2][:, c, :], hidden[:, k % 2, c, :], g.ident[:])
                    ins.then_inc(turned, 1)

                def go_down(tile, k):
                    e = expert_of(pe, tile)
                    pe.wait_ge(hidden_t_ready, tile + 1)
                    pe.wait_ge(y_ready, tile + 1)
                    for c in range(FC):
                        ins = pe.matmul(down_ps[k % 2][:, 0:C], hidden_t[:, k % 2, c, :], down_w(e, c), start=(c == 0), stop=(c == FC - 1))
                    ins.then_inc(down_made, 1)

                pe.wait_ge(rows_loaded, 16)
                turn_x()
                pe.wait_ge(x_t_ready, 1)
                for k in range(2):
                    go_up(k, k)
                with pe.Fori(0, STEPS) as i:
                    for k in range(UNROLL):
                        tile = i * UNROLL + k
                        turn_hidden(tile, k)
                        if k == 2:
                            pe.wait_ge(x_t_ready, i + 2)
                        go_up(i * UNROLL + (k + 2), k + 2)
                        if k == 1:
                            pe.wait_ge(rows_loaded, i * 16 + 32)
                            turn_x()
                        go_down(tile, k)
        a.clear_sems()


def experts1(nc, g, moe):
    ROWS_BATCH = moe.slots
    PARTS = [(n, min(n + 4, moe.tiles)) for n in range(0, moe.tiles, 4)]
    with ExitStack() as ctx:
        a = Alloc(nc, ctx, "_experts1")
        combine = Combine(nc, g, moe, a)
        x_rows = a.sb("x_rows", [P, moe.tiles, C])
        x_t = a.sb("x_t", [C, ROWS_BATCH])
        hidden = a.sb("hidden", [P, 2, FC, CAPACITY])
        y_t = a.sb("y_t", [C, ROWS_BATCH])
        y_rows = a.sb("y_rows", [P, moe.tiles, C])
        turn_ps = [a.ps(f"turn_ps{i}", [P, 4, P]) for i in range(2)]
        up_ps = [a.ps(f"up_ps{i}", [P, FC, 256]) for i in range(2)]
        down_ps = [a.ps(f"down_ps{i}", [C, 512]) for i in range(2)]
        rows_loaded = a.sem("rows_loaded")
        x_turned = a.sem("x_turned")
        x_t_ready = a.sem("x_t_ready")
        up_made = a.sem("up_made")
        hidden_act = a.sem("hidden_act")
        hidden_dve = a.sem("hidden_dve")
        down_made = a.sem("down_made")
        y_t_ready = a.sem("y_t_ready")
        y_turned = a.sem("y_turned")
        y_ready = a.sem("y_ready")
        stored = a.sem("stored")
        sp_rounds = a.sem("sp_rounds")
        NP = len(PARTS)
        H = FC // 2

        with nc.Block() as block:

            @block.sync
            def _(sp):
                rows = lambda of: of.rearrange("(n p) c -> p n c", p=P)
                sp.dma_start(x_rows[:], rows(moe.rows[0:ROWS_BATCH])).then_inc(rows_loaded, 16)
                with sp.Fori(0, B) as b:
                    sp.wait_ge(x_turned, b * NP + NP)
                    sp.dma_start(x_rows[:], rows(moe.rows[bass.ds(b * ROWS_BATCH + ROWS_BATCH, ROWS_BATCH), :])).then_inc(rows_loaded, 16)
                    sp.wait_ge(y_ready, b * NP + NP)
                    sp.dma_start(rows(moe.rows[bass.ds(b * ROWS_BATCH, ROWS_BATCH), :]), y_rows[:]).then_inc(stored, 16)
                    sp.wait_ge(stored, b * 16 + 16)
                    sp.sem_inc(sp_rounds, 1)
                sp.wait_ge(rows_loaded, (B + 1) * 16)

            @block.gpsimd
            def _(pool):
                with pool.Fori(0, B) as b:
                    pool.wait_ge(stored, b * 16 + 16)
                    combine.batch(pool, b)

            @block.vector
            def _(dve):
                with dve.Fori(0, B) as b:

                    def relu(e):
                        dve.wait_ge(up_made, b * E + (e + 1))
                        for k in range(H, FC):
                            dve.tensor_scalar(
                                hidden[:, e % 2, k, :], up_ps[e % 2][:, k, 0:CAPACITY], g.bias(B_UP1 + e * FC + k), 0.0, ALU.add, ALU.max
                            ).then_inc(hidden_dve, 1)

                    def add_bias(e):
                        dve.wait_ge(down_made, b * E + (e + 1))
                        dve.tensor_scalar(
                            y_t[:, e * CAPACITY : (e + 1) * CAPACITY], down_ps[e % 2][:, 0:CAPACITY], g.bias(B_DOWN1 + e), None, ALU.add
                        ).then_inc(y_t_ready, 1)

                    relu(0)
                    for e in range(1, E):
                        relu(e)
                        add_bias(e - 1)
                    add_bias(E - 1)
                    for n, (n0, n1) in enumerate(PARTS):
                        dve.wait_ge(y_turned, b * NP + (n + 1))
                        dve.tensor_copy(y_rows[:, n0:n1, :], turn_ps[n % 2][:, 0 : n1 - n0, :]).then_inc(y_ready, 1)
                    dve.wait_ge(stored, b * 16 + 16)
                    dve.sem_inc(sp_rounds, 1)

            @block.scalar
            def _(act):
                with act.Fori(0, B) as b:
                    for n, (n0, n1) in enumerate(PARTS):
                        act.wait_ge(x_turned, b * NP + (n + 1))
                        act.activation(x_t[:, n0 * P : n1 * P].rearrange("p (n c) -> p n c", c=P), turn_ps[n % 2][:, 0 : n1 - n0, :], ACT.Copy).then_inc(x_t_ready, 1)
                    for e in range(E):
                        act.wait_ge(up_made, b * E + (e + 1))
                        for k in range(H):
                            act.activation(
                                hidden[:, e % 2, k, :], up_ps[e % 2][:, k, 0:CAPACITY], ACT.Relu, bias=g.bias(B_UP1 + e * FC + k)
                            ).then_inc(hidden_act, 1)

            @block.tensor
            def _(pe):
                with pe.Fori(0, B) as b:

                    def go_up(e):
                        if e >= 2:
                            pe.wait_ge(hidden_act, b * (E * H) + (e - 1) * H)
                            pe.wait_ge(hidden_dve, b * (E * H) + (e - 1) * H)
                        for k in range(FC):
                            ins = pe.matmul(
                                up_ps[e % 2][:, k, 0:CAPACITY], moe.up[:, e, k * P : k * P + P], x_t[:, e * CAPACITY : (e + 1) * CAPACITY], start=True, stop=True
                            )
                        ins.then_inc(up_made, 1)

                    def go_down(e):
                        pe.wait_ge(hidden_act, b * (E * H) + (e + 1) * H)
                        pe.wait_ge(hidden_dve, b * (E * H) + (e + 1) * H)
                        if e >= 2:
                            pe.wait_ge(y_t_ready, b * E + (e - 1))
                        for k in range(FC):
                            ins = pe.matmul(
                                down_ps[e % 2][:, 0:CAPACITY], moe.down[:, e * FC + k, :], hidden[:, e % 2, k, :], start=(k == 0), stop=(k == FC - 1)
                            )
                        ins.then_inc(down_made, 1)

                    pe.wait_ge(rows_loaded, b * 16 + 16)
                    for n, (n0, n1) in enumerate(PARTS):
                        if n >= 2:
                            pe.wait_ge(x_t_ready, b * NP + (n - 1))
                        for m in range(n0, n1):
                            ins = pe.transpose(turn_ps[n % 2][:, m - n0, :], x_rows[:, m, :], g.ident[:])
                        ins.then_inc(x_turned, 1)
                    pe.wait_ge(x_t_ready, b * NP + NP)
                    go_up(0)
                    for e in range(1, E):
                        go_up(e)
                        go_down(e - 1)
                    go_down(E - 1)
                    pe.wait_ge(y_t_ready, b * E + E)
                    for n, (n0, n1) in enumerate(PARTS):
                        if n >= 2:
                            pe.wait_ge(y_ready, b * NP + (n - 1))
                        for m in range(n0, n1):
                            ins = pe.transpose(turn_ps[n % 2][:, m - n0, :], y_t[:, m * P : m * P + P], g.ident[:])
                        ins.then_inc(y_turned, 1)
                    pe.wait_ge(y_ready, b * NP + NP)


ROWS = ["L0_attn_out_b", "L1_attn_out_proj_b", "L1_attn_Vp_b", "L1_attn_ff2_b", "L1_attn_ln1_g", "L1_attn_ln1_b", "L1_attn_ln2_g", "L1_attn_ln2_b"]


class Shared:

    def __init__(self, a):
        self.x = a.sb("x", [P, TILES, C])
        self.ident = a.sb("ident", [P, P])
        self.causal = a.sb("causal", [P, P])
        self.minus_half = a.sb("minus_half", [P, 16])
        self.mods = [None, a.sb("mod1", [P, B, 6 * C])]
        self.wt1 = a.sb("weights1_t", [P, W_SLOTS - W_SLOTS_L0, P])
        self.rows = a.sb("bias_rows", [P, len(ROWS), C])
        self.lam = a.sb("lam", [P, 1])
        self.v_bias = a.sb("v_bias", [P, C])
        self.expert_rank = a.sb("expert_rank", [P, E])
        self.before = a.sb("before", [P, P], BF16)
        self.ones_b = a.sb("ones_bf16", [P, P], BF16)
        self.rows_sent = a.sem("rows_sent")
        self.rows_picked = a.sem("rows_picked")
        self.zeros = a.sb("zeros", [P, C])
        self.wr1 = a.sb("router1", [C, E])

    def bias(self, row):
        return self.weights(W_BIAS)[:, row : row + 1]

    def weights(self, slot, n=None):
        w, at = (self.wt0, slot) if slot < W_SLOTS_L0 else (self.wt1, slot - W_SLOTS_L0)
        return w[:, at, :] if n is None else w[:, at : at + n, :]

    def row(self, name):
        return self.rows[:, ROWS.index(name), :]

    def mod_part(self, layer, b, part):
        return self.mods[layer][:, bass.ds(b, 1), part * C : part * C + C].rearrange("p n c -> p (n c)")

    def mod_row(self, layer, b, part):
        return self.mods[layer][:, bass.ds(b, 1), part * C : part * C + C].to_broadcast([P, NT, C])

    def small_loads(self, dram):
        return [(self.rows[:, i, :], dram[n].partition_broadcast(P)) for i, n in enumerate(ROWS)] + [
            (self.wr1[:], dram["L1_ffn_Wr"]),
            (self.lam[:], dram["L1_attn_lam"].partition_broadcast(P)),
            (self.v_bias[:], dram["L1_attn_in_proj_b"][2 * C : 3 * C].partition_broadcast(P)),
        ]


def store(nc, g, out):
    with ExitStack() as ctx:
        a = Alloc(nc, ctx)
        stored = a.sem("stored")
        with nc.Block() as block:

            @block.sync
            def _(sp):
                sp.dma_start(out.rearrange("b (n p) c -> p (b n) c", p=P), g.x[:]).then_inc(stored, 16)
                sp.wait_ge(stored, 16)


HEADS, DH = 16, 8
GROUPS = HEADS // 4
PIECES = 3
SHIFT_ROW = PIECES * PIECES * DH
PACK_ROWS = SHIFT_ROW + PIECES
TOP = max(1, int(T * 0.2))
SCALE1 = float(DH) ** -0.5
HEADROOM = 60.0
FLOOR = 50.0


class Scratch:

    def __init__(self, nc):
        self.q = nc.dram_tensor("q_pieces_dram", [B, PIECES, C, T], BF16, kind="Internal").ap()
        self.k = nc.dram_tensor("k_pieces_dram", [B, PIECES, C, T], BF16, kind="Internal").ap()
        self.shift = nc.dram_tensor("shift_pieces_dram", [B, PIECES, HEADS, T], BF16, kind="Internal").ap()
        self.v = nc.dram_tensor("v_dram", [B, NT, P, C], F32, kind="Internal").ap()
        self.sparse_q = nc.dram_tensor("sparse_q_dram", [B, RQ, T], F32, kind="Internal").ap()
        self.sparse_out = nc.dram_tensor("sparse_out_dram", [B, NT, P, C], F32, kind="Internal").ap()


class Fused:

    def __init__(self, a):
        self.v = a.sb("v1", [P, TILES, C])
        self.sparse_k = a.sb("sparse_k", [P, B * T])
        self.sparse_v = a.sb("sparse_v", [P, TILES, C])
        self.minus_mean = a.sb("minus_mean", [P, TILES])
        self.doubt = a.sb("doubt", [P, 2])


def prepare(nc, g, f, scratch, dram):
    with ExitStack() as ctx:
        a = Alloc(nc, ctx)
        norm = Norm(a, "ln1", g.minus_half)
        h = a.sb("h1", [P, NT, C])
        h_t = a.sb("h1_t", [P, T])
        q = a.sb("q1", [P, T])
        k = a.sb("k1", [P, T])
        rest = a.sb("rest", [P, 2, T])
        q_p = a.sb("q1_pieces", [P, PIECES, T], BF16)
        k_p = a.sb("k1_pieces", [P, PIECES, T], BF16)
        square = a.sb("square", [P, 2, T])
        head_sum = a.sb("head_sum", [P, HEADS])
        bound = a.sb("bound", [HEADS, T])
        shift = a.sb("shift", [HEADS, T])
        shift_rest = a.sb("shift_rest", [HEADS, T])
        shift_p = a.sb("shift_pieces", [HEADS, PIECES, T], BF16)
        k_max = a.sb("k_max", [HEADS, 1])
        sq = a.sb("sparse_q_t", [P, T])
        sk_sum = a.sb("sparse_k_sum", [P, 1])
        sq_w = a.sb("sparse_q_w", [P, P])
        sk_w = a.sb("sparse_k_w", [P, P])
        ps_a = a.ps("prep_ps_a", [P, T])
        ps_b = a.ps("prep_ps_b", [P, T])
        ps_c = a.ps("prep_ps_c", [P, T])
        ps_d = a.ps("prep_ps_d", [P, T])
        vec = a.sem("prep_vec")
        const_ready = a.sem("prep_const")
        pads_ready = a.sem("pads_ready")
        h_ready = a.sem("h1_ready")
        h_turned = a.sem("h1_turned")
        h_t_ready = a.sem("h1_t_ready")
        q_made = a.sem("q1_made")
        k_made = a.sem("k1_made")
        v_made = a.sem("v1_made")
        q_ready = a.sem("q1_ready")
        k_ready = a.sem("k1_ready")
        v_ready = a.sem("v1_ready")
        sq_made = a.sem("sparse_q_made")
        sk_made = a.sem("sparse_k_made")
        sv_made = a.sem("sparse_v_made")
        sq_ready = a.sem("sparse_q_ready")
        sk_ready = a.sem("sparse_k_ready")
        mean_made = a.sem("sparse_mean_made")
        q_squared = a.sem("q1_squared")
        k_squared = a.sem("k1_squared")
        norms_made = a.sem("norms_made")
        norms_used = a.sem("norms_used")
        bound_ready = a.sem("bound_ready")
        sqrt_ready = a.sem("sqrt_ready")
        piece = a.sem("pieces_act")
        left = a.sem("pieces_dve")
        shift_ready = a.sem("shift_ready")
        stored = a.sem("prep_stored")
        sp_rounds = a.sem("prep_sp_rounds")
        STORES = 3 * PIECES + 2

        with nc.Block() as block:

            @block.gpsimd
            def _(pool):
                pool.memset(head_sum[:], 1.0).then_inc(const_ready, 1)
                pool.wait_ge(const_ready, 1)
                pool.affine_select(
                    out=head_sum[:], in_=head_sum[:], compare_op=ALU.is_ge, fill=0.0, base=0, pattern=[[-DH, HEADS]], channel_multiplier=1
                ).then_inc(const_ready, 1)
                pool.wait_ge(const_ready, 2)
                pool.affine_select(
                    out=head_sum[:], in_=head_sum[:], compare_op=ALU.is_ge, fill=0.0, base=DH - 1, pattern=[[DH, HEADS]], channel_multiplier=-1
                ).then_inc(const_ready, 1)
                with pool.Fori(0, B) as b:
                    norm.pool(pool, b + 1)

            @block.vector
            def _(dve):
                step = Steps(dve, vec)
                step(dve.memset(sq_w[:], 0.0))
                step(dve.memset(sk_w[:], 0.0))
                step.settle()
                dve.tensor_copy(sq_w[:, 0:RQ], g.weights(W_QK1)[:, 0:RQ]).then_inc(pads_ready, 1)
                dve.tensor_copy(sk_w[:, 0:RQ], g.weights(W_QK1)[:, RQ : 2 * RQ]).then_inc(pads_ready, 1)
                step.again()
                with dve.Fori(0, B) as b:
                    step = Steps(dve, vec)
                    rows = g.x[:, bass.ds(b * NT, NT), :]
                    layer_norm(dve, step, norm, rows, h[:], g.mod_row(1, b, CA), lambda: dve.wait_ge(norm.rstd_ready, b + 1))
                    dve.tensor_tensor(h[:], h[:], g.mod_row(1, b, SA), ALU.add).then_inc(h_ready, 1)
                    dve.wait_ge(k_made, b + 1)
                    dve.tensor_scalar(k[:], ps_c[:], g.bias(B_K1), None, ALU.add).then_inc(k_ready, 1)
                    dve.wait_ge(v_made, b + 1)
                    dve.tensor_tensor(
                        f.v[:, bass.ds(b * NT, NT), :], ps_a[:].rearrange("p (n c) -> p n c", c=C), bc(g.v_bias[:], NT), ALU.add
                    ).then_inc(v_ready, 1)
                    dve.wait_ge(sq_made, b + 1)
                    dve.tensor_scalar(sq[:], ps_b[:], g.bias(B_SQ1), float(RQ) ** -0.5, ALU.add, ALU.mult).then_inc(sq_ready, 1)
                    for i in range(PIECES - 1):
                        for n, (whole, pieces) in enumerate(((q, q_p), (k, k_p))):
                            dve.wait_ge(piece, b * 4 + 2 * i + n + 1)
                            of = whole[:] if i == 0 else rest[:, n, :]
                            to = rest[:, n, :] if i == 0 else pieces[:, 2, :]
                            dve.tensor_tensor(to, of, pieces[:, i, :], ALU.subtract).then_inc(left, 1)
                    dve.wait_ge(sv_made, b + 1)
                    step(
                        dve.tensor_tensor(
                            f.sparse_v[:, bass.ds(b * NT, NT), :], ps_a[:].rearrange("p (n c) -> p n c", c=C), bc(g.row("L1_attn_Vp_b"), NT), ALU.add
                        )
                    )
                    dve.wait_ge(mean_made, b + 1)
                    step(dve.tensor_scalar(f.minus_mean[:, bass.ds(b * NT, NT)], ps_b[:, 0:NT], -1.0 / T, None, ALU.mult))
                    dve.wait_ge(norms_made, 2 * b + 1)
                    dve.reduce_max(k_max[:], ps_d[0:HEADS, :], AX.X).then_inc(norms_used, 1)
                    dve.wait_ge(norms_used, 2 * b + 1)
                    dve.wait_ge(norms_made, 2 * b + 2)
                    dve.tensor_scalar(bound[:], ps_d[0:HEADS, :], k_max[:, 0:1], 1e-30, ALU.mult, ALU.max).then_inc(norms_used, 1)
                    dve.wait_ge(sqrt_ready, b + 1)
                    step(dve.tensor_scalar(shift[:], bound[:], -1.0, HEADROOM / SCALE1, ALU.mult, ALU.add))
                    step.settle()
                    step(dve.tensor_copy(shift_p[:, 0, :], shift[:]))
                    step.settle()
                    step(dve.tensor_tensor(shift_rest[:], shift[:], shift_p[:, 0, :], ALU.subtract))
                    step.settle()
                    step(dve.tensor_copy(shift_p[:, 1, :], shift_rest[:]))
                    step.settle()
                    dve.tensor_tensor(shift_p[:, 2, :], shift_rest[:], shift_p[:, 1, :], ALU.subtract).then_inc(shift_ready, 1)
                    step.again()

            @block.scalar
            def _(act):
                with act.Fori(0, B) as b:
                    for n in range(2):
                        act.wait_ge(h_turned, b * 2 + n + 1)
                        act.activation(h_t[:, n * 512 : n * 512 + 512], ps_a[:, n * 512 : n * 512 + 512], ACT.Copy).then_inc(h_t_ready, 1)
                    act.wait_ge(q_made, b + 1)
                    act.activation(q[:], ps_b[:], ACT.Identity, bias=g.bias(B_Q1)).then_inc(q_ready, 1)
                    act.wait_ge(q_ready, b + 1)
                    act.activation(q_p[:, 0, :], q[:], ACT.Copy).then_inc(piece, 1)
                    act.wait_ge(k_ready, b + 1)
                    act.activation(k_p[:, 0, :], k[:], ACT.Copy).then_inc(piece, 1)
                    act.activation(square[:, 0, :], k[:], ACT.Square).then_inc(k_squared, 1)
                    act.activation(square[:, 1, :], q[:], ACT.Square).then_inc(q_squared, 1)
                    act.wait_ge(sk_made, b + 1)
                    act.activation(f.sparse_k[:, bass.ds(b * T, T)], ps_c[:], ACT.Identity, bias=g.bias(B_SK1), accum_out=sk_sum[:, 0:1]).then_inc(sk_ready, 1)
                    for n, pieces in enumerate((q_p, k_p)):
                        act.wait_ge(left, b * 4 + n + 1)
                        act.activation(pieces[:, 1, :], rest[:, n, :], ACT.Copy).then_inc(piece, 1)
                    act.wait_ge(norms_used, 2 * b + 2)
                    act.activation(bound[:], bound[:], ACT.Sqrt).then_inc(sqrt_ready, 1)
                    act.wait_ge(stored, 16 * STORES * (b + 1))

            @block.sync
            def _(sp):
                with sp.Fori(0, B) as b:

                    def keep(to, of):
                        sp.dma_start(to, of).then_inc(stored, 16)

                    at = bass.ds(b, 1)
                    sp.wait_ge(sq_ready, b + 1)
                    keep(scratch.sparse_q[at].rearrange("b r t -> (b r) t"), sq[0:RQ, :])
                    sp.wait_ge(v_ready, b + 1)
                    keep(scratch.v[at].rearrange("b n p c -> p (b n) c"), f.v[:, bass.ds(b * NT, NT), :])
                    sp.wait_ge(left, b * 4 + 4)
                    for i in range(PIECES):
                        keep(scratch.q[at, i].rearrange("b r t -> (b r) t"), q_p[:, i, :])
                        keep(scratch.k[at, i].rearrange("b r t -> (b r) t"), k_p[:, i, :])
                    sp.wait_ge(shift_ready, b + 1)
                    for i in range(PIECES):
                        keep(scratch.shift[at, i].rearrange("b r t -> (b r) t"), shift_p[:, i, :])
                    sp.wait_ge(stored, 16 * STORES * (b + 1))
                    sp.sem_inc(sp_rounds, 1)

            @block.tensor
            def _(pe):
                pe.wait_ge(const_ready, 3)
                pe.wait_ge(pads_ready, 2)
                with pe.Fori(0, B) as b:

                    def project(to, w, of):
                        for n in range(2):
                            cols = slice(n * 512, n * 512 + 512)
                            ins = pe.matmul(to[0 : w.shape[1], cols], w, of[:, cols], start=True, stop=True)
                        return ins

                    def values(slot):
                        for n in range(NT):
                            ins = pe.matmul(ps_a[:, n * P : n * P + P], h_t[:, n * P : n * P + P], g.weights(slot), start=True, stop=True)
                        return ins

                    pe.wait_ge(h_ready, b + 1)
                    for n in range(NT):
                        ins = pe.transpose(ps_a[:, n * P : n * P + P], h[:, n, :], g.ident[:])
                        if n % 4 == 3:
                            ins.then_inc(h_turned, 1)
                    pe.wait_ge(h_t_ready, b * 2 + 2)
                    project(ps_b, g.weights(W_QKV1), h_t).then_inc(q_made, 1)
                    project(ps_c, g.weights(W_QKV1 + 1), h_t).then_inc(k_made, 1)
                    values(W_QKV1 + 2).then_inc(v_made, 1)
                    pe.wait_ge(q_ready, b + 1)
                    project(ps_b, sq_w[:], h_t).then_inc(sq_made, 1)
                    pe.wait_ge(k_ready, b + 1)
                    project(ps_c, sk_w[:], h_t).then_inc(sk_made, 1)
                    pe.wait_ge(v_ready, b + 1)
                    values(W_V1).then_inc(sv_made, 1)
                    pe.wait_ge(sk_ready, b + 1)
                    pe.wait_ge(sq_ready, b + 1)
                    for n in range(NT):
                        ins = pe.matmul(ps_b[:, n : n + 1], sq[:, n * P : n * P + P], sk_sum[:, 0:1], start=True, stop=True)
                    ins.then_inc(mean_made, 1)
                    pe.wait_ge(k_squared, b + 1)
                    project(ps_d, head_sum[:], square[:, 0, :]).then_inc(norms_made, 1)
                    pe.wait_ge(q_squared, b + 1)
                    pe.wait_ge(norms_used, 2 * b + 1)
                    project(ps_d, head_sum[:], square[:, 1, :]).then_inc(norms_made, 1)
        a.clear_sems()


SEARCH = 7
TRUST = (0.85, 0.8, 0.5, 0.5, 0.35, 0.35)
IN_MIN, IN_MAX = TOP - 7, TOP - 1
AIM = 0.5 * (IN_MIN + IN_MAX)
Z_TOP, DENSITY, MEAN_EXCESS = 0.8416, 0.2800, 0.3989423


def after(eng, sem, count):
    if not isinstance(count, int) or count > 0:
        eng.wait_ge(sem, count)


def attend(nc, g, f, scratch):
    STEPS = 4 * NT
    PER = GROUPS * STEPS
    LAST = GROUPS - 1
    LOADS = 2 * PIECES * PIECES + 1
    with ExitStack() as ctx:
        a = Alloc(nc, ctx)
        q_pack = a.sb("q_pack", [P, 2, 4, T], BF16)
        k_pack = a.sb("k_pack", [P, 2, 4, T], BF16)
        probs = a.sb("probs1", [P, 2, 4, T])
        v_pad = a.sb("v_pad", [P, 2, NT, 4, 32])
        pv = a.sb("pv", [P, T])
        inv = a.sb("pv_inv", [P, NT, 4])
        sq = a.sb("sparse_q_tile", [P, 2, P])
        s = a.sb("sparse_scores", [P, 2, T])
        e = a.sb("sparse_exp", [P, 2, T])
        junk = a.sb("junk", [P, T])
        above = a.sb("above_mean", [P, 2, T], BF16)
        w_t = a.sb("sparse_w_t", [P, NT, P])
        so = a.sb("sparse_out_tile", [P, 2, C])
        excess = a.sb("row_excess", [P, 2])
        top = a.sb("row_max", [P, 2])
        nmax = a.sb("minus_row_max", [P, 2])
        z = a.sb("row_exp_sum", [P, 2])
        at = a.sb("at", [P, 2])
        trust = a.sb("trust", [P, len(TRUST), 2])
        gain = a.sb("gain", [P, len(TRUST), 2])
        count = a.sb("count", [P, 2])
        off = a.sb("off", [P, 2])
        square = a.sb("off_squared", [P, 2])
        near = a.sb("near", [P, NT, 8])
        order = a.sb("order", [P, 8])
        nearer = a.sb("nearer", [P, NT, 8])
        pick = a.sb("pick", [P, 8])
        rank = a.sb("rank", [P, NT])
        cut = a.sb("cut", [P, NT])
        wrong = a.sb("wrong", [P, NT])
        tied = a.sb("tied", [P, NT])
        worst = a.sb("worst", [P, 2])
        w_sum = a.sb("w_sum", [P, 2, 2])
        scores_ps = [a.ps(f"scores1_ps{i}", [P, T]) for i in range(2)]
        pv_ps = a.ps("pv_ps", [P, 2, 512])
        misc = a.ps("misc_ps", [P, T])
        vec = a.sem("attend_vec")
        const_ready = a.sem("attend_const")
        packs_loaded = [a.sem(f"packs_loaded{i}") for i in range(2)]
        sq_loaded = [a.sem(f"sparse_q_loaded{i}") for i in range(2)]
        so_stored = [a.sem(f"sparse_out_stored{i}") for i in range(2)]
        v_staged = a.sem("v_staged")
        scored = a.sem("scored1")
        exp_done = a.sem("exp1_done")
        pv_done = a.sem("pv_done")
        pv_kept = a.sem("pv_kept")
        misc_made = a.sem("misc_made")
        misc_used = a.sem("misc_used")
        scores_kept = a.sem("sparse_scores_kept")
        max_ready = a.sem("sparse_max_ready")
        excess_ready = a.sem("excess_ready")
        sparse_exp = a.sem("sparse_exp_done")
        w_ready = a.sem("sparse_w_ready")
        w_t_ready = a.sem("sparse_w_t_ready")
        out_ready = a.sem("sparse_out_ready")
        USES = 7

        def use(b, group, k):
            if k < 2:
                return b * (USES * GROUPS) + (USES * group - 4 + k) if not (group == 0 and isinstance(b, int)) else k + 1
            return b * (USES * GROUPS) + (USES * group + 3 + k)

        def last_use(k):
            return USES * (B * GROUPS - 1) + 1 + k

        def before(b, group):
            return (b, group - 1) if group > 0 else (b - 1, LAST)

        def over_batches(eng, body, end):
            body(0, True)
            with eng.Fori(1, B) as b:
                body(b, False)
            end(B - 1)

        with nc.Block() as block:

            @block.sync
            def _(sp):

                def store(b, group, made):
                    for t in range(2):
                        sp.wait_ge(out_ready, made(b, group) + t + 1)
                        sp.dma_start(
                            scratch.sparse_out[bass.ds(b, 1), 2 * group + t].rearrange("b p c -> (b p) c"), so[:, t, :]
                        ).then_inc(so_stored[t], 16)

                def outs(b, group):
                    return b * NT + group * 2

                def body(b, first):
                    one = bass.ds(b, 1)
                    for group in range(GROUPS):
                        half = group % 2
                        after(sp, scored, b * PER + (group - 1) * STEPS + 1)
                        for i in range(PIECES):
                            for j in range(PIECES):
                                rows = slice((i * PIECES + j) * DH, (i * PIECES + j + 1) * DH)
                                for pack, of, n in ((q_pack, scratch.q, i), (k_pack, scratch.k, j)):
                                    sp.dma_start(
                                        pack[rows, half], of[one, n, group * 32 : group * 32 + 32].rearrange("b (h d) t -> d (b h) t", d=DH)
                                    ).then_inc(packs_loaded[half], 16)
                        sp.dma_start(
                            q_pack[SHIFT_ROW:PACK_ROWS, half], scratch.shift[one, :, group * 4 : group * 4 + 4].rearrange("b i h t -> (b i) h t")
                        ).then_inc(packs_loaded[half], 16)
                        for t in range(2):
                            tile = group * 2 + t
                            if not (first and group == 0):
                                sp.wait_ge(misc_made, use(*before(b, group), t))
                            sp.dma_start(
                                sq[0:RQ, t, :], scratch.sparse_q[one, :, tile * P : tile * P + P].rearrange("b r t -> (b r) t")
                            ).then_inc(sq_loaded[t], 16)
                        if not (first and group == 0):
                            store(*before(b, group), outs)

                def end(b):
                    store(b, LAST, outs)
                    for t in range(2):
                        sp.wait_ge(so_stored[t], 16 * B * GROUPS)

                sp.wait_ge(const_ready, 6)
                over_batches(sp, body, end)

            @block.gpsimd
            def _(pool):
                pool.memset(v_pad[:], 0.0).then_inc(const_ready, 1)
                pool.wait_ge(const_ready, 1)
                pool.memset(q_pack[64:128], 0.0).then_inc(const_ready, 1)
                pool.wait_ge(const_ready, 2)
                pool.memset(k_pack[64:128], 1.0).then_inc(const_ready, 1)
                pool.wait_ge(const_ready, 3)
                pool.memset(sq[RQ:P], 0.0).then_inc(const_ready, 1)
                pool.wait_ge(const_ready, 4)
                pool.iota(order[:], pattern=[[1, 8]], base=1, channel_multiplier=0, allow_small_or_imprecise_dtypes=True).then_inc(const_ready, 1)
                pool.wait_ge(const_ready, 5)
                for k, part in enumerate(TRUST):
                    pool.memset(trust[:, k, :], part / (T * DENSITY * MEAN_EXCESS))
                pool.memset(v_pad[:, :, :, :, DH : DH + 1], 1.0).then_inc(const_ready, 1)
                pool.wait_ge(const_ready, 6)
                with pool.Fori(0, B) as b:
                    for group in range(GROUPS):
                        if group >= 2:
                            pool.wait_ge(pv_done, (b * GROUPS + group - 1) * NT)
                        pool.tensor_copy(
                            v_pad[:, group % 2, :, :, 0:DH],
                            f.v[:, bass.ds(b * NT, NT), group * 32 : group * 32 + 32].rearrange("p n (h d) -> p n h d", d=DH),
                        ).then_inc(v_staged, 1)
                    pool.wait_ge(pv_done, (b + 1) * GROUPS * NT)

            @block.scalar
            def _(act):

                def rows_excess(b, group, t):
                    act.wait_ge(scores_kept, (b * GROUPS + group) * 2 + t + 1)
                    act.activation(
                        above[:, t, :], s[:, t, :], ACT.Relu, bias=f.minus_mean[:, bass.ds(b * NT + (group * 2 + t), 1)], accum_out=excess[:, t : t + 1]
                    ).then_inc(excess_ready, 1)

                def rows_exp(b, group, t, first):
                    act.wait_ge(max_ready, b * GROUPS + group + 1)
                    if not first:
                        act.wait_ge(misc_made, use(*before(b, group), 3 + 2 * t))
                    act.activation(e[:, t, :], s[:, t, :], ACT.Exp, bias=nmax[:, t : t + 1], accum_out=z[:, t : t + 1]).then_inc(sparse_exp, 1)

                def keep_turned(b, group, t, number):
                    act.wait_ge(misc_made, number)
                    act.activation(w_t[:], misc[:].rearrange("p (n c) -> p n c", n=NT), ACT.Copy).then_inc(w_t_ready, 1)

                def body(b, first):
                    for group in range(GROUPS):
                        alone = first and group == 0
                        prev = before(b, group)
                        side = {
                            3: lambda: rows_excess(b, group, 0),
                            5: lambda: rows_excess(b, group, 1),
                            11: lambda: rows_exp(b, group, 0, alone),
                            17: lambda: rows_exp(b, group, 1, alone),
                        }
                        if not alone:
                            side |= {
                                8: lambda: keep_turned(*prev, 0, use(*prev, 3)),
                                15: lambda: keep_turned(*prev, 1, use(*prev, 5)),
                            }
                        for n in range(STEPS):
                            kt, j = n // 4, n % 4
                            act.wait_ge(scored, b * PER + group * STEPS + n + 2)
                            if j == 0:
                                after(act, pv_done, b * GROUPS * NT + group * NT + kt - 1)
                            act.activation(probs[:, kt % 2, j, :], scores_ps[n % 2][:], ACT.Exp, scale=SCALE1).then_inc(exp_done, 1)
                            if n in side:
                                side[n]()

                def end(b):
                    for t in range(2):
                        keep_turned(b, LAST, t, last_use(3 + 2 * t))

                over_batches(act, body, end)

            @block.tensor
            def _(pe):

                def score(b, group, n):
                    kt, j = n // 4, n % 4
                    if n == 0:
                        pe.wait_ge(packs_loaded[group % 2], 16 * LOADS * (b * 2 + group // 2 + 1))
                    after(pe, exp_done, b * PER + group * STEPS + n - 1)
                    for c in range(2):
                        ins = pe.matmul(
                            scores_ps[n % 2][:, c * 512 : c * 512 + 512],
                            k_pack[:, group % 2, j, kt * P : kt * P + P],
                            q_pack[:, group % 2, j, c * 512 : c * 512 + 512],
                            start=True,
                            stop=True,
                        )
                    ins.then_inc(scored, 1)

                def values(b, group, kt, c):
                    if c == 0:
                        pe.wait_ge(exp_done, b * PER + group * STEPS + kt * 4 + 4)
                        if kt == 0:
                            pe.wait_ge(v_staged, b * GROUPS + group + 1)
                            after(pe, pv_kept, b * GROUPS + group)
                    for j in range(4):
                        ins = pe.matmul(
                            pv_ps[32 * j : 32 * j + 32, c, :],
                            v_pad[:, group % 2, kt, j, :],
                            probs[:, kt % 2, j, c * 512 : c * 512 + 512],
                            start=(kt == 0),
                            stop=(kt == NT - 1),
                        )
                    if c == 1:
                        ins.then_inc(pv_done, 1)

                def free(number):
                    after(pe, misc_used, number - 1)

                def sparse_scores(b, group, t):
                    free(use(b, group, t))
                    pe.wait_ge(sq_loaded[t], 16 * (b * GROUPS + group + 1))
                    for c in range(2):
                        ins = pe.matmul(misc[:, c * 512 : c * 512 + 512], sq[:, t, :], f.sparse_k[:, bass.ds(b * T + c * 512, 512)], start=True, stop=True)
                    ins.then_inc(misc_made, 1)

                def turn_out(b, group, number):
                    free(number)
                    pe.wait_ge(pv_kept, b * GROUPS + group + 1)
                    for n in range(NT):
                        ins = pe.transpose(misc[:, n * P : n * P + P], pv[:, n * P : n * P + P], g.ident[:])
                    ins.then_inc(misc_made, 1)

                def turn_weights(b, group, t, number):
                    free(number)
                    pe.wait_ge(w_ready, b * GROUPS + group + 1)
                    for n in range(NT):
                        ins = pe.transpose(misc[:, n * P : n * P + P], e[:, t, n * P : n * P + P], g.ident[:])
                    ins.then_inc(misc_made, 1)

                def sparse_values(b, group, t):
                    pe.wait_ge(w_t_ready, (b * GROUPS + group) * 2 + t + 1)
                    for n in range(NT):
                        ins = pe.matmul(
                            misc[:, 0:C],
                            w_t[:, n, :],
                            f.sparse_v[:, bass.ds(b * NT + n, 1), :].rearrange("p n c -> p (n c)"),
                            start=(n == 0),
                            stop=(n == NT - 1),
                        )
                    ins.then_inc(misc_made, 1)

                def body(b, first):
                    for group in range(GROUPS):
                        prev = before(b, group)
                        alone = first and group == 0
                        side = {0: lambda: sparse_scores(b, group, 0), 2: lambda: sparse_scores(b, group, 1)}
                        if not alone:
                            side |= {
                                4: lambda: turn_out(*prev, use(*prev, 2)),
                                7: lambda: turn_weights(*prev, 0, use(*prev, 3)),
                                9: lambda: sparse_values(*prev, 0),
                                14: lambda: turn_weights(*prev, 1, use(*prev, 5)),
                                17: lambda: sparse_values(*prev, 1),
                            }
                        for n in range(STEPS):
                            score(b, group, n)
                            if n % 4 in (1, 2):
                                if n >= 4:
                                    values(b, group, n // 4 - 1, n % 4 - 1)
                                elif not alone:
                                    values(*prev, NT - 1, n % 4 - 1)
                            if n in side:
                                side[n]()

                def end(b):
                    values(b, LAST, NT - 1, 0)
                    values(b, LAST, NT - 1, 1)
                    turn_out(b, LAST, last_use(2))
                    for t in range(2):
                        turn_weights(b, LAST, t, last_use(3 + 2 * t))
                        sparse_values(b, LAST, t)

                pe.wait_ge(const_ready, 6)
                pe.sem_inc(scored, 1)
                over_batches(pe, body, end)

            @block.vector
            def _(dve):

                def keep_pv(step, b, group):
                    dve.wait_ge(pv_done, (b * GROUPS + group + 1) * NT)
                    dve.tensor_copy(pv[:], pv_ps[:].rearrange("p c t -> p (c t)")).then_inc(pv_kept, 1)

                def keep_scores(step, b, group, t):
                    dve.wait_ge(misc_made, use(b, group, t))
                    dve.tensor_scalar(s[:, t, :], misc[:], 1.0, None, ALU.mult, ALU.max, accum_out=top[:, t : t + 1]).then_inc(scores_kept, 1)
                    dve.wait_ge(scores_kept, (b * GROUPS + group) * 2 + t + 1)
                    dve.sem_inc(misc_used, 1)

                def heads_out(step, b, group, number):
                    dve.wait_ge(misc_made, number)
                    turned = misc[:].rearrange("p (n j c) -> p n j c", n=NT, j=4)
                    step(dve.reciprocal(inv[:], turned[:, :, :, DH]))
                    step.settle()
                    for n in range(NT):
                        step(
                            dve.tensor_tensor(
                                f.v[:, bass.ds(b * NT + n, 1), group * 32 : group * 32 + 32].rearrange("p n (j d) -> p (n j) d", d=DH),
                                turned[:, n, :, 0:DH],
                                inv[:, n, :].unsqueeze(2).to_broadcast([P, 4, DH]),
                                ALU.mult,
                            )
                        )
                    step(dve.reduce_max(worst[:, 0:1], inv[:].rearrange("p n j -> p (n j)"), AX.X))
                    step.settle()
                    dve.sem_inc(misc_used, 1)
                    step(dve.scalar_tensor_tensor(out=f.doubt[:, 0:1], in0=worst[:, 0:1], scalar=float(np.exp(FLOOR)), in1=f.doubt[:, 0:1], op0=ALU.is_gt, op1=ALU.max))

                def keep_out(step, b, group, t, number):
                    dve.wait_ge(misc_made, number)
                    after(dve, so_stored[t], 16 * (b * GROUPS + group))
                    dve.tensor_scalar(so[:, t, :], misc[:, 0:C], w_sum[:, group % 2, t : t + 1], None, ALU.mult).then_inc(out_ready, 1)
                    dve.wait_ge(out_ready, b * NT + group * 2 + t + 1)
                    dve.sem_inc(misc_used, 2)

                def start_search(step, b, group):
                    dve.wait_ge(excess_ready, (b * GROUPS + group) * 2 + 2)
                    minus_mean = f.minus_mean[:, bass.ds(b * NT + 2 * group, 2)]
                    step(dve.scalar_tensor_tensor(out=at[:], in0=excess[:], scalar=Z_TOP / (T * MEAN_EXCESS), in1=minus_mean, op0=ALU.mult, op1=ALU.subtract))
                    step(dve.scalar_tensor_tensor(out=gain[:], in0=trust[:], scalar=1.0 / T, in1=bc(excess[:], len(TRUST)), op0=ALU.mult, op1=ALU.mult))
                    step.settle()

                def search(step, k):
                    for t in range(2):
                        step(dve.tensor_scalar(junk[:], s[:, t, :], at[:, t : t + 1], None, ALU.is_ge, ALU.add, accum_out=count[:, t : t + 1]))
                        step.settle()
                    if k == SEARCH - 1:
                        return
                    step(dve.tensor_scalar(off[:], count[:], -AIM, None, ALU.add))
                    step.settle()
                    step(dve.tensor_tensor(square[:], off[:], off[:], ALU.mult))
                    step(dve.tensor_tensor(off[:], off[:], gain[:, k, :], ALU.mult))
                    step.settle()
                    step(dve.scalar_tensor_tensor(out=off[:], in0=square[:], scalar=(AIM - IN_MIN + 0.5) ** 2, in1=off[:], op0=ALU.is_gt, op1=ALU.mult))
                    step.settle()
                    step(dve.tensor_tensor(at[:], at[:], off[:], ALU.add))
                    step.settle()

                def weigh(step, b, group):
                    half = group % 2
                    step(dve.tensor_scalar(rank[:, 2 * group : 2 * group + 2], count[:], -1.0, float(TOP), ALU.mult, ALU.add))
                    for t in range(2):
                        tile = slice(2 * group + t, 2 * group + t + 1)
                        dve.wait_ge(sparse_exp, (b * GROUPS + group) * 2 + t + 1)
                        step(dve.scalar_tensor_tensor(out=junk[:], in0=s[:, t, :], scalar=at[:, t : t + 1], in1=e[:, t, :], op0=ALU.is_lt, op1=ALU.mult))
                        step.settle()
                        step(dve.max(near[:, 2 * group + t, :], junk[:]))
                        step.settle()
                        step(
                            dve.scalar_tensor_tensor(
                                out=pick[:], in0=order[:], scalar=rank[:, tile], in1=near[:, 2 * group + t, :], op0=ALU.is_equal, op1=ALU.mult, accum_out=cut[:, tile]
                            )
                        )
                        step.settle()
                        step(
                            dve.scalar_tensor_tensor(
                                out=e[:, t, :], in0=e[:, t, :], scalar=cut[:, tile], in1=e[:, t, :], op0=ALU.is_ge, op1=ALU.mult, accum_out=w_sum[:, half, t : t + 1]
                            )
                        )
                    step.settle()
                    step(dve.scalar_tensor_tensor(out=w_sum[:, half, :], in0=z[:], scalar=1e-9, in1=w_sum[:, half, :], op0=ALU.mult, op1=ALU.add))
                    step.settle()
                    dve.reciprocal(w_sum[:, half, :], w_sum[:, half, :]).then_inc(w_ready, 1)
                    dve.wait_ge(w_ready, b * GROUPS + group + 1)

                def doubts(step):
                    step(dve.tensor_scalar(wrong[:], rank[:], float(TOP - IN_MAX), None, ALU.is_lt))
                    step(dve.tensor_scalar(tied[:], rank[:], 1.0, None, ALU.add))
                    step.settle()
                    step(dve.scalar_tensor_tensor(out=wrong[:], in0=rank[:], scalar=float(TOP - IN_MIN), in1=wrong[:], op0=ALU.is_gt, op1=ALU.max))
                    step(dve.tensor_tensor(nearer[:], bc(order[:], NT), tied[:].unsqueeze(2).to_broadcast([P, NT, 8]), ALU.is_equal))
                    step.settle()
                    step(dve.tensor_tensor(nearer[:], nearer[:], near[:], ALU.mult))
                    step.settle()
                    step(dve.reduce_max(tied[:], nearer[:], AX.X))
                    step.settle()
                    step(dve.tensor_tensor(tied[:], tied[:], cut[:], ALU.is_equal))
                    step.settle()
                    step(dve.scalar_tensor_tensor(out=tied[:], in0=cut[:], scalar=0.0, in1=tied[:], op0=ALU.is_gt, op1=ALU.mult))
                    step.settle()
                    step(dve.tensor_tensor(wrong[:], wrong[:], tied[:], ALU.max))
                    step.settle()
                    step(dve.reduce_max(worst[:, 1:2], wrong[:], AX.X))
                    step.settle()
                    step(dve.tensor_tensor(f.doubt[:, 1:2], f.doubt[:, 1:2], worst[:, 1:2], ALU.max))

                def body(b, first):
                    step = Steps(dve, vec)
                    for group in range(GROUPS):
                        prev = None if first and group == 0 else before(b, group)
                        if prev:
                            keep_pv(step, *prev)
                        keep_scores(step, b, group, 0)
                        keep_scores(step, b, group, 1)
                        dve.tensor_scalar(nmax[:], top[:], -1.0, None, ALU.mult).then_inc(max_ready, 1)
                        if prev:
                            heads_out(step, *prev, use(*prev, 2))
                        start_search(step, b, group)
                        for k in range(SEARCH):
                            search(step, k)
                            if prev and k in (2, 4):
                                t = k // 2 - 1
                                keep_out(step, *prev, t, use(*prev, 4 + 2 * t))
                        weigh(step, b, group)
                    doubts(step)
                    step.again()

                def end(b):
                    step = Steps(dve, vec)
                    keep_pv(step, b, LAST)
                    heads_out(step, b, LAST, last_use(2))
                    for t in range(2):
                        keep_out(step, b, LAST, t, last_use(4 + 2 * t))
                    step.again()

                dve.wait_ge(const_ready, 6)
                step = Steps(dve, vec)
                step(dve.memset(f.doubt[:], 0.0))
                step.again()
                over_batches(dve, body, end)


def heads_again(nc, g, f, scratch):
    with ExitStack() as ctx:
        a = Alloc(nc, ctx, "_again")
        flag, flag_ready = doubt_flag(nc, g, f, a, 0)
        q_pack = a.sb("q_pack", [P, T], BF16)
        k_pack = a.sb("k_pack", [P, T], BF16)
        v = a.sb("v", [P, NT, DH])
        probs = a.sb("probs", [P, T])
        probs_t = a.sb("probs_t", [P, T])
        nmax = a.sb("minus_max", [P, 1])
        total = a.sb("total", [P, 1])
        scores_ps = a.ps("scores_ps", [P, T])
        turn_ps = a.ps("turn_ps", [P, T])
        out_ps = a.ps("out_ps", [P, 512])
        vec = a.sem("vec")
        cleared = a.sem("cleared")
        loaded = a.sem("loaded")
        scored = a.sem("scored")
        max_ready = a.sem("max_ready")
        probs_ready = a.sem("probs_ready")
        probs_turned = a.sem("probs_turned")
        probs_t_ready = a.sem("probs_t_ready")
        out_made = a.sem("out_made")
        done = a.sem("done")
        sp_rounds = a.sem("sp_rounds")
        LOADS = 2 * PIECES * PIECES + 1

        with nc.Block() as block:

            @block.sync
            def _(sp):
                sp.wait_ge(flag_ready, 1)
                with sp.If(sp.value_load(flag[0:1, 0:1], min_val=0, max_val=P) != 0):
                    sp.wait_ge(cleared, 2)
                    with sp.Fori(0, B) as b:
                        with sp.Fori(0, HEADS) as head:
                            at = bass.ds(b, 1)
                            dims = bass.ds(head * DH, DH)
                            for i in range(PIECES):
                                for j in range(PIECES):
                                    rows = slice((i * PIECES + j) * DH, (i * PIECES + j + 1) * DH)
                                    sp.dma_start(q_pack[rows, :], scratch.q[at, i, dims].rearrange("b d t -> (b d) t")).then_inc(loaded, 16)
                                    sp.dma_start(k_pack[rows, :], scratch.k[at, j, dims].rearrange("b d t -> (b d) t")).then_inc(loaded, 16)
                            sp.dma_start(v[:], scratch.v[at, :, :, dims].rearrange("b n p d -> p (b n) d")).then_inc(loaded, 16)
                            sp.wait_ge(done, (b * HEADS + head + 1) * NT)
                            sp.sem_inc(sp_rounds, 1)

            @block.vector
            def _(dve):
                dve.wait_ge(flag_ready, 1)
                with dve.If(dve.value_load(flag[0:1, 0:1], min_val=0, max_val=P) != 0):
                    dve.memset(q_pack[64:128], 0.0).then_inc(cleared, 1)
                    dve.memset(k_pack[64:128], 0.0).then_inc(cleared, 1)
                    with dve.Fori(0, B) as b:
                        with dve.Fori(0, HEADS) as head:
                            with dve.Fori(0, NT) as n:
                                step = Steps(dve, vec)
                                at = (b * HEADS + head) * NT + n
                                dve.wait_ge(scored, at + 1)
                                step(dve.tensor_reduce(nmax[:], scores_ps[:], AX.X, ALU.max, negate=True))
                                step.settle()
                                dve.tensor_scalar(nmax[:], nmax[:], SCALE1, None, ALU.mult).then_inc(max_ready, 1)
                                dve.wait_ge(out_made, at + 1)
                                step(dve.reciprocal(total[:], total[:]))
                                step.settle()
                                dve.tensor_scalar(
                                    f.v[:, bass.ds(b * NT + n, 1), bass.ds(head * DH, DH)].rearrange("p n d -> p (n d)"), out_ps[:, 0:DH], total[:, 0:1], None, ALU.mult
                                ).then_inc(done, 1)
                                step.again()

            @block.scalar
            def _(act):
                act.wait_ge(flag_ready, 1)
                with act.If(act.value_load(flag[0:1, 0:1], min_val=0, max_val=P) != 0):
                    with act.Fori(0, B * HEADS * NT) as at:
                        act.wait_ge(max_ready, at + 1)
                        act.activation(probs[:], scores_ps[:], ACT.Exp, bias=nmax[:, 0:1], scale=SCALE1, accum_out=total[:, 0:1]).then_inc(probs_ready, 1)
                        act.wait_ge(probs_turned, at + 1)
                        act.activation(probs_t[:], turn_ps[:], ACT.Copy).then_inc(probs_t_ready, 1)
                        act.wait_ge(done, at + 1)

            @block.tensor
            def _(pe):
                pe.wait_ge(flag_ready, 1)
                with pe.If(pe.value_load(flag[0:1, 0:1], min_val=0, max_val=P) != 0):
                    with pe.Fori(0, B * HEADS) as head:
                        with pe.Fori(0, NT) as n:
                            pe.wait_ge(loaded, head * (16 * LOADS) + 16 * LOADS)
                            at = head * NT + n
                            for c in range(2):
                                cols = slice(c * 512, c * 512 + 512)
                                ins = pe.matmul(scores_ps[:, cols], q_pack[:, bass.ds(n * P, P)], k_pack[:, cols], start=True, stop=True)
                            ins.then_inc(scored, 1)
                            pe.wait_ge(probs_ready, at + 1)
                            for m in range(NT):
                                ins = pe.transpose(turn_ps[:, m * P : m * P + P], probs[:, m * P : m * P + P], g.ident[:])
                            ins.then_inc(probs_turned, 1)
                            pe.wait_ge(probs_t_ready, at + 1)
                            for m in range(NT):
                                ins = pe.matmul(out_ps[:, 0:DH], probs_t[:, m * P : m * P + P], v[:, m, :], start=(m == 0), stop=(m == NT - 1))
                            ins.then_inc(out_made, 1)
                            pe.wait_ge(done, at + 1)


def sparse_again(nc, g, f, scratch):
    with ExitStack() as ctx:
        a = Alloc(nc, ctx, "_sparse_again")
        flag, flag_ready = doubt_flag(nc, g, f, a, 1)
        sq = a.sb("sq", [P, P])
        e = a.sb("e", [P, T])
        left = a.sb("left", [P, T])
        w_t = a.sb("w_t", [P, T])
        so = a.sb("so", [P, C])
        best = a.sb("best", [P, 8])
        nmax = a.sb("minus_max", [P, 1])
        z = a.sb("z", [P, 1])
        w_sum = a.sb("w_sum", [P, 1])
        scores_ps = a.ps("scores_ps", [P, T])
        turn_ps = a.ps("turn_ps", [P, T])
        out_ps = a.ps("out_ps", [P, 512])
        vec = a.sem("vec")
        cleared = a.sem("cleared")
        loaded = a.sem("loaded")
        scored = a.sem("scored")
        max_ready = a.sem("max_ready")
        exp_ready = a.sem("exp_ready")
        w_ready = a.sem("w_ready")
        w_turned = a.sem("w_turned")
        w_t_ready = a.sem("w_t_ready")
        out_made = a.sem("out_made")
        out_ready = a.sem("out_ready")
        stored = a.sem("stored")
        sp_rounds = a.sem("sp_rounds")
        ROUNDS, LAST = TOP // 8, TOP % 8

        with nc.Block() as block:

            @block.sync
            def _(sp):
                sp.wait_ge(flag_ready, 1)
                with sp.If(sp.value_load(flag[0:1, 0:1], min_val=0, max_val=P) != 0):
                    sp.wait_ge(cleared, 1)
                    with sp.Fori(0, B) as b:
                        with sp.Fori(0, NT) as n:
                            sp.dma_start(sq[0:RQ, :], scratch.sparse_q[bass.ds(b, 1), :, bass.ds(n * P, P)].rearrange("b r t -> (b r) t")).then_inc(loaded, 16)
                            sp.wait_ge(out_ready, b * NT + n + 1)
                            sp.dma_start(scratch.sparse_out[bass.ds(b, 1), bass.ds(n, 1)].rearrange("b n p c -> (b n p) c"), so[:]).then_inc(stored, 16)
                            sp.wait_ge(stored, (b * NT + n) * 16 + 16)
                            sp.sem_inc(sp_rounds, 1)

            @block.vector
            def _(dve):
                dve.wait_ge(flag_ready, 1)
                with dve.If(dve.value_load(flag[0:1, 0:1], min_val=0, max_val=P) != 0):
                    dve.memset(sq[RQ:P], 0.0).then_inc(cleared, 1)
                    with dve.Fori(0, TILES) as at:
                        step = Steps(dve, vec)
                        dve.wait_ge(scored, at + 1)
                        dve.tensor_reduce(nmax[:], scores_ps[:], AX.X, ALU.max, negate=True).then_inc(max_ready, 1)
                        dve.wait_ge(exp_ready, at + 1)
                        step(dve.tensor_copy(left[:], e[:]))
                        step.again()
                        with dve.Fori(0, ROUNDS) as _:
                            step = Steps(dve, vec)
                            step(dve.max(best[:], left[:]))
                            step.settle()
                            step(dve.match_replace(left[:], best[:], left[:], -1.0))
                            step.again()
                        step = Steps(dve, vec)
                        if LAST:
                            step(dve.max(best[:], left[:]))
                            step.settle()
                            step(dve.memset(best[:, LAST:8], 2.0))
                            step.settle()
                            step(dve.match_replace(left[:], best[:], left[:], -1.0))
                            step.settle()
                        step(dve.scalar_tensor_tensor(out=left[:], in0=left[:], scalar=0.0, in1=e[:], op0=ALU.is_lt, op1=ALU.mult, accum_out=w_sum[:]))
                        step.settle()
                        step(dve.scalar_tensor_tensor(out=w_sum[:], in0=z[:], scalar=1e-9, in1=w_sum[:], op0=ALU.mult, op1=ALU.add))
                        step.settle()
                        dve.reciprocal(w_sum[:], w_sum[:]).then_inc(w_ready, 1)
                        dve.wait_ge(out_made, at + 1)
                        dve.wait_ge(w_ready, at + 1)
                        dve.tensor_scalar(so[:], out_ps[:, 0:C], w_sum[:, 0:1], None, ALU.mult).then_inc(out_ready, 1)
                        step.again()

            @block.scalar
            def _(act):
                act.wait_ge(flag_ready, 1)
                with act.If(act.value_load(flag[0:1, 0:1], min_val=0, max_val=P) != 0):
                    with act.Fori(0, TILES) as at:
                        act.wait_ge(max_ready, at + 1)
                        act.activation(e[:], scores_ps[:], ACT.Exp, bias=nmax[:, 0:1], accum_out=z[:, 0:1]).then_inc(exp_ready, 1)
                        act.wait_ge(w_turned, at + 1)
                        act.activation(w_t[:], turn_ps[:], ACT.Copy).then_inc(w_t_ready, 1)

            @block.tensor
            def _(pe):
                pe.wait_ge(flag_ready, 1)
                with pe.If(pe.value_load(flag[0:1, 0:1], min_val=0, max_val=P) != 0):
                    with pe.Fori(0, B) as b:
                        with pe.Fori(0, NT) as n:
                            at = b * NT + n
                            pe.wait_ge(loaded, at * 16 + 16)
                            for c in range(2):
                                ins = pe.matmul(scores_ps[:, c * 512 : c * 512 + 512], sq[:], f.sparse_k[:, bass.ds(b * T + c * 512, 512)], start=True, stop=True)
                            ins.then_inc(scored, 1)
                            pe.wait_ge(w_ready, at + 1)
                            for m in range(NT):
                                ins = pe.transpose(turn_ps[:, m * P : m * P + P], left[:, m * P : m * P + P], g.ident[:])
                            ins.then_inc(w_turned, 1)
                            pe.wait_ge(w_t_ready, at + 1)
                            for m in range(NT):
                                ins = pe.matmul(
                                    out_ps[:, 0:C],
                                    w_t[:, m * P : m * P + P],
                                    f.sparse_v[:, bass.ds(b * NT + m, 1), :].rearrange("p n c -> p (n c)"),
                                    start=(m == 0),
                                    stop=(m == NT - 1),
                                )
                            ins.then_inc(out_made, 1)


def doubt_flag(nc, g, f, a, kind):
    flag = a.sb("flag", [P, 1], I32)
    doubt = a.sb("doubt_bf16", [P, 1], BF16)
    flag_ps = a.ps("flag_ps", [P, 1])
    doubt_ready = a.sem("doubt_ready")
    counted = a.sem("doubt_counted")
    flag_ready = a.sem("flag_ready")
    with nc.Block() as block:

        @block.vector
        def _(dve):
            dve.tensor_copy(doubt[:], f.doubt[:, kind : kind + 1]).then_inc(doubt_ready, 1)
            dve.wait_ge(counted, 1)
            dve.tensor_copy(flag[:], flag_ps[:]).then_inc(flag_ready, 1)

        @block.tensor
        def _(pe):
            pe.wait_ge(doubt_ready, 1)
            pe.matmul(flag_ps[:], g.ones_b[:], doubt[:], start=True, stop=True).then_inc(counted, 1)

    return flag, flag_ready


def finish_attention(nc, g, f, scratch):
    with ExitStack() as ctx:
        a = Alloc(nc, ctx)
        norm = Norm(a, "ln_post", g.minus_half)
        h = a.sb("h1_again", [P, NT, C])
        sparse = a.sb("sparse_in", [P, NT, C])
        ctx_rows = a.sb("ctx1_rows", [P, NT, C])
        ctx_t = a.sb("ctx1_t", [P, T])
        y = a.sb("y1", [P, NT, C])
        y_t = a.sb("y1_t", [P, T])
        ff = a.sb("ff1", [P, FC, T])
        lam_e = a.sb("lam_exp", [P, 1])
        sig = a.sb("sigmoid_lam", [P, 1])
        cosig = a.sb("one_minus_sigmoid", [P, 1])
        turn_ps = a.ps("post_turn_ps", [P, T])
        out_ps = a.ps("post_out_ps", [P, T])
        ff_ps = [a.ps(f"post_ff_ps{i}", [P, 512]) for i in range(4)]
        vec = a.sem("post_vec")
        lam_ready = a.sem("lam_exp_ready")
        sparse_loaded = a.sem("sparse_loaded")
        rows_ready = a.sem("ctx1_rows_ready")
        ctx_turned = a.sem("ctx1_turned")
        ctx_t_ready = a.sem("ctx1_t_ready")
        dense_made = a.sem("dense_made")
        y_ready = a.sem("y1_ready")
        y_turned = a.sem("y1_turned")
        y_t_ready = a.sem("y1_t_ready")
        ff_made = a.sem("ff1_made")
        ff_act = a.sem("ff1_kept_act")
        down_made = a.sem("ff2_made")
        done = a.sem("post_done")
        sp_rounds = a.sem("post_sp_rounds")

        with nc.Block() as block:

            @block.sync
            def _(sp):
                with sp.Fori(0, B) as b:
                    sp.dma_start(sparse[:], scratch.sparse_out[bass.ds(b, 1)].rearrange("b n p c -> p (b n) c")).then_inc(sparse_loaded, 16)
                    sp.wait_ge(done, b + 1)
                    sp.sem_inc(sp_rounds, 1)

            @block.gpsimd
            def _(pool):
                with pool.Fori(0, B) as b:
                    pool.tensor_copy(ctx_rows[:], f.v[:, bass.ds(b * NT, NT), :]).then_inc(rows_ready, 1)
                    for n in range(3):
                        norm.pool(pool, 3 * b + n + 1)

            @block.vector
            def _(dve):
                step = Steps(dve, vec)
                dve.wait_ge(lam_ready, 1)
                step(dve.tensor_scalar(lam_e[:], lam_e[:], 1.0, None, ALU.add))
                step.settle()
                step(dve.reciprocal(sig[:], lam_e[:]))
                step.settle()
                step(dve.tensor_scalar(cosig[:], sig[:], -1.0, 1.0, ALU.mult, ALU.add))
                step.again()
                flat = lambda t: t[:].rearrange("p n c -> p (n c)")
                with dve.Fori(0, B) as b:
                    step = Steps(dve, vec)
                    rows = g.x[:, bass.ds(b * NT, NT), :]
                    layer_norm(dve, step, norm, rows, h[:], g.mod_row(1, b, CA), lambda: dve.wait_ge(norm.rstd_ready, 3 * b + 1))
                    step(dve.tensor_tensor(h[:], h[:], g.mod_row(1, b, SA), ALU.add))
                    dve.wait_ge(sparse_loaded, 16 * (b + 1))
                    step.settle()
                    step(dve.scalar_tensor_tensor(out=flat(h), in0=flat(sparse), scalar=cosig[:, 0:1], in1=flat(h), op0=ALU.mult, op1=ALU.add))
                    dve.wait_ge(dense_made, b + 1)
                    step(dve.tensor_tensor(y[:], out_ps[:].rearrange("p (n c) -> p n c", c=C), bc(g.row("L1_attn_out_proj_b"), NT), ALU.add))
                    step.settle()
                    step(dve.scalar_tensor_tensor(out=flat(h), in0=flat(y), scalar=sig[:, 0:1], in1=flat(h), op0=ALU.mult, op1=ALU.add))
                    step.settle()
                    layer_norm(dve, step, norm, h, y[:], bc(g.row("L1_attn_ln1_g"), NT), lambda: dve.wait_ge(norm.rstd_ready, 3 * b + 2))
                    dve.tensor_tensor(y[:], y[:], bc(g.row("L1_attn_ln1_b"), NT), ALU.add).then_inc(y_ready, 1)
                    dve.wait_ge(y_ready, b + 1)
                    dve.wait_ge(down_made, b + 1)
                    step(dve.tensor_tensor(h[:], out_ps[:].rearrange("p (n c) -> p n c", c=C), bc(g.row("L1_attn_ff2_b"), NT), ALU.add))
                    step.settle()
                    step(dve.tensor_tensor(h[:], h[:], y[:], ALU.add))
                    step.settle()
                    layer_norm(dve, step, norm, h, y[:], bc(g.row("L1_attn_ln2_g"), NT), lambda: dve.wait_ge(norm.rstd_ready, 3 * b + 3))
                    step(dve.tensor_tensor(y[:], y[:], bc(g.row("L1_attn_ln2_b"), NT), ALU.add))
                    step.settle()
                    step(dve.tensor_tensor(y[:], y[:], g.mod_row(1, b, GA), ALU.mult))
                    step.settle()
                    step(dve.tensor_tensor(rows, rows, y[:], ALU.add))
                    step.settle()
                    dve.sem_inc(done, 1)
                    step.again()

            @block.scalar
            def _(act):
                act.activation(lam_e[:], g.lam[:], ACT.Exp, scale=-1.0).then_inc(lam_ready, 1)
                with act.Fori(0, B) as b:
                    for n in range(2):
                        act.wait_ge(ctx_turned, 2 * b + n + 1)
                        act.activation(ctx_t[:, n * 512 : n * 512 + 512], turn_ps[:, n * 512 : n * 512 + 512], ACT.Copy).then_inc(ctx_t_ready, 1)
                    for n in range(2):
                        act.wait_ge(y_turned, 2 * b + n + 1)
                        act.activation(y_t[:, n * 512 : n * 512 + 512], turn_ps[:, n * 512 : n * 512 + 512], ACT.Copy).then_inc(y_t_ready, 1)
                    for n in range(2):
                        for k in range(FC):
                            act.wait_ge(ff_made, b * 2 * FC + n * FC + k + 1)
                            act.activation(ff[:, k, n * 512 : n * 512 + 512], ff_ps[k][:], ACT.Relu, bias=g.bias(B_FF1 + k)).then_inc(ff_act, 1)

            @block.tensor
            def _(pe):
                with pe.Fori(0, B) as b:

                    def turn(of, made):
                        for n in range(NT):
                            ins = pe.transpose(turn_ps[:, n * P : n * P + P], of[:, n, :], g.ident[:])
                            if n % 4 == 3:
                                ins.then_inc(made, 1)

                    pe.wait_ge(rows_ready, b + 1)
                    turn(ctx_rows, ctx_turned)
                    pe.wait_ge(ctx_t_ready, 2 * b + 2)
                    for n in range(NT):
                        ins = pe.matmul(out_ps[:, n * C : n * C + C], ctx_t[:, n * P : n * P + P], g.weights(W_OUT1), start=True, stop=True)
                    ins.then_inc(dense_made, 1)
                    pe.wait_ge(y_ready, b + 1)
                    turn(y, y_turned)
                    for n in range(2):
                        pe.wait_ge(y_t_ready, 2 * b + n + 1)
                        for k in range(FC):
                            if n == 1:
                                pe.wait_ge(ff_act, b * 2 * FC + k + 1)
                            pe.matmul(ff_ps[k][:], g.weights(W_FF1 + k), y_t[:, n * 512 : n * 512 + 512], start=True, stop=True).then_inc(ff_made, 1)
                    for n in range(2):
                        pe.wait_ge(ff_act, b * 2 * FC + (n + 1) * FC)
                        for m in range(4 * n, 4 * n + 4):
                            for k in range(FC):
                                ins = pe.matmul(out_ps[:, m * C : m * C + C], ff[:, k, m * P : m * P + P], g.weights(W_FF2 + k), start=(k == 0), stop=(k == FC - 1))
                    ins.then_inc(down_made, 1)


def fused_attention(nc, g, dram):
    with ExitStack() as ctx:
        f = Fused(Alloc(nc, ctx))
        scratch = Scratch(nc)
        prepare(nc, g, f, scratch, dram)
        attend(nc, g, f, scratch)
        heads_again(nc, g, f, scratch)
        sparse_again(nc, g, f, scratch)
        finish_attention(nc, g, f, scratch)


def adaln_program(nc, dram, out):
    with ExitStack() as whole:
        g = Shared(Alloc(nc, whole))
        rows = [ExpertRows(nc, layer) for layer in range(2)]
        with ExitStack() as layer0:
            a = Alloc(nc, layer0)
            g.wt0 = a.sb("weights0_t", [P, W_SLOTS_L0, P])
            g.mods[0] = a.sb("mod0", [P, B, 6 * C])
            setup(nc, g, dram)
            causal_attention(nc, g, rows)
            moe = Moe(a, rows[0], 0)
            route(nc, g, moe, dram, 0)
            experts0(nc, g, moe)
        with ExitStack() as attn1:
            fused_attention(nc, g, dram)
        with ExitStack() as ffn1:
            moe = Moe(Alloc(nc, ffn1), rows[1], 1)
            route(nc, g, moe, dram, 1)
            experts1(nc, g, moe)
        store(nc, g, out)


_INS = [
    "L0_attn_x",
    "L0_attn_qkv_w",
    "L0_attn_out_w",
    "L0_attn_out_b",
    "L0_ffn_router_w",
    "L0_ffn_expert_w1",
    "L0_ffn_expert_b1",
    "L0_ffn_expert_w2",
    "L0_ffn_expert_b2",
    "L0_c",
    "L0_wmod",
    "L1_attn_in_proj_w",
    "L1_attn_in_proj_b",
    "L1_attn_out_proj_w",
    "L1_attn_out_proj_b",
    "L1_attn_Qp_w",
    "L1_attn_Qp_b",
    "L1_attn_Kp_w",
    "L1_attn_Kp_b",
    "L1_attn_Vp_w",
    "L1_attn_Vp_b",
    "L1_attn_lam",
    "L1_attn_ff1_w",
    "L1_attn_ff1_b",
    "L1_attn_ff2_w",
    "L1_attn_ff2_b",
    "L1_attn_ln1_g",
    "L1_attn_ln1_b",
    "L1_attn_ln2_g",
    "L1_attn_ln2_b",
    "L1_ffn_Wr",
    "L1_ffn_W1",
    "L1_ffn_b1",
    "L1_ffn_W2",
    "L1_ffn_b2",
    "L1_c",
    "L1_wmod",
]
_OUT = (B, T, C)


def kernel(**inputs):
    import numpy as _np
    import concourse.bacc as _bacc
    from concourse import mybir as _mybir
    from concourse.bass_utils import run_bass_kernel_spmd as _run

    nc = _bacc.Bacc("TRN2", target_bir_lowering=False, num_devices=1)
    arrays, dram = {}, {}
    for name in _INS:
        a = _np.ascontiguousarray(inputs[name])
        if a.ndim == 0:
            a = a.reshape(1)
        arrays[f"in_{name}_dram"] = a
        dram[name] = nc.dram_tensor(f"in_{name}_dram", a.shape, _mybir.dt.from_np(a.dtype), kind="ExternalInput").ap()
    out = nc.dram_tensor("out_dram", _OUT, F32, kind="ExternalOutput").ap()
    adaln_program(nc, dram, out)
    r = _run(nc, [arrays], core_ids=[0])
    return r.results[0]["out_dram"]
```

```python
from contextlib import ExitStack

import numpy as np

import concourse.bass as bass
from concourse import mybir

ALU = mybir.AluOpType
ACT = mybir.ActivationFunctionType
AX = mybir.AxisListType
F32 = mybir.dt.float32
BF16 = mybir.dt.bfloat16
I32 = mybir.dt.int32

P = 128
B, T, C = 4, 1024, 128
NT = T // P
TILES = B * NT
E, FF = 8, 512
RQ = 64
FC = FF // P
LN_EPS = 1e-5

W_QKV0, W_OUT0 = 0, 3
W_UP0 = 4
W_DOWN0 = W_UP0 + E * FC
W_QKV1 = W_DOWN0 + E * FC
W_OUT1 = W_QKV1 + 3
W_QK1 = W_OUT1 + 1
W_ROUTER0 = W_QK1 + 1
W_V1 = W_ROUTER0 + 1
W_FF1 = W_V1 + 1
W_FF2 = W_FF1 + FC
W_BIAS = W_FF2 + FC
W_SLOTS = W_BIAS + 1
W_SLOTS_L0 = W_QKV1

B_UP1 = 0
B_FF1 = B_UP1 + E * FC
B_Q1 = B_FF1 + FC
B_K1, B_SQ1, B_SK1, B_DOWN1 = B_Q1 + 1, B_Q1 + 2, B_Q1 + 3, B_Q1 + 4
B_UP0 = B_DOWN1 + E
CAPACITY = int(T / E * 1.25)

SA, CA, GA, SB, CB, GB = range(6)


class Alloc:

    def __init__(self, nc, ctx, tag=""):
        self.nc, self.ctx, self.tag = nc, ctx, tag
        self.sems = []

    def sb(self, name, shape, dt=F32):
        return self.ctx.enter_context(self.nc.sbuf_tensor(name + self.tag, shape, dt))

    def ps(self, name, shape, dt=F32):
        return self.ctx.enter_context(self.nc.psum_tensor(name + self.tag, shape, dt))

    def sem(self, name):
        self.sems.append(self.ctx.enter_context(self.nc.semaphore(name + self.tag)))
        return self.sems[-1]

    def clear_sems(self):
        nums = sorted(s.num for s in self.sems)
        firsts = [n for n in nums if n - 1 not in nums]
        lasts = [n for n in nums if n + 1 not in nums]
        with self.nc.Block() as block:

            @block.gpsimd
            def _(pool):
                for first, last in zip(firsts, lasts):
                    pool.sem_clear(range(first, last + 1))


class Steps:

    def __init__(self, eng, sem):
        self.eng, self.sem, self.n = eng, sem, 0

    def __call__(self, ins):
        self.n += 1
        return ins.then_inc(self.sem, 1)

    def settle(self):
        self.eng.wait_ge(self.sem, self.n)

    def again(self):
        self.settle()
        self.eng.sem_clear(self.sem)


def bc(ap, n):
    return ap.unsqueeze(1).to_broadcast([ap.shape[0], n, ap.shape[1]])


def setup(nc, g, dram):
    with ExitStack() as ctx:
        a = Alloc(nc, ctx)
        nat = a.sb("weights_natural", [P, W_SLOTS, P])
        wmod = a.sb("wmod", [P, 2, 6 * C])
        cond = a.sb("cond", [2 * B, C])
        cond_t = a.sb("cond_t", [P, 2 * B])
        cond_e = a.sb("cond_e", [P, 2 * B])
        silu = a.sb("silu", [P, 2 * B])
        silu_b = a.sb("silu_b", [P, 2 * B, P])
        gate_sign = a.sb("gate_sign", [P, 4, B, C])
        weight_ps = [a.ps(f"weight_ps{i}", [P, 4, P]) for i in range(4)]
        mod_ps = [a.ps(f"mod_ps{i}", [P, 512]) for i in range(4)]
        cond_loaded = a.sem("cond_loaded")
        w0_loaded = a.sem("w0_loaded")
        w1_loaded = a.sem("w1_loaded")
        x_loaded = a.sem("x_loaded")
        rows_loaded = a.sem("rows_loaded")
        zeroed = a.sem("zeroed")
        ident_ready = a.sem("ident_ready")
        turned = a.sem("turned")
        kept_act = a.sem("kept_act")
        kept_dve = a.sem("kept_dve")
        cond_turned = a.sem("cond_turned")
        cond_kept = a.sem("cond_kept")
        cond_exp = a.sem("cond_exp")
        silu_ready = a.sem("silu_ready")
        mod_ready = a.sem("mod_ready")
        mod_kept = a.sem("mod_kept")
        vec = a.sem("setup_vec")
        GROUPS = -(-W_SLOTS // 4)
        W0_GROUPS = W_SLOTS_L0 // 4
        MODS = 2 * B * 2
        HALF = 3 * C

        def group(i):
            return 4 * i, min(4, W_SLOTS - 4 * i)

        with nc.Block() as block:

            @block.sync
            def _(sp):
                for half in range(2):
                    sp.dma_start(cond[half * B : half * B + B, :], dram[f"L{half}_c"]).then_inc(cond_loaded, 16)
                sp.dma_start(nat[:, W_QKV0 : W_QKV0 + 3, :], dram["L0_attn_qkv_w"].rearrange("(n p) c -> p n c", p=P)).then_inc(w0_loaded, 16)
                sp.dma_start(nat[:, W_OUT0, :], dram["L0_attn_out_w"]).then_inc(w0_loaded, 16)
                sp.dma_start(
                    nat[:, W_UP0 : W_UP0 + E * FC, :], dram["L0_ffn_expert_w1"].rearrange("e (k p) c -> p (e k) c", p=P)
                ).then_inc(w0_loaded, 16)
                sp.dma_start(
                    nat[:, W_DOWN0 : W_DOWN0 + E * FC, :].rearrange("p (e k) f -> p e (k f)", e=E),
                    dram["L0_ffn_expert_w2"].rearrange("e c f -> c e f"),
                ).then_inc(w0_loaded, 16)
                for half in range(2):
                    sp.dma_start(wmod[:, half, :], dram[f"L{half}_wmod"]).then_inc(cond_loaded, 16)
                sp.dma_start(g.x[:], dram["L0_attn_x"].rearrange("b (n p) c -> p (b n) c", p=P)).then_inc(x_loaded, 16)
                sp.wait_ge(x_loaded, 16)

            @block.gpsimd
            def _(pool):
                pool.memset(nat[:, W_ROUTER0, :], 0.0).then_inc(zeroed, 1)
                pool.memset(nat[:, W_BIAS, :], 0.0).then_inc(zeroed, 1)
                pool.memset(g.ident[:], 0.0).then_inc(zeroed, 1)
                pool.memset(g.causal[:], 0.0).then_inc(zeroed, 1)
                pool.memset(g.minus_half[:], -0.5)
                pool.memset(g.zeros[:], 0.0)
                for e in range(E):
                    pool.memset(g.expert_rank[:, e : e + 1], float(E - e))
                pool.memset(g.ones_b[:], 1.0).then_inc(zeroed, 1)
                pool.wait_ge(zeroed, 5)
                pool.affine_select(
                    out=g.ident[:], in_=g.ident[:], compare_op=ALU.not_equal, fill=1.0, base=0, pattern=[[-1, P]], channel_multiplier=1
                ).then_inc(ident_ready, 1)
                pool.affine_select(
                    out=g.causal[:], in_=g.causal[:], compare_op=ALU.is_ge, fill=-1e30, base=0, pattern=[[-1, P]], channel_multiplier=1
                )
                pool.affine_select(
                    out=g.before[:], in_=g.ones_b[:], compare_op=ALU.is_gt, fill=0.0, base=0, pattern=[[1, P]], channel_multiplier=-1
                )

            @block.scalar
            def _(act):
                act.wait_ge(zeroed, 2)
                act.dma_start(nat[0:E, W_ROUTER0, :], dram["L0_ffn_router_w"]).then_inc(w1_loaded, 16)
                act.dma_start(nat[:, W_QKV1 : W_QKV1 + 3, :], dram["L1_attn_in_proj_w"].rearrange("(n p) c -> p n c", p=P)).then_inc(w1_loaded, 16)
                act.dma_start(nat[:, W_OUT1, :], dram["L1_attn_out_proj_w"]).then_inc(w1_loaded, 16)
                act.dma_start(nat[0:RQ, W_QK1, :], dram["L1_attn_Qp_w"]).then_inc(w1_loaded, 16)
                act.dma_start(nat[RQ : 2 * RQ, W_QK1, :], dram["L1_attn_Kp_w"]).then_inc(w1_loaded, 16)
                act.dma_start(nat[:, W_V1, :], dram["L1_attn_Vp_w"]).then_inc(w1_loaded, 16)
                act.dma_start(nat[:, W_FF1 : W_FF1 + FC, :], dram["L1_attn_ff1_w"].rearrange("(k p) c -> p k c", p=P)).then_inc(w1_loaded, 16)
                act.dma_start(nat[:, W_FF2 : W_FF2 + FC, :].rearrange("p k f -> p (k f)"), dram["L1_attn_ff2_w"]).then_inc(w1_loaded, 16)
                bias = nat[:, W_BIAS, :]
                act.dma_start(bias[B_DOWN1 : B_DOWN1 + E, :], dram["L1_ffn_b2"]).then_inc(w1_loaded, 16)
                act.dma_start(bias[B_UP1 : B_UP1 + E * FC, :], dram["L1_ffn_b1"].rearrange("e (k p) -> (e k) p", p=P)).then_inc(w1_loaded, 16)
                act.dma_start(bias[B_UP0 : B_UP0 + E * FC, :], dram["L0_ffn_expert_b1"].rearrange("e (k p) -> (e k) p", p=P)).then_inc(w1_loaded, 16)
                act.dma_start(bias[B_FF1 : B_FF1 + FC, :], dram["L1_attn_ff1_b"].rearrange("(k p) -> k p", p=P)).then_inc(w1_loaded, 16)
                act.dma_start(bias[B_Q1 : B_Q1 + 2, :], dram["L1_attn_in_proj_b"][0 : 2 * C].rearrange("(k p) -> k p", p=P)).then_inc(w1_loaded, 16)
                act.dma_start(bias[B_SQ1 : B_SQ1 + 1, 0:RQ], dram["L1_attn_Qp_b"].rearrange("(a r) -> a r", a=1)).then_inc(w1_loaded, 16)
                act.dma_start(bias[B_SK1 : B_SK1 + 1, 0:RQ], dram["L1_attn_Kp_b"].rearrange("(a r) -> a r", a=1)).then_inc(w1_loaded, 16)
                for dst, src in g.small_loads(dram):
                    act.dma_start(dst, src).then_inc(rows_loaded, 16)
                act.wait_ge(cond_kept, 1)
                act.activation(cond_e[:], cond_t[:], ACT.Exp, scale=-1.0).then_inc(cond_exp, 1)
                for i in range(0, GROUPS, 2):
                    first, n = group(i)
                    act.wait_ge(turned, i + 1)
                    act.activation(g.weights(first, n), weight_ps[i % 4][:, 0:n, :], ACT.Copy).then_inc(kept_act, 1)
                for i in range(MODS):
                    col, part = i // 2, i % 2
                    act.wait_ge(mod_ready, i + 1)
                    act.activation(g.mods[col // B][:, col % B, part * HALF : part * HALF + HALF], mod_ps[i % 4][:, 0:HALF], ACT.Copy).then_inc(mod_kept, 1)
                act.wait_ge(rows_loaded, 16 * len(g.small_loads(dram)))

            @block.vector
            def _(dve):
                step = Steps(dve, vec)
                dve.wait_ge(cond_turned, 1)
                step(dve.tensor_copy(cond_t[:], mod_ps[0][:, 0 : 2 * B]))
                step.settle()
                dve.tensor_copy(cond_t[:], cond_t[:]).then_inc(cond_kept, 1)
                dve.wait_ge(cond_exp, 1)
                step(dve.tensor_scalar(cond_e[:], cond_e[:], 1.0, None, ALU.add))
                step.settle()
                step(dve.reciprocal(cond_e[:], cond_e[:]))
                step.settle()
                step(dve.tensor_tensor(silu[:], cond_t[:], cond_e[:], ALU.mult))
                step.settle()
                dve.tensor_copy(silu_b[:], silu[:].unsqueeze(2).to_broadcast([P, 2 * B, P])).then_inc(silu_ready, 1)
                for i in range(1, GROUPS, 2):
                    first, n = group(i)
                    dve.wait_ge(turned, i + 1)
                    dve.tensor_copy(g.weights(first, n), weight_ps[i % 4][:, 0:n, :]).then_inc(kept_dve, 1)
                for layer, mod in enumerate(g.mods):
                    dve.wait_ge(mod_kept, (layer + 1) * (MODS // 2))
                    parts = [(mod[:, :, part * C : part * C + C], gate_sign[:, 2 * layer + i]) for i, part in enumerate((GA, GB))]
                    for v, sign in parts:
                        step(dve.tensor_scalar(sign, v, 0.0, 2.0, ALU.is_ge, ALU.mult))
                    step.settle()
                    for v, sign in parts:
                        step(dve.tensor_scalar(sign, sign, -1.0, None, ALU.add))
                    step.settle()
                    for v, sign in parts:
                        step(dve.tensor_tensor(v, v, sign, ALU.mult))
                    for part in (CA, CB):
                        v = mod[:, :, part * C : part * C + C]
                        step(dve.tensor_scalar(v, v, 1.0, None, ALU.add))
                    step.settle()
                    for v, sign in parts:
                        step(dve.scalar_tensor_tensor(out=v, in0=v, scalar=0.25, in1=sign, op0=ALU.max, op1=ALU.mult))

            @block.tensor
            def _(pe):
                pe.wait_ge(ident_ready, 1)
                pe.wait_ge(cond_loaded, 64)
                pe.transpose(mod_ps[0][:, 0 : 2 * B], cond[:], g.ident[0 : 2 * B, 0 : 2 * B]).then_inc(cond_turned, 1)
                for i in range(GROUPS):
                    if i == 0:
                        pe.wait_ge(w0_loaded, 64)
                    if i == W0_GROUPS:
                        pe.wait_ge(w1_loaded, 240)
                    if i >= 4:
                        pe.wait_ge(kept_dve if i % 2 else kept_act, (i - 4) // 2 + 1)
                    first, n = group(i)
                    for k in range(n):
                        ins = pe.transpose(weight_ps[i % 4][:, k, :], nat[:, first + k, :], g.ident[:])
                    ins.then_inc(turned, 1)
                pe.wait_ge(silu_ready, 1)
                for i in range(MODS):
                    col, part = i // 2, i % 2
                    if i >= 4:
                        pe.wait_ge(mod_kept, i - 3)
                    pe.matmul(
                        mod_ps[i % 4][:, 0:HALF], silu_b[:, col, :], wmod[:, col // B, part * HALF : part * HALF + HALF], start=True, stop=True
                    ).then_inc(mod_ready, 1)
        a.clear_sems()


def layer_norm(dve, step, st, rows, out, scale, rstd_wait):
    for n in range(NT):
        step(dve.bn_stats(st.stats[:, n, :], rows[:, n, :]))
    step.settle()
    for n in range(NT):
        step(dve.bn_aggr(st.mean_var[:, n, :], st.stats[:, n, :]))
    step.settle()
    dve.tensor_scalar(st.var_eps[:], st.mean_var[:, :, 1], LN_EPS, None, ALU.add).then_inc(st.var_ready, 1)
    rstd_wait()
    for n in range(NT):
        step(
            dve.tensor_scalar(
                out[:, n, :], rows[:, n, :], st.mean_var[:, n, 0:1], st.rstd[:, n : n + 1], ALU.subtract, ALU.mult
            )
        )
    step.settle()
    step(dve.tensor_tensor(out, out, scale, ALU.mult))
    step.settle()


class Norm:

    def __init__(self, a, name, minus_half):
        self.stats = a.sb(f"{name}_stats", [P, NT, 6])
        self.mean_var = a.sb(f"{name}_mean_var", [P, NT, 2])
        self.var_eps = a.sb(f"{name}_var_eps", [P, NT])
        self.rstd = a.sb(f"{name}_rstd", [P, NT])
        self.var_ready = a.sem(f"{name}_var_ready")
        self.rstd_ready = a.sem(f"{name}_rstd_ready")
        self.minus_half = minus_half

    def pool(self, pool, n):
        pool.wait_ge(self.var_ready, n)
        pool.tensor_tensor(self.rstd[:], self.var_eps[:], self.minus_half[:, 0:NT], ALU.pow).then_inc(self.rstd_ready, 1)


def causal_attention(nc, g, rows):
    SCALE = float(C) ** -0.5
    NORM_AT = 5
    with ExitStack() as ctx:
        a = Alloc(nc, ctx)
        norm = Norm(a, "ln0", g.minus_half)
        h = a.sb("h0", [P, NT, C])
        h_t = a.sb("h0_t", [P, T])
        q_t = a.sb("q0_t", [P, T])
        k_t = a.sb("k0_t", [P, T])
        v = a.sb("v0", [P, NT, C])
        probs = a.sb("probs0", [P, 2, T])
        probs_t = a.sb("probs0_t", [P, NT, P])
        ctx_t = a.sb("ctx0_t", [P, 2, P])
        mx = a.sb("max0", [P, 2])
        nmx = a.sb("minus_max0", [P, 2])
        total = a.sb("total0", [P, NT])
        inv = a.sb("inv0", [P, 2])
        o = a.sb("o0", [P, 2, C])
        scores_ps = [a.ps(f"scores0_ps{i}", [P, T]) for i in range(2)]
        turn_ps = a.ps("turn0_ps", [P, T])
        ctx_ps = a.ps("ctx0_ps", [P, 512])
        out_ps = a.ps("out0_ps", [P, 512])
        vec = a.sem("attn0_vec")
        h_ready = a.sem("h0_ready")
        h_turned = a.sem("h0_turned")
        h_t_ready = a.sem("h0_t_ready")
        q_made = a.sem("q0_made")
        k_made = a.sem("k0_made")
        v_made = a.sem("v0_made")
        q_ready = a.sem("q0_ready")
        k_ready = a.sem("k0_ready")
        v_ready = a.sem("v0_ready")
        scored = a.sem("scored0")
        max_ready = a.sem("max0_ready")
        probs_ready = a.sem("probs0_ready")
        probs_turned = a.sem("probs0_turned")
        probs_t_act = a.sem("probs0_t_act")
        probs_t_dve = a.sem("probs0_t_dve")
        ctx_made = a.sem("ctx0_made")
        ctx_ready = a.sem("ctx0_ready")
        out_made = a.sem("out0_made")
        out_used = a.sem("out0_used")
        cleared = a.sem("rows_cleared")
        H = NT // 2

        with nc.Block() as block:

            @block.sync
            def _(sp):
                for of in rows:
                    of.clear(sp, g.zeros[:], cleared)
                sp.wait_ge(cleared, 16 * len(rows))

            @block.gpsimd
            def _(pool):
                with pool.Fori(0, B) as b:
                    norm.pool(pool, b + 1)

            @block.vector
            def _(dve):

                def normalise(step, b):
                    rows = g.x[:, bass.ds(b * NT, NT), :]
                    layer_norm(dve, step, norm, rows, h[:], g.mod_row(0, b, CA), lambda: dve.wait_ge(norm.rstd_ready, b + 1))
                    dve.tensor_tensor(h[:], h[:], g.mod_row(0, b, SA), ALU.add).then_inc(h_ready, 1)

                def attend_batch(b, next_too):
                    step = Steps(dve, vec)
                    dve.wait_ge(k_made, b + 1)
                    dve.tensor_copy(k_t[:], scores_ps[1][:]).then_inc(k_ready, 1)

                    def row_max(i):
                        n = (i + 1) * P
                        s = scores_ps[i % 2]
                        dve.wait_ge(scored, b * NT + i + 1)
                        step(dve.tensor_tensor(s[:, n - P : n], s[:, n - P : n], g.causal[:], ALU.add))
                        step.settle()
                        step(dve.reduce_max(mx[:, i % 2 : i % 2 + 1], s[:, 0:n], AX.X))
                        step.settle()
                        dve.tensor_scalar(nmx[:, i % 2 : i % 2 + 1], mx[:, i % 2 : i % 2 + 1], -SCALE, None, ALU.mult).then_inc(max_ready, 1)

                    def keep_probs(i):
                        if i >= H:
                            dve.wait_ge(probs_turned, b * NT + i + 1)
                            dve.tensor_copy(
                                probs_t[:, H : i + 1, :], turn_ps[:, H * P : (i + 1) * P].rearrange("p (n c) -> p n c", c=P)
                            ).then_inc(probs_t_dve, 1)

                    def residual(i):
                        one = slice(i % 2, i % 2 + 1)
                        dve.wait_ge(out_made, b * NT + i + 1)
                        step(dve.reciprocal(inv[:, one], total[:, i : i + 1]))
                        step.settle()
                        dve.scalar_tensor_tensor(
                            out=o[:, i % 2, :], in0=out_ps[:, 0:C], scalar=inv[:, one], in1=g.row("L0_attn_out_b"), op0=ALU.mult, op1=ALU.add
                        ).then_inc(out_used, 1)
                        dve.wait_ge(out_used, b * NT + i + 1)
                        step(dve.tensor_tensor(o[:, i % 2, :], o[:, i % 2, :], g.mod_part(0, b, GA), ALU.mult))
                        step.settle()
                        xr = g.x[:, bass.ds(b * NT + i, 1), :].rearrange("p n c -> p (n c)")
                        step(dve.tensor_tensor(xr, xr, o[:, i % 2, :], ALU.add))

                    row_max(0)
                    for i in range(NT):
                        if i + 1 < NT:
                            row_max(i + 1)
                        keep_probs(i)
                        if i >= 1:
                            residual(i - 1)
                        if i == NORM_AT and next_too:
                            normalise(step, b + 1)
                    residual(NT - 1)
                    step.again()

                step = Steps(dve, vec)
                normalise(step, 0)
                step.again()
                with dve.Fori(0, B - 1) as b:
                    attend_batch(b, True)
                attend_batch(B - 1, False)

            @block.scalar
            def _(act):
                with act.Fori(0, B) as b:
                    for k in range(2):
                        act.wait_ge(h_turned, b * 2 + k + 1)
                        act.activation(h_t[:, k * 512 : k * 512 + 512], turn_ps[:, k * 512 : k * 512 + 512], ACT.Copy).then_inc(h_t_ready, 1)
                    act.wait_ge(q_made, b + 1)
                    act.activation(q_t[:], scores_ps[0][:], ACT.Copy).then_inc(q_ready, 1)
                    act.wait_ge(v_made, b + 1)
                    act.activation(v[:], turn_ps[:].rearrange("p (n c) -> p n c", c=C), ACT.Copy).then_inc(v_ready, 1)

                    def exp(i):
                        one = slice(i % 2, i % 2 + 1)
                        n = (i + 1) * P
                        act.wait_ge(max_ready, b * NT + i + 1)
                        act.activation(
                            probs[:, i % 2, 0:n], scores_ps[i % 2][:, 0:n], ACT.Exp, bias=nmx[:, one], scale=SCALE, accum_out=total[:, i : i + 1]
                        ).then_inc(probs_ready, 1)

                    exp(0)
                    for i in range(NT):
                        m = min(i + 1, H)
                        act.wait_ge(probs_turned, b * NT + i + 1)
                        act.activation(probs_t[:, 0:m, :], turn_ps[:, 0 : m * P].rearrange("p (n c) -> p n c", c=P), ACT.Copy).then_inc(probs_t_act, 1)
                        if i + 1 < NT:
                            exp(i + 1)
                        act.wait_ge(ctx_made, b * NT + i + 1)
                        act.activation(ctx_t[:, i % 2, :], ctx_ps[:, 0:P], ACT.Copy).then_inc(ctx_ready, 1)

            @block.tensor
            def _(pe):
                with pe.Fori(0, B) as b:
                    pe.wait_ge(h_ready, b + 1)
                    for n in range(NT):
                        ins = pe.transpose(turn_ps[:, n * P : n * P + P], h[:, n, :], g.ident[:])
                        if n % H == H - 1:
                            ins.then_inc(h_turned, 1)
                    for k in range(2):
                        cols = slice(k * 512, k * 512 + 512)
                        pe.wait_ge(h_t_ready, b * 2 + k + 1)
                        q_ins = pe.matmul(scores_ps[0][:, cols], g.weights(W_QKV0), h_t[:, cols], start=True, stop=True)
                        if k == 1:
                            q_ins.then_inc(q_made, 1)
                        k_ins = pe.matmul(scores_ps[1][:, cols], g.weights(W_QKV0 + 1), h_t[:, cols], start=True, stop=True)
                        if k == 1:
                            k_ins.then_inc(k_made, 1)
                    for n in range(NT):
                        ins = pe.matmul(turn_ps[:, n * P : n * P + P], h_t[:, n * P : n * P + P], g.weights(W_QKV0 + 2), start=True, stop=True)
                    ins.then_inc(v_made, 1)
                    pe.wait_ge(q_ready, b + 1)
                    pe.wait_ge(k_ready, b + 1)

                    def score(i):
                        n = (i + 1) * P
                        if i >= 2:
                            pe.wait_ge(probs_ready, b * NT + i - 1)
                        for c0 in range(0, n, 512):
                            c1 = min(n, c0 + 512)
                            ins = pe.matmul(scores_ps[i % 2][:, c0:c1], q_t[:, i * P : i * P + P], k_t[:, c0:c1], start=True, stop=True)
                        ins.then_inc(scored, 1)

                    def project(i):
                        pe.wait_ge(ctx_ready, b * NT + i + 1)
                        if i >= 1:
                            pe.wait_ge(out_used, b * NT + i)
                        pe.matmul(out_ps[:, 0:C], ctx_t[:, i % 2, :], g.weights(W_OUT0), start=True, stop=True).then_inc(out_made, 1)

                    score(0)
                    pe.wait_ge(v_ready, b + 1)
                    for i in range(NT):
                        if i + 1 < NT:
                            score(i + 1)
                        pe.wait_ge(probs_ready, b * NT + i + 1)
                        for n in range(i + 1):
                            ins = pe.transpose(turn_ps[:, n * P : n * P + P], probs[:, i % 2, n * P : n * P + P], g.ident[:])
                        ins.then_inc(probs_turned, 1)
                        if i >= 1:
                            project(i - 1)
                        pe.wait_ge(probs_t_act, b * NT + i + 1)
                        if i >= H:
                            pe.wait_ge(probs_t_dve, b * H + i - H + 1)
                        for n in range(i + 1):
                            ins = pe.matmul(ctx_ps[:, 0:P], v[:, n, :], probs_t[:, n, :], start=(n == 0), stop=(n == i))
                        ins.then_inc(ctx_made, 1)
                    project(NT - 1)
        a.clear_sems()


BATCH_TILES = (2 * T // P + E - 1, E * CAPACITY // P)
UNROLL = 4


class ExpertRows:

    def __init__(self, nc, layer):
        self.tiles = BATCH_TILES[layer]
        self.trash = B * self.tiles * P
        self.total = self.trash + (2 * UNROLL if layer == 0 else 2 * NT) * P
        self.rows = nc.dram_tensor(f"expert_rows{layer}_dram", [self.total, C], F32, kind="Internal").ap()

    def clear(self, eng, zeros, sem):
        n = self.total // P
        eng.dma_start(self.rows.rearrange("(p n) c -> p n c", n=n), zeros.unsqueeze(1).to_broadcast([P, n, C])).then_inc(sem, 16)


class Moe:

    def __init__(self, a, rows, layer):
        self.layer, self.tiles, self.slots, self.trash = layer, rows.tiles, rows.tiles * P, rows.trash
        self.rows = rows.rows
        self.gates = a.sb(f"gates{layer}", [P, B, 2, NT])
        self.pick = a.sb(f"pick{layer}", [P, B, 2, NT], I32)
        self.h = a.sb(f"expert_input{layer}", [P, TILES, C])
        self.send = a.sb(f"send{layer}", [P, 2, TILES], I32)
        if layer == 0:
            self.tile_expert = a.sb("tile_expert", [P, B * self.tiles + UNROLL], I32)
            self.b2 = a.sb("down_bias0", [P, E, C])
        else:
            self.up = a.sb("up1", [C, E, FF])
            self.down = a.sb("down1", [P, E * FC, C])

    def send_rows(self, g, pool, here):
        sent, before = g.rows_sent, self.layer * B * 2 * NT * 16
        for b in range(B):
            for k in range(2):
                for n in range(b * NT, b * NT + NT):
                    pool.indirect_dma_start(
                        self.rows, bass.IndirectOffsetOnAxis(ap=self.send[:, k, n : n + 1], axis=0), self.h[:, n, :], None
                    ).then_inc(sent, 16)
            pool.wait_ge(sent, before + (b + 1) * (16 * 2 * NT))
            pool.sem_inc(here, self.tiles)
        pool.sem_inc(here, max(self.tiles, 2 * UNROLL))

    def loads(self, dram):
        if self.layer == 0:
            return [
                (self.b2[:].rearrange("p e c -> p (e c)"), dram["L0_ffn_expert_b2"].rearrange("e c -> (e c)").partition_broadcast(P)),
            ]
        return [
            (self.up[:], dram["L1_ffn_W1"].rearrange("e c h -> c e h")),
            (self.down[:], dram["L1_ffn_W2"].rearrange("e (k p) c -> p (e k) c", p=P)),
        ]


def route(nc, g, moe, dram, layer):
    with ExitStack() as ctx:
        a = Alloc(nc, ctx, f"_route{layer}")
        stats = a.sb("stats", [P, TILES, 6])
        mean_var = a.sb("mean_var", [P, TILES, 2])
        var_eps = a.sb("var_eps", [P, TILES])
        rstd = a.sb("rstd", [P, TILES])
        halves = a.sb("minus_halves", [P, TILES])
        h = moe.h
        h_now = a.sb("h_now", [P, NT, C])
        h_t = a.sb("h_t", [P, T])
        logits = a.sb("logits", [P, TILES, E])
        expl = a.sb("exp_logits", [P, TILES, E])
        best = a.sb("two_best", [P, 2, TILES, E])
        masked = a.sb("masked", [P, TILES, E])
        sel_b = a.sb("selected_bf16", [P, TILES, E], BF16)
        slot = a.sb("slot", [P, TILES, E])
        kept = a.sb("kept", [P, TILES, E])
        of_best = a.sb("of_best", [P, 2, TILES, E])
        row = a.sb("row", [P, 2, TILES])
        keep = a.sb("keep", [P, 2, TILES])
        to = a.sb("to", [P, 2, TILES])
        trash = a.sb("trash", [P, 2, NT])
        m1 = a.sb("best_logit", [P, TILES])
        m2 = a.sb("next_logit", [P, TILES])
        rank = a.sb("best_rank", [P, TILES])
        total = a.sb("total_exp", [P, TILES])
        e2 = a.sb("next_exp", [P, TILES])
        share = a.sb("share", [P, TILES])
        expert_slot = a.sb("expert_slot", [P, B, E])
        first_tile = a.sb("first_tile", [P, B, E])
        full_tiles = a.sb("full_tiles", [P, NT])
        earlier = a.sb("earlier", [P, E, E])
        more = a.sb("more", [P, B * E, NT])
        tiles = a.sb("tiles", [P, B, E])
        ahead = a.sb("ahead", [P, B, E, E])
        start = a.sb("start", [P, B, E])
        tile_no = a.sb("tile_no", [P, B * moe.tiles])
        begun = a.sb("begun", [P, B, moe.tiles, E])
        expert = a.sb("expert", [P, B * moe.tiles])
        turn_ps = a.ps("turn_ps", [P, T])
        logits_ps = a.ps("logits_ps", [P, 512])
        pos_ps = a.ps("pos_ps", [P, 512])
        count_ps = a.ps("count_ps", [P, 512])
        vec = a.sem("vec")
        const_ready = a.sem("const_ready")
        var_ready = a.sem("var_ready")
        rstd_ready = a.sem("rstd_ready")
        h_ready = a.sem("h_ready")
        h_turned = a.sem("h_turned")
        h_t_ready = a.sem("h_t_ready")
        h_kept = a.sem("h_kept")
        scored = a.sem("logits_made")
        shifted = a.sem("logits_shifted")
        exp_ready = a.sem("logits_exp")
        sel_ready = a.sem("selected_ready")
        pos_made = a.sem("pos_made")
        loaded = a.sem("loaded")
        H = NT // 2

        def tall(ap):
            return ap.unsqueeze(2).to_broadcast([P, TILES, E])

        with nc.Block() as block:

            @block.sync
            def _(sp):
                for dst, src in moe.loads(dram):
                    sp.dma_start(dst, src).then_inc(loaded, 16)
                sp.wait_ge(loaded, 16 * len(moe.loads(dram)))

            @block.gpsimd
            def _(pool):
                pool.memset(halves[:], -0.5).then_inc(const_ready, 1)
                pool.wait_ge(const_ready, 1)
                consts = 1
                if layer == 0:
                    for n in range(NT):
                        pool.memset(full_tiles[:, n : n + 1], float(n * P)).then_inc(const_ready, 1)
                    for b in range(B):
                        pool.memset(first_tile[:, b, :], float(b * moe.tiles)).then_inc(const_ready, 1)
                    for e in range(E):
                        pool.memset(earlier[:, e, e:E], 0.0).then_inc(const_ready, 1)
                        if e > 0:
                            pool.memset(earlier[:, e, 0:e], 1.0).then_inc(const_ready, 1)
                    pool.memset(moe.tile_expert[:], 0).then_inc(const_ready, 1)
                    pool.iota(tile_no[:], pattern=[[1, B * moe.tiles]], base=0, channel_multiplier=0, allow_small_or_imprecise_dtypes=True).then_inc(const_ready, 1)
                    consts += NT + B + 2 * E - 1 + 2
                else:
                    pool.iota(
                        expert_slot[:], pattern=[[moe.slots, B], [CAPACITY, E]], base=0, channel_multiplier=0, allow_small_or_imprecise_dtypes=True
                    ).then_inc(const_ready, 1)
                    pool.iota(trash[:].rearrange("p k n -> p (k n)"), pattern=[[P, 2 * NT]], base=moe.trash, channel_multiplier=1, allow_small_or_imprecise_dtypes=True).then_inc(const_ready, 1)
                    consts += 2
                pool.wait_ge(const_ready, consts)
                pool.wait_ge(var_ready, 1)
                pool.tensor_tensor(rstd[:], var_eps[:], halves[:], ALU.pow).then_inc(rstd_ready, 1)

            @block.vector
            def _(dve):
                step = Steps(dve, vec)
                for n in range(TILES):
                    step(dve.bn_stats(stats[:, n, :], g.x[:, n, :]))
                step.settle()
                for n in range(TILES):
                    step(dve.bn_aggr(mean_var[:, n, :], stats[:, n, :]))
                step.settle()
                dve.tensor_scalar(var_eps[:], mean_var[:, :, 1], LN_EPS, None, ALU.add).then_inc(var_ready, 1)
                dve.wait_ge(rstd_ready, 1)
                step.again()
                with dve.Fori(0, B) as b:
                    step = Steps(dve, vec)
                    rows = h[:, bass.ds(b * NT, NT), :]
                    for n in range(NT):
                        at = bass.ds(b * NT + n, 1)
                        step(
                            dve.tensor_scalar(
                                h[:, at, :].rearrange("p n c -> p (n c)"),
                                g.x[:, at, :].rearrange("p n c -> p (n c)"),
                                mean_var[:, at, 0:1].rearrange("p n c -> p (n c)"),
                                rstd[:, at],
                                ALU.subtract,
                                ALU.mult,
                            )
                        )
                    step.settle()
                    step(dve.tensor_tensor(rows, rows, g.mod_row(layer, b, CB), ALU.mult))
                    step.settle()
                    dve.wait_ge(h_kept, b + 1)
                    dve.tensor_tensor(h_now[:], rows, g.mod_row(layer, b, SB), ALU.add).then_inc(h_ready, 1)
                    step.again()

                step = Steps(dve, vec)
                dve.wait_ge(scored, B)
                step(dve.tensor_copy(logits[:].rearrange("p n e -> p (n e)"), logits_ps[:, 0 : TILES * E]))
                step.settle()
                step(dve.reduce_max(m1[:], logits[:], AX.X))
                step.settle()
                dve.tensor_tensor(expl[:], logits[:], tall(m1[:]), ALU.subtract).then_inc(shifted, 1)

                def choose(chosen, of, top):
                    step(dve.tensor_tensor(chosen, of[:], tall(top[:]), ALU.is_equal))
                    step.settle()
                    step(dve.tensor_tensor(chosen, chosen, bc(g.expert_rank[:], TILES), ALU.mult))
                    step.settle()
                    step(dve.reduce_max(rank[:], chosen, AX.X))
                    step.settle()
                    step(dve.tensor_tensor(chosen, chosen, tall(rank[:]), ALU.is_equal))
                    step.settle()

                first, second = best[:, 0], best[:, 1]
                choose(first, logits, m1)
                step(dve.scalar_tensor_tensor(out=masked[:], in0=first, scalar=-1e30, in1=logits[:], op0=ALU.mult, op1=ALU.add))
                step.settle()
                step(dve.reduce_max(m2[:], masked[:], AX.X))
                step.settle()
                choose(second, masked, m2)
                dve.tensor_tensor(sel_b[:], first, second, ALU.add).then_inc(sel_ready, 1)
                dve.wait_ge(exp_ready, 1)
                step(dve.reduce_sum(total[:], expl[:], AX.X))
                step(dve.tensor_tensor(masked[:], expl[:], second, ALU.mult))
                step.settle()
                step(dve.reduce_sum(e2[:], masked[:], AX.X))
                step.settle()
                if layer == 0:
                    step(dve.scalar_tensor_tensor(out=total[:], in0=total[:], scalar=1e-9, in1=e2[:], op0=ALU.mult, op1=ALU.add))
                    step.settle()
                    step(dve.tensor_scalar(total[:], total[:], 1.0, None, ALU.add))
                    step.settle()
                step(dve.reciprocal(share[:], total[:]))
                step.settle()
                step(dve.tensor_tensor(e2[:], e2[:], share[:], ALU.mult))
                dve.wait_ge(pos_made, 1)
                pos = pos_ps[:, 0 : TILES * E].rearrange("p (b n e) -> p b n e", b=B, e=E)
                slots = slot[:].rearrange("p (b n) e -> p b n e", b=B)
                if layer == 0:
                    step(dve.tensor_tensor(more[:], count_ps[:, 0 : B * E].unsqueeze(2).to_broadcast([P, B * E, NT]), bc(full_tiles[:], B * E), ALU.is_gt))
                    step.settle()
                    step(dve.reduce_sum(tiles[:].rearrange("p b e -> p (b e)"), more[:], AX.X))
                    step.settle()
                    step(
                        dve.tensor_tensor(
                            ahead[:], tiles[:].unsqueeze(2).to_broadcast([P, B, E, E]), earlier[:].unsqueeze(1).to_broadcast([P, B, E, E]), ALU.mult
                        )
                    )
                    step.settle()
                    step(dve.reduce_sum(start[:], ahead[:], AX.X))
                    step.settle()
                    step(dve.tensor_tensor(start[:], start[:], first_tile[:], ALU.add))
                    step.settle()
                    for b in range(B):
                        step(dve.scalar_tensor_tensor(out=slots[:, b], in0=bc(start[:, b], NT), scalar=float(P), in1=pos[:, b], op0=ALU.mult, op1=ALU.add))
                    of_batch = [P, B, moe.tiles, E]
                    step(
                        dve.tensor_tensor(
                            begun[:],
                            start[:].unsqueeze(2).to_broadcast(of_batch),
                            tile_no[:].rearrange("p (b n) -> p b n", b=B).unsqueeze(3).to_broadcast(of_batch),
                            ALU.is_le,
                        )
                    )
                    step.settle()
                    step(dve.reduce_sum(expert[:], begun[:].rearrange("p b n e -> p (b n) e"), AX.X))
                    step.settle()
                    step(dve.tensor_scalar(moe.tile_expert[:, 0 : B * moe.tiles], expert[:], -1.0, None, ALU.add))
                else:
                    step(dve.tensor_scalar(kept[:].rearrange("p n e -> p (n e)"), pos_ps[:, 0 : TILES * E], float(CAPACITY), None, ALU.is_lt))
                    for b in range(B):
                        step(
                            dve.scalar_tensor_tensor(
                                out=slots[:, b], in0=pos[:, b], scalar=float(CAPACITY - 1), in1=bc(expert_slot[:, b], NT), op0=ALU.min, op1=ALU.add
                            )
                        )
                    step.settle()
                both = lambda ap: ap.unsqueeze(1).to_broadcast([P, 2, TILES, E])
                step(dve.tensor_tensor(of_best[:], best[:], both(slot[:]), ALU.mult))
                step.settle()
                step(dve.reduce_sum(row[:], of_best[:], AX.X))
                step.settle()
                gate = lambda k: moe.gates[:, :, k, :]
                batches = lambda ap: ap.rearrange("p (b n) -> p b n", b=B)
                if layer == 0:
                    step(dve.tensor_copy(moe.send[:], row[:]))
                    step(dve.tensor_copy(gate(0), batches(share[:])))
                    step(dve.tensor_copy(gate(1), batches(e2[:])))
                else:
                    step(dve.tensor_tensor(of_best[:], best[:], both(kept[:]), ALU.mult))
                    step.settle()
                    step(dve.reduce_sum(keep[:], of_best[:], AX.X))
                    step.settle()
                    aside = trash[:].unsqueeze(2).to_broadcast([P, 2, B, NT])
                    tos = to[:].rearrange("p k (b n) -> p k b n", b=B)
                    step(dve.tensor_tensor(tos, row[:].rearrange("p k (b n) -> p k b n", b=B), aside, ALU.subtract))
                    step.settle()
                    step(dve.tensor_tensor(to[:], to[:], keep[:], ALU.mult))
                    step.settle()
                    step(dve.tensor_tensor(moe.send[:].rearrange("p k (b n) -> p k b n", b=B), tos, aside, ALU.add))
                    step(dve.tensor_tensor(gate(0), batches(share[:]), batches(keep[:, 0]), ALU.mult))
                    step(dve.tensor_tensor(gate(1), batches(e2[:]), batches(keep[:, 1]), ALU.mult))
                for k in range(2):
                    step(dve.tensor_copy(moe.pick[:, :, k, :], batches(row[:, k])))
                step.again()

            @block.scalar
            def _(act):
                act.sem_inc(h_kept, 1)
                with act.Fori(0, B) as b:
                    for k in range(2):
                        act.wait_ge(h_turned, b * 2 + k + 1)
                        act.activation(h_t[:, k * 512 : k * 512 + 512], turn_ps[:, k * 512 : k * 512 + 512], ACT.Copy).then_inc(h_t_ready, 1)
                    act.activation(h[:, bass.ds(b * NT, NT), :], h_now[:], ACT.Copy).then_inc(h_kept, 1)
                act.wait_ge(shifted, 1)
                act.activation(expl[:], expl[:], ACT.Exp).then_inc(exp_ready, 1)

            @block.tensor
            def _(pe):
                router = g.weights(W_ROUTER0)[:, 0:E] if layer == 0 else g.wr1[:]
                with pe.Fori(0, B) as b:
                    pe.wait_ge(h_ready, b + 1)
                    for n in range(NT):
                        ins = pe.transpose(turn_ps[:, n * P : n * P + P], h_now[:, n, :], g.ident[:])
                        if n % H == H - 1:
                            ins.then_inc(h_turned, 1)
                    pe.wait_ge(h_t_ready, b * 2 + 2)
                    for n in range(NT):
                        ins = pe.matmul(logits_ps[:, bass.ds(b * (NT * E) + n * E, E)], h_t[:, n * P : n * P + P], router, start=True, stop=True)
                    ins.then_inc(scored, 1)
                pe.wait_ge(sel_ready, 1)
                for b in range(B):
                    if layer == 0:
                        for m in range(NT):
                            pe.matmul(count_ps[:, b * E : b * E + E], g.ones_b[:], sel_b[:, b * NT + m, :], start=(m == 0), stop=(m == NT - 1))
                    for n in range(NT):
                        to_tile = slice((b * NT + n) * E, (b * NT + n + 1) * E)
                        for m in range(n + 1):
                            ins = pe.matmul(
                                pos_ps[:, to_tile], g.before[:] if m == n else g.ones_b[:], sel_b[:, b * NT + m, :], start=(m == 0), stop=(m == n)
                            )
                ins.then_inc(pos_made, 1)
        a.clear_sems()


class Combine:

    def __init__(self, nc, g, moe, a):
        self.g, self.moe = g, moe
        self.y = a.sb("picked", [P, B, 2, NT, C])
        self.vec = a.sem("combine_vec")
        self.picked, self.picked_before = g.rows_picked, moe.layer * B * 2 * NT * 16
        self.rounds = a.sem("combine_rounds")
        self.here = a.sem("picked_here")

    def gather(self, pool, b):
        moe = self.moe
        pool.sem_inc(self.rounds, 1)
        for k in range(2):
            for n in range(NT):
                pool.indirect_dma_start(
                    self.y[:, b, k, n, :], None, moe.rows, bass.IndirectOffsetOnAxis(ap=moe.pick[:, b, k, n : n + 1], axis=0)
                ).then_inc(self.picked, 16)
        pool.wait_ge(self.picked, self.picked_before + (b + 1) * (16 * 2 * NT))
        pool.sem_inc(self.here, 1)

    def add(self, dve):
        g, moe = self.g, self.moe
        with dve.Fori(0, B) as b:
            step = Steps(dve, self.vec)
            one = bass.ds(b, 1)
            y = self.y[:, one].rearrange("p b k n c -> p (b k n) c")
            first, second = y[:, 0:NT], y[:, NT : 2 * NT]
            gates = moe.gates[:, one].rearrange("p b k n -> p (b k n)").unsqueeze(2).to_broadcast([P, 2 * NT, C])
            dve.wait_ge(self.here, b + 1)
            step(dve.tensor_tensor(y, y, gates, ALU.mult))
            step.settle()
            step(dve.tensor_tensor(first, first, second, ALU.add))
            step.settle()
            step(dve.tensor_tensor(first, first, g.mod_row(moe.layer, b, GB), ALU.mult))
            step.settle()
            xr = g.x[:, bass.ds(b * NT, NT), :]
            step(dve.tensor_tensor(xr, xr, first, ALU.add))
            step.again()


def experts0(nc, g, moe):
    STEPS = B * moe.tiles // UNROLL
    AHEAD = -(-moe.tiles // UNROLL)
    HALF = UNROLL // 2
    with ExitStack() as ctx:
        a = Alloc(nc, ctx, "_experts0")
        combine = Combine(nc, g, moe, a)
        x_rows = a.sb("x_rows", [P, UNROLL, C])
        x_t = a.sb("x_t", [C, UNROLL, P])
        up_now = a.sb("up_weights_now", [C, UNROLL, FC, P])
        pre = a.sb("pre", [P, 2, FC, P])
        hidden = a.sb("hidden", [P, 2, FC, P])
        y_rows = a.sb("y_rows", [P, UNROLL, C])
        xt_ps = a.ps("xt_ps", [C, UNROLL, P])
        up_ps = [a.ps(f"up_ps{i}", [P, FC, P]) for i in range(2)]
        down_ps = [a.ps(f"down_ps{i}", [P, 512]) for i in range(2)]
        rows_loaded = a.sem("rows_loaded")
        x_turned = a.sem("x_turned")
        x_t_ready = a.sem("x_t_ready")
        up_here = a.sem("up_weights_here")
        up_made = a.sem("up_made")
        pre_ready = a.sem("pre_ready")
        hidden_ready = a.sem("hidden_ready")
        down_made = a.sem("down_made")
        y_ready = a.sem("y_ready")
        stored = a.sem("stored")
        y_free = a.sem("y_free")
        rows_here = a.sem("rows_here")
        sp_rounds = a.sem("sp_rounds")
        up_w = lambda e: g.wt0[:, bass.ds(e * FC + W_UP0, FC), :]
        up_bias = lambda e: g.weights(W_BIAS)[:, bass.ds(e * FC + B_UP0, FC)]
        down_w = lambda e, k: g.wt0[:, bass.ds(e * FC + (W_DOWN0 + k), 1), :].rearrange("p k c -> p (k c)")

        def experts_of(engine, tile, n):
            at = slice(tile, tile + n) if isinstance(tile, int) else bass.ds(tile, n)
            return nc.values_load_multi_w_load_instructions(
                moe.tile_expert[0:1, at],
                engines=(engine,),
                min_val=0,
                max_val=E - 1,
                skip_runtime_bounds_check_because="the router counts the experts that begin at a tile: the first always, all E at most",
            )[1]

        with nc.Block() as block:

            @block.sync
            def _(sp):
                rows = lambda of, at: of[bass.ds(at * (UNROLL * P), UNROLL * P), :].rearrange("(n p) c -> p n c", p=P)
                sp.wait_ge(rows_here, UNROLL)
                sp.dma_start(x_rows[:], moe.rows[0 : UNROLL * P, :].rearrange("(n p) c -> p n c", p=P)).then_inc(rows_loaded, 16)
                sp.sem_inc(y_free, 1)
                sp.wait_ge(x_turned, 1)
                sp.sem_inc(sp_rounds, 1)
                sp.wait_ge(rows_here, 2 * UNROLL)
                sp.dma_start(x_rows[:], moe.rows[UNROLL * P : 2 * UNROLL * P, :].rearrange("(n p) c -> p n c", p=P)).then_inc(rows_loaded, 16)
                with sp.Fori(0, STEPS) as i:
                    for k in range(2):
                        sp.wait_ge(y_ready, i * UNROLL + (HALF * (k + 1) + 2))
                        at = bass.ds(i * (UNROLL * P) + k * HALF * P, HALF * P)
                        sp.dma_start(moe.rows[at, :].rearrange("(n p) c -> p n c", p=P), y_rows[:, k * HALF : (k + 1) * HALF, :]).then_inc(stored, 16)
                        if k == 0:
                            sp.wait_ge(x_turned, i + 2)
                            sp.sem_inc(sp_rounds, 1)
                            sp.wait_ge(rows_here, i * UNROLL + 3 * UNROLL)
                            sp.dma_start(x_rows[:], rows(moe.rows, i + 2)).then_inc(rows_loaded, 16)
                        sp.wait_ge(stored, i * 32 + (k + 1) * 16)
                        sp.sem_inc(y_free, 1)
                sp.wait_ge(rows_loaded, (STEPS + 2) * 16)
                sp.sem_inc(y_free, 2 * (AHEAD * B - STEPS))

            @block.gpsimd
            def _(pool):
                moe.send_rows(g, pool, rows_here)
                for b in range(B):
                    pool.wait_ge(y_free, b * (2 * AHEAD) + (2 * AHEAD + 1))
                    combine.gather(pool, b)

            @block.vector
            def _(dve):

                def bring_up(e, k):
                    dve.tensor_copy(up_now[:, k % UNROLL], up_w(e)).then_inc(up_here, 1)

                def add_bias(e, tile, k):
                    dve.wait_ge(up_made, tile + 1)
                    dve.tensor_tensor(
                        pre[:, k % 2], up_ps[k % 2][:], up_bias(e).unsqueeze(2).to_broadcast([P, FC, P]), ALU.add
                    ).then_inc(pre_ready, 1)

                def add_down_bias(e, i, tile, k):
                    if k % HALF == 0:
                        dve.wait_ge(y_free, i * 2 + (k // HALF + 1))
                    dve.wait_ge(down_made, tile + 1)
                    dve.tensor_tensor(
                        y_rows[:, k, :], down_ps[k % 2][:, 0:C], moe.b2[:, bass.ds(e, 1), :].rearrange("p e c -> p (e c)"), ALU.add
                    ).then_inc(y_ready, 1)

                dve.sem_inc(y_ready, 2)
                e = experts_of(mybir.EngineType.DVE, 0, UNROLL)
                for k in range(UNROLL):
                    bring_up(e[k], k)
                for k in range(2):
                    add_bias(e[k], k, k)
                with dve.Fori(0, STEPS) as i:
                    e = experts_of(mybir.EngineType.DVE, i * UNROLL, 2 * UNROLL)
                    for k in range(UNROLL):
                        add_bias(e[k + 2], i * UNROLL + (k + 2), k)
                        add_down_bias(e[k], i, i * UNROLL + k, k)
                        bring_up(e[k + UNROLL], k)
                combine.add(dve)

            @block.scalar
            def _(act):

                def keep_x(i):
                    act.wait_ge(x_turned, i + 1)
                    act.activation(x_t[:], xt_ps[:], ACT.Copy).then_inc(x_t_ready, 1)

                def gelu(tile, k):
                    act.wait_ge(pre_ready, tile + 1)
                    if k >= 2:
                        act.wait_ge(down_made, tile - 1)
                    act.activation(hidden[:, k % 2], pre[:, k % 2], ACT.Gelu).then_inc(hidden_ready, 1)

                keep_x(0)
                for k in range(2):
                    gelu(k, k)
                with act.Fori(0, STEPS) as i:
                    for k in range(UNROLL):
                        if k == 1:
                            keep_x(i + 1)
                        gelu(i * UNROLL + (k + 2), k + 2)

            @block.tensor
            def _(pe):

                def turn_x():
                    for k in range(UNROLL):
                        ins = pe.transpose(xt_ps[:, k, :], x_rows[:, k, :], g.ident[:])
                    ins.then_inc(x_turned, 1)

                def go_up(tile, k):
                    pe.wait_ge(up_here, tile + 1)
                    for c in range(FC):
                        ins = pe.matmul(up_ps[k % 2][:, c, :], up_now[:, k % UNROLL, c, :], x_t[:, k % UNROLL, :], start=True, stop=True)
                    ins.then_inc(up_made, 1)

                def go_down(e, tile, k):
                    pe.wait_ge(y_ready, tile + 1)
                    for c in range(FC):
                        ins = pe.matmul(down_ps[k % 2][:, 0:C], hidden[:, k % 2, c, :], down_w(e, c), start=(c == 0), stop=(c == FC - 1))
                    ins.then_inc(down_made, 1)

                pe.wait_ge(rows_loaded, 16)
                turn_x()
                pe.wait_ge(x_t_ready, 1)
                for k in range(2):
                    go_up(k, k)
                with pe.Fori(0, STEPS) as i:
                    e = experts_of(mybir.EngineType.PE, i * UNROLL, UNROLL)
                    for k in range(UNROLL):
                        tile = i * UNROLL + k
                        pe.wait_ge(hidden_ready, tile + 1)
                        if k == 2:
                            pe.wait_ge(x_t_ready, i + 2)
                        go_up(i * UNROLL + (k + 2), k + 2)
                        if k == 1:
                            pe.wait_ge(rows_loaded, i * 16 + 32)
                            turn_x()
                        go_down(e[k], tile, k)
        a.clear_sems()


def experts1(nc, g, moe):
    ROWS_BATCH = moe.slots
    PARTS = [(n, min(n + 4, moe.tiles)) for n in range(0, moe.tiles, 4)]
    with ExitStack() as ctx:
        a = Alloc(nc, ctx, "_experts1")
        combine = Combine(nc, g, moe, a)
        x_rows = a.sb("x_rows", [P, moe.tiles, C])
        x_t = a.sb("x_t", [C, ROWS_BATCH])
        hidden = a.sb("hidden", [P, 2, FC, CAPACITY])
        y_t = a.sb("y_t", [C, ROWS_BATCH])
        y_rows = a.sb("y_rows", [P, moe.tiles, C])
        turn_ps = [a.ps(f"turn_ps{i}", [P, 4, P]) for i in range(2)]
        up_ps = [a.ps(f"up_ps{i}", [P, FC, 256]) for i in range(2)]
        down_ps = [a.ps(f"down_ps{i}", [C, 512]) for i in range(2)]
        rows_loaded = a.sem("rows_loaded")
        x_turned = a.sem("x_turned")
        x_t_ready = a.sem("x_t_ready")
        up_made = a.sem("up_made")
        hidden_act = a.sem("hidden_act")
        hidden_dve = a.sem("hidden_dve")
        down_made = a.sem("down_made")
        y_t_ready = a.sem("y_t_ready")
        y_turned = a.sem("y_turned")
        y_ready = a.sem("y_ready")
        stored = a.sem("stored")
        sp_rounds = a.sem("sp_rounds")
        rows_here = a.sem("rows_here")
        NP = len(PARTS)
        H = FC // 2

        with nc.Block() as block:

            @block.sync
            def _(sp):
                rows = lambda of: of.rearrange("(n p) c -> p n c", p=P)
                sp.wait_ge(rows_here, moe.tiles)
                sp.dma_start(x_rows[:], rows(moe.rows[0:ROWS_BATCH])).then_inc(rows_loaded, 16)
                with sp.Fori(0, B) as b:
                    sp.wait_ge(x_turned, b * NP + NP)
                    sp.sem_inc(sp_rounds, 1)
                    sp.wait_ge(rows_here, b * moe.tiles + 2 * moe.tiles)
                    sp.dma_start(x_rows[:], rows(moe.rows[bass.ds(b * ROWS_BATCH + ROWS_BATCH, ROWS_BATCH), :])).then_inc(rows_loaded, 16)
                    sp.wait_ge(y_ready, b * NP + NP)
                    sp.dma_start(rows(moe.rows[bass.ds(b * ROWS_BATCH, ROWS_BATCH), :]), y_rows[:]).then_inc(stored, 16)
                    sp.wait_ge(stored, b * 16 + 16)
                    sp.sem_inc(sp_rounds, 1)
                sp.wait_ge(rows_loaded, (B + 1) * 16)

            @block.gpsimd
            def _(pool):
                moe.send_rows(g, pool, rows_here)
                for b in range(B):
                    pool.wait_ge(stored, b * 16 + 16)
                    combine.gather(pool, b)

            @block.vector
            def _(dve):
                with dve.Fori(0, B) as b:

                    def relu(e):
                        dve.wait_ge(up_made, b * E + (e + 1))
                        for k in range(H, FC):
                            dve.tensor_scalar(
                                hidden[:, e % 2, k, :], up_ps[e % 2][:, k, 0:CAPACITY], g.bias(B_UP1 + e * FC + k), 0.0, ALU.add, ALU.max
                            ).then_inc(hidden_dve, 1)

                    def add_bias(e):
                        dve.wait_ge(down_made, b * E + (e + 1))
                        dve.tensor_scalar(
                            y_t[:, e * CAPACITY : (e + 1) * CAPACITY], down_ps[e % 2][:, 0:CAPACITY], g.bias(B_DOWN1 + e), None, ALU.add
                        ).then_inc(y_t_ready, 1)

                    relu(0)
                    for e in range(1, E):
                        relu(e)
                        add_bias(e - 1)
                    add_bias(E - 1)
                    for n, (n0, n1) in enumerate(PARTS):
                        dve.wait_ge(y_turned, b * NP + (n + 1))
                        dve.tensor_copy(y_rows[:, n0:n1, :], turn_ps[n % 2][:, 0 : n1 - n0, :]).then_inc(y_ready, 1)
                    dve.wait_ge(stored, b * 16 + 16)
                    dve.sem_inc(sp_rounds, 1)
                combine.add(dve)

            @block.scalar
            def _(act):
                with act.Fori(0, B) as b:
                    for n, (n0, n1) in enumerate(PARTS):
                        act.wait_ge(x_turned, b * NP + (n + 1))
                        act.activation(x_t[:, n0 * P : n1 * P].rearrange("p (n c) -> p n c", c=P), turn_ps[n % 2][:, 0 : n1 - n0, :], ACT.Copy).then_inc(x_t_ready, 1)
                    for e in range(E):
                        act.wait_ge(up_made, b * E + (e + 1))
                        for k in range(H):
                            act.activation(
                                hidden[:, e % 2, k, :], up_ps[e % 2][:, k, 0:CAPACITY], ACT.Relu, bias=g.bias(B_UP1 + e * FC + k)
                            ).then_inc(hidden_act, 1)

            @block.tensor
            def _(pe):
                with pe.Fori(0, B) as b:

                    def go_up(e):
                        if e >= 2:
                            pe.wait_ge(hidden_act, b * (E * H) + (e - 1) * H)
                            pe.wait_ge(hidden_dve, b * (E * H) + (e - 1) * H)
                        for k in range(FC):
                            ins = pe.matmul(
                                up_ps[e % 2][:, k, 0:CAPACITY], moe.up[:, e, k * P : k * P + P], x_t[:, e * CAPACITY : (e + 1) * CAPACITY], start=True, stop=True
                            )
                        ins.then_inc(up_made, 1)

                    def go_down(e):
                        pe.wait_ge(hidden_act, b * (E * H) + (e + 1) * H)
                        pe.wait_ge(hidden_dve, b * (E * H) + (e + 1) * H)
                        if e >= 2:
                            pe.wait_ge(y_t_ready, b * E + (e - 1))
                        for k in range(FC):
                            ins = pe.matmul(
                                down_ps[e % 2][:, 0:CAPACITY], moe.down[:, e * FC + k, :], hidden[:, e % 2, k, :], start=(k == 0), stop=(k == FC - 1)
                            )
                        ins.then_inc(down_made, 1)

                    pe.wait_ge(rows_loaded, b * 16 + 16)
                    for n, (n0, n1) in enumerate(PARTS):
                        if n >= 2:
                            pe.wait_ge(x_t_ready, b * NP + (n - 1))
                        for m in range(n0, n1):
                            ins = pe.transpose(turn_ps[n % 2][:, m - n0, :], x_rows[:, m, :], g.ident[:])
                        ins.then_inc(x_turned, 1)
                    pe.wait_ge(x_t_ready, b * NP + NP)
                    go_up(0)
                    for e in range(1, E):
                        go_up(e)
                        go_down(e - 1)
                    go_down(E - 1)
                    pe.wait_ge(y_t_ready, b * E + E)
                    for n, (n0, n1) in enumerate(PARTS):
                        if n >= 2:
                            pe.wait_ge(y_ready, b * NP + (n - 1))
                        for m in range(n0, n1):
                            ins = pe.transpose(turn_ps[n % 2][:, m - n0, :], y_t[:, m * P : m * P + P], g.ident[:])
                        ins.then_inc(y_turned, 1)
                    pe.wait_ge(y_ready, b * NP + NP)


ROWS = ["L0_attn_out_b", "L1_attn_out_proj_b", "L1_attn_Vp_b", "L1_attn_ff2_b", "L1_attn_ln1_g", "L1_attn_ln1_b", "L1_attn_ln2_g", "L1_attn_ln2_b"]


class Shared:

    def __init__(self, a):
        self.x = a.sb("x", [P, TILES, C])
        self.ident = a.sb("ident", [P, P])
        self.causal = a.sb("causal", [P, P])
        self.minus_half = a.sb("minus_half", [P, 16])
        self.mods = [None, a.sb("mod1", [P, B, 6 * C])]
        self.wt1 = a.sb("weights1_t", [P, W_SLOTS - W_SLOTS_L0, P])
        self.rows = a.sb("bias_rows", [P, len(ROWS), C])
        self.lam = a.sb("lam", [P, 1])
        self.v_bias = a.sb("v_bias", [P, C])
        self.expert_rank = a.sb("expert_rank", [P, E])
        self.before = a.sb("before", [P, P], BF16)
        self.ones_b = a.sb("ones_bf16", [P, P], BF16)
        self.rows_sent = a.sem("rows_sent")
        self.rows_picked = a.sem("rows_picked")
        self.zeros = a.sb("zeros", [P, C])
        self.wr1 = a.sb("router1", [C, E])

    def bias(self, row):
        return self.weights(W_BIAS)[:, row : row + 1]

    def weights(self, slot, n=None):
        w, at = (self.wt0, slot) if slot < W_SLOTS_L0 else (self.wt1, slot - W_SLOTS_L0)
        return w[:, at, :] if n is None else w[:, at : at + n, :]

    def row(self, name):
        return self.rows[:, ROWS.index(name), :]

    def mod_part(self, layer, b, part):
        return self.mods[layer][:, bass.ds(b, 1), part * C : part * C + C].rearrange("p n c -> p (n c)")

    def mod_row(self, layer, b, part):
        return self.mods[layer][:, bass.ds(b, 1), part * C : part * C + C].to_broadcast([P, NT, C])

    def small_loads(self, dram):
        return [(self.rows[:, i, :], dram[n].partition_broadcast(P)) for i, n in enumerate(ROWS)] + [
            (self.wr1[:], dram["L1_ffn_Wr"]),
            (self.lam[:], dram["L1_attn_lam"].partition_broadcast(P)),
            (self.v_bias[:], dram["L1_attn_in_proj_b"][2 * C : 3 * C].partition_broadcast(P)),
        ]


def store(nc, g, out):
    with ExitStack() as ctx:
        a = Alloc(nc, ctx)
        stored = a.sem("stored")
        with nc.Block() as block:

            @block.sync
            def _(sp):
                sp.dma_start(out.rearrange("b (n p) c -> p (b n) c", p=P), g.x[:]).then_inc(stored, 16)
                sp.wait_ge(stored, 16)


HEADS, DH = 16, 8
GROUPS = HEADS // 4
PIECES = 3
SHIFT_ROW = PIECES * PIECES * DH
PACK_ROWS = SHIFT_ROW + PIECES
TOP = max(1, int(T * 0.2))
SCALE1 = float(DH) ** -0.5
HEADROOM = 60.0
FLOOR = 50.0


class Scratch:

    def __init__(self, nc):
        self.q = nc.dram_tensor("q_pieces_dram", [B, PIECES, C, T], BF16, kind="Internal").ap()
        self.k = nc.dram_tensor("k_pieces_dram", [B, PIECES, C, T], BF16, kind="Internal").ap()
        self.shift = nc.dram_tensor("shift_pieces_dram", [B, PIECES, HEADS, T], BF16, kind="Internal").ap()
        self.h = nc.dram_tensor("h1_dram", [B, NT, P, C], F32, kind="Internal").ap()
        self.v = nc.dram_tensor("v_dram", [B, NT, P, C], F32, kind="Internal").ap()
        self.sparse_q = nc.dram_tensor("sparse_q_dram", [B, RQ, T], F32, kind="Internal").ap()
        self.sparse_out = nc.dram_tensor("sparse_out_dram", [B, NT, P, C], F32, kind="Internal").ap()


class Fused:

    def __init__(self, a):
        self.v = a.sb("v1", [P, TILES, C])
        self.sparse_k = a.sb("sparse_k", [P, B * T])
        self.sparse_v = a.sb("sparse_v", [P, TILES, C])
        self.minus_mean = a.sb("minus_mean", [P, TILES])
        self.doubt = a.sb("doubt", [P, 2])


def prepare(nc, g, f, scratch, dram):
    with ExitStack() as ctx:
        a = Alloc(nc, ctx)
        norm = Norm(a, "ln1", g.minus_half)
        h = a.sb("h1", [P, NT, C])
        h_t = a.sb("h1_t", [P, T])
        q = a.sb("q1", [P, T])
        k = a.sb("k1", [P, T])
        rest = a.sb("rest", [P, 2, T])
        q_p = a.sb("q1_pieces", [P, PIECES, T], BF16)
        k_p = a.sb("k1_pieces", [P, PIECES, T], BF16)
        square = a.sb("square", [P, 2, T])
        head_sum = a.sb("head_sum", [P, HEADS])
        bound = a.sb("bound", [HEADS, T])
        shift = a.sb("shift", [HEADS, T])
        shift_rest = a.sb("shift_rest", [HEADS, T])
        shift_p = a.sb("shift_pieces", [HEADS, PIECES, T], BF16)
        k_max = a.sb("k_max", [HEADS, 1])
        sq = a.sb("sparse_q_t", [P, T])
        sk_sum = a.sb("sparse_k_sum", [P, 1])
        sq_w = a.sb("sparse_q_w", [P, P])
        sk_w = a.sb("sparse_k_w", [P, P])
        ps_a = a.ps("prep_ps_a", [P, T])
        ps_b = a.ps("prep_ps_b", [P, T])
        ps_c = a.ps("prep_ps_c", [P, T])
        ps_d = a.ps("prep_ps_d", [P, T])
        vec = a.sem("prep_vec")
        const_ready = a.sem("prep_const")
        pads_ready = a.sem("pads_ready")
        h_ready = a.sem("h1_ready")
        h_turned = a.sem("h1_turned")
        h_t_ready = a.sem("h1_t_ready")
        q_made = a.sem("q1_made")
        k_made = a.sem("k1_made")
        v_made = a.sem("v1_made")
        q_ready = a.sem("q1_ready")
        k_ready = a.sem("k1_ready")
        v_ready = a.sem("v1_ready")
        sq_made = a.sem("sparse_q_made")
        sk_made = a.sem("sparse_k_made")
        sv_made = a.sem("sparse_v_made")
        sq_ready = a.sem("sparse_q_ready")
        sk_ready = a.sem("sparse_k_ready")
        mean_made = a.sem("sparse_mean_made")
        q_squared = a.sem("q1_squared")
        k_squared = a.sem("k1_squared")
        norms_made = a.sem("norms_made")
        norms_used = a.sem("norms_used")
        bound_ready = a.sem("bound_ready")
        sqrt_ready = a.sem("sqrt_ready")
        piece = a.sem("pieces_act")
        left = a.sem("pieces_dve")
        shift_ready = a.sem("shift_ready")
        stored = a.sem("prep_stored")
        pieces_free = a.sem("pieces_free")
        h_stored = a.sem("h1_stored")
        STORES = 3 * PIECES + 2

        with nc.Block() as block:

            @block.gpsimd
            def _(pool):
                pool.memset(head_sum[:], 1.0).then_inc(const_ready, 1)
                pool.wait_ge(const_ready, 1)
                pool.affine_select(
                    out=head_sum[:], in_=head_sum[:], compare_op=ALU.is_ge, fill=0.0, base=0, pattern=[[-DH, HEADS]], channel_multiplier=1
                ).then_inc(const_ready, 1)
                pool.wait_ge(const_ready, 2)
                pool.affine_select(
                    out=head_sum[:], in_=head_sum[:], compare_op=ALU.is_ge, fill=0.0, base=DH - 1, pattern=[[DH, HEADS]], channel_multiplier=-1
                ).then_inc(const_ready, 1)
                with pool.Fori(0, B) as b:
                    norm.pool(pool, b + 1)

            @block.vector
            def _(dve):
                step = Steps(dve, vec)
                step(dve.memset(sq_w[:], 0.0))
                step(dve.memset(sk_w[:], 0.0))
                step.settle()
                dve.tensor_copy(sq_w[:, 0:RQ], g.weights(W_QK1)[:, 0:RQ]).then_inc(pads_ready, 1)
                dve.tensor_copy(sk_w[:, 0:RQ], g.weights(W_QK1)[:, RQ : 2 * RQ]).then_inc(pads_ready, 1)
                step.again()
                def normalise(step, b):
                    rows = g.x[:, bass.ds(b * NT, NT), :]
                    if not isinstance(b, int):
                        dve.wait_ge(h_stored, 16 * b)
                    layer_norm(dve, step, norm, rows, h[:], g.mod_row(1, b, CA), lambda: dve.wait_ge(norm.rstd_ready, b + 1))
                    step(dve.tensor_tensor(h[:], h[:], g.mod_row(1, b, SA), ALU.add))
                    step.settle()
                    dve.sem_inc(h_ready, 1)

                def project(b, next_too):
                    step = Steps(dve, vec)
                    dve.wait_ge(k_made, b + 1)
                    dve.tensor_scalar(k[:], ps_c[:], g.bias(B_K1), None, ALU.add).then_inc(k_ready, 1)
                    dve.wait_ge(v_made, b + 1)
                    dve.tensor_tensor(
                        f.v[:, bass.ds(b * NT, NT), :], ps_a[:].rearrange("p (n c) -> p n c", c=C), bc(g.v_bias[:], NT), ALU.add
                    ).then_inc(v_ready, 1)
                    dve.wait_ge(pieces_free, b + 1)
                    dve.wait_ge(sq_made, b + 1)
                    dve.tensor_scalar(sq[:], ps_b[:], g.bias(B_SQ1), float(RQ) ** -0.5, ALU.add, ALU.mult).then_inc(sq_ready, 1)
                    for i in range(PIECES - 1):
                        for n, (whole, pieces) in enumerate(((q, q_p), (k, k_p))):
                            dve.wait_ge(piece, b * 4 + 2 * i + n + 1)
                            of = whole[:] if i == 0 else rest[:, n, :]
                            to = rest[:, n, :] if i == 0 else pieces[:, 2, :]
                            dve.tensor_tensor(to, of, pieces[:, i, :], ALU.subtract).then_inc(left, 1)
                    dve.wait_ge(sv_made, b + 1)
                    step(
                        dve.tensor_tensor(
                            f.sparse_v[:, bass.ds(b * NT, NT), :], ps_a[:].rearrange("p (n c) -> p n c", c=C), bc(g.row("L1_attn_Vp_b"), NT), ALU.add
                        )
                    )
                    dve.wait_ge(mean_made, b + 1)
                    step(dve.tensor_scalar(f.minus_mean[:, bass.ds(b * NT, NT)], ps_b[:, 0:NT], -1.0 / T, None, ALU.mult))
                    if next_too:
                        normalise(step, b + 1)
                    dve.wait_ge(norms_made, 2 * b + 1)
                    dve.reduce_max(k_max[:], ps_d[0:HEADS, :], AX.X).then_inc(norms_used, 1)
                    dve.wait_ge(norms_used, 2 * b + 1)
                    dve.wait_ge(norms_made, 2 * b + 2)
                    dve.tensor_scalar(bound[:], ps_d[0:HEADS, :], k_max[:, 0:1], 1e-30, ALU.mult, ALU.max).then_inc(norms_used, 1)
                    dve.wait_ge(sqrt_ready, b + 1)
                    step(dve.tensor_scalar(shift[:], bound[:], -1.0, HEADROOM / SCALE1, ALU.mult, ALU.add))
                    step.settle()
                    step(dve.tensor_copy(shift_p[:, 0, :], shift[:]))
                    step.settle()
                    step(dve.tensor_tensor(shift_rest[:], shift[:], shift_p[:, 0, :], ALU.subtract))
                    step.settle()
                    step(dve.tensor_copy(shift_p[:, 1, :], shift_rest[:]))
                    step.settle()
                    dve.tensor_tensor(shift_p[:, 2, :], shift_rest[:], shift_p[:, 1, :], ALU.subtract).then_inc(shift_ready, 1)
                    step.again()

                step = Steps(dve, vec)
                normalise(step, 0)
                step.again()
                with dve.Fori(0, B - 1) as b:
                    project(b, True)
                project(B - 1, False)

            @block.scalar
            def _(act):
                with act.Fori(0, B) as b:
                    for n in range(2):
                        act.wait_ge(h_turned, b * 2 + n + 1)
                        act.activation(h_t[:, n * 512 : n * 512 + 512], ps_a[:, n * 512 : n * 512 + 512], ACT.Copy).then_inc(h_t_ready, 1)
                    act.wait_ge(q_made, b + 1)
                    act.activation(q[:], ps_b[:], ACT.Identity, bias=g.bias(B_Q1)).then_inc(q_ready, 1)
                    act.wait_ge(q_ready, b + 1)
                    act.wait_ge(pieces_free, b + 1)
                    act.activation(q_p[:, 0, :], q[:], ACT.Copy).then_inc(piece, 1)
                    act.wait_ge(k_ready, b + 1)
                    act.activation(k_p[:, 0, :], k[:], ACT.Copy).then_inc(piece, 1)
                    act.activation(square[:, 0, :], k[:], ACT.Square).then_inc(k_squared, 1)
                    act.activation(square[:, 1, :], q[:], ACT.Square).then_inc(q_squared, 1)
                    act.wait_ge(sk_made, b + 1)
                    act.activation(f.sparse_k[:, bass.ds(b * T, T)], ps_c[:], ACT.Identity, bias=g.bias(B_SK1), accum_out=sk_sum[:, 0:1]).then_inc(sk_ready, 1)
                    for n, pieces in enumerate((q_p, k_p)):
                        act.wait_ge(left, b * 4 + n + 1)
                        act.activation(pieces[:, 1, :], rest[:, n, :], ACT.Copy).then_inc(piece, 1)
                    act.wait_ge(norms_used, 2 * b + 2)
                    act.activation(bound[:], bound[:], ACT.Sqrt).then_inc(sqrt_ready, 1)

            @block.sync
            def _(sp):
                sp.sem_inc(pieces_free, 1)
                with sp.Fori(0, B) as b:

                    def keep(to, of):
                        sp.dma_start(to, of).then_inc(stored, 16)

                    at = bass.ds(b, 1)
                    sp.wait_ge(h_ready, b + 1)
                    sp.dma_start(scratch.h[at].rearrange("b n p c -> p (b n) c"), h[:]).then_inc(h_stored, 16)
                    sp.wait_ge(sq_ready, b + 1)
                    keep(scratch.sparse_q[at].rearrange("b r t -> (b r) t"), sq[0:RQ, :])
                    sp.wait_ge(v_ready, b + 1)
                    keep(scratch.v[at].rearrange("b n p c -> p (b n) c"), f.v[:, bass.ds(b * NT, NT), :])
                    sp.wait_ge(left, b * 4 + 4)
                    for i in range(PIECES):
                        keep(scratch.q[at, i].rearrange("b r t -> (b r) t"), q_p[:, i, :])
                        keep(scratch.k[at, i].rearrange("b r t -> (b r) t"), k_p[:, i, :])
                    sp.wait_ge(shift_ready, b + 1)
                    for i in range(PIECES):
                        keep(scratch.shift[at, i].rearrange("b r t -> (b r) t"), shift_p[:, i, :])
                    sp.wait_ge(stored, 16 * STORES * (b + 1))
                    sp.sem_inc(pieces_free, 1)
                sp.wait_ge(h_stored, 16 * B)

            @block.tensor
            def _(pe):
                pe.wait_ge(const_ready, 3)
                pe.wait_ge(pads_ready, 2)
                with pe.Fori(0, B) as b:

                    def project(to, w, of):
                        for n in range(2):
                            cols = slice(n * 512, n * 512 + 512)
                            ins = pe.matmul(to[0 : w.shape[1], cols], w, of[:, cols], start=True, stop=True)
                        return ins

                    def values(slot):
                        for n in range(NT):
                            ins = pe.matmul(ps_a[:, n * P : n * P + P], h_t[:, n * P : n * P + P], g.weights(slot), start=True, stop=True)
                        return ins

                    pe.wait_ge(h_ready, b + 1)
                    for n in range(NT):
                        ins = pe.transpose(ps_a[:, n * P : n * P + P], h[:, n, :], g.ident[:])
                        if n % 4 == 3:
                            ins.then_inc(h_turned, 1)
                    pe.wait_ge(h_t_ready, b * 2 + 2)
                    project(ps_b, g.weights(W_QKV1), h_t).then_inc(q_made, 1)
                    project(ps_c, g.weights(W_QKV1 + 1), h_t).then_inc(k_made, 1)
                    values(W_QKV1 + 2).then_inc(v_made, 1)
                    pe.wait_ge(q_ready, b + 1)
                    project(ps_b, sq_w[:], h_t).then_inc(sq_made, 1)
                    pe.wait_ge(k_ready, b + 1)
                    project(ps_c, sk_w[:], h_t).then_inc(sk_made, 1)
                    pe.wait_ge(v_ready, b + 1)
                    values(W_V1).then_inc(sv_made, 1)
                    pe.wait_ge(sk_ready, b + 1)
                    pe.wait_ge(sq_ready, b + 1)
                    for n in range(NT):
                        ins = pe.matmul(ps_b[:, n : n + 1], sq[:, n * P : n * P + P], sk_sum[:, 0:1], start=True, stop=True)
                    ins.then_inc(mean_made, 1)
                    pe.wait_ge(k_squared, b + 1)
                    project(ps_d, head_sum[:], square[:, 0, :]).then_inc(norms_made, 1)
                    pe.wait_ge(q_squared, b + 1)
                    pe.wait_ge(norms_used, 2 * b + 1)
                    project(ps_d, head_sum[:], square[:, 1, :]).then_inc(norms_made, 1)
        a.clear_sems()


SEARCH = 7
TRUST = (0.85, 0.8, 0.5, 0.5, 0.35, 0.35)
IN_MIN, IN_MAX = TOP - 7, TOP - 1
AIM = 0.5 * (IN_MIN + IN_MAX)
Z_TOP, DENSITY, MEAN_EXCESS = 0.8416, 0.2800, 0.3989423


PE_AT = (0, 4, 8, 11, 15, 19, 23)
ACT_AT = (3, 8, 14, 22, 12, 20)
DVE_AT = (1, 4)


def after(eng, sem, count):
    if not isinstance(count, int) or count > 0:
        eng.wait_ge(sem, count)


def attend(nc, g, f, scratch):
    STEPS = 4 * NT
    PER = GROUPS * STEPS
    LAST = GROUPS - 1
    LOADS = 2 * PIECES * PIECES + 1
    with ExitStack() as ctx:
        a = Alloc(nc, ctx)
        q_pack = a.sb("q_pack", [P, 2, 4, T], BF16)
        k_pack = a.sb("k_pack", [P, 2, 4, T], BF16)
        probs = a.sb("probs1", [P, 2, 4, T])
        v_pad = a.sb("v_pad", [P, 2, NT, 4, 32])
        pv = a.sb("pv", [P, T])
        inv = a.sb("pv_inv", [P, NT, 4])
        sq = a.sb("sparse_q_tile", [P, 2, P])
        s = a.sb("sparse_scores", [P, 2, T])
        e = a.sb("sparse_exp", [P, 2, T])
        junk = a.sb("junk", [P, T])
        above = a.sb("above_mean", [P, 2, T], BF16)
        w_t = a.sb("sparse_w_t", [P, NT, P])
        so = a.sb("sparse_out_tile", [P, 2, C])
        excess = a.sb("row_excess", [P, 2])
        top = a.sb("row_max", [P, 2])
        nmax = a.sb("minus_row_max", [P, 2])
        z = a.sb("row_exp_sum", [P, 2])
        at = a.sb("at", [P, 2])
        trust = a.sb("trust", [P, len(TRUST), 2])
        gain = a.sb("gain", [P, len(TRUST), 2])
        count = a.sb("count", [P, 2])
        off = a.sb("off", [P, 2])
        square = a.sb("off_squared", [P, 2])
        near = a.sb("near", [P, 2, 8])
        order = a.sb("order", [P, 8])
        pick = a.sb("pick", [P, 8])
        rank = a.sb("rank", [P, 2])
        cut = a.sb("cut", [P, 2])
        nears = a.sb("nears", [P, TILES, 8])
        nearer = a.sb("nearer", [P, TILES, 8])
        ranks = a.sb("ranks", [P, TILES])
        cuts = a.sb("cuts", [P, TILES])
        wrong = a.sb("wrong", [P, TILES])
        tied = a.sb("tied", [P, TILES])
        worst = a.sb("worst", [P, 2])
        w_sum = a.sb("w_sum", [P, 2, 2])
        scores_ps = [a.ps(f"scores1_ps{i}", [P, T]) for i in range(2)]
        pv_ps = a.ps("pv_ps", [P, 2, 512])
        misc = a.ps("misc_ps", [P, T])
        vec = a.sem("attend_vec")
        const_ready = a.sem("attend_const")
        packs_loaded = [a.sem(f"packs_loaded{i}") for i in range(2)]
        sq_loaded = [a.sem(f"sparse_q_loaded{i}") for i in range(2)]
        so_stored = [a.sem(f"sparse_out_stored{i}") for i in range(2)]
        v_staged = a.sem("v_staged")
        scored = a.sem("scored1")
        exp_done = a.sem("exp1_done")
        pv_done = a.sem("pv_done")
        pv_kept = a.sem("pv_kept")
        misc_made = a.sem("misc_made")
        misc_used = a.sem("misc_used")
        scores_kept = a.sem("sparse_scores_kept")
        max_ready = a.sem("sparse_max_ready")
        excess_ready = a.sem("excess_ready")
        sparse_exp = a.sem("sparse_exp_done")
        w_ready = a.sem("sparse_w_ready")
        w_t_ready = a.sem("sparse_w_t_ready")
        out_ready = a.sem("sparse_out_ready")
        USES = 7

        def use(b, group, k):
            if k < 2:
                return b * (USES * GROUPS) + (USES * group - 4 + k) if not (group == 0 and isinstance(b, int)) else k + 1
            return b * (USES * GROUPS) + (USES * group + 3 + k)

        def last_use(k):
            return USES * (B * GROUPS - 1) + 1 + k

        def before(b, group):
            return (b, group - 1) if group > 0 else (b - 1, LAST)

        def over_batches(eng, body, end):
            body(0, True)
            with eng.Fori(1, B) as b:
                body(b, False)
            end(B - 1)

        with nc.Block() as block:

            @block.sync
            def _(sp):

                def store(b, group, made):
                    for t in range(2):
                        sp.wait_ge(out_ready, made(b, group) + t + 1)
                        sp.dma_start(
                            scratch.sparse_out[bass.ds(b, 1), 2 * group + t].rearrange("b p c -> (b p) c"), so[:, t, :]
                        ).then_inc(so_stored[t], 16)

                def outs(b, group):
                    return b * NT + group * 2

                def body(b, first):
                    one = bass.ds(b, 1)
                    for group in range(GROUPS):
                        half = group % 2
                        after(sp, scored, b * PER + (group - 1) * STEPS + 1)
                        for i in range(PIECES):
                            for j in range(PIECES):
                                rows = slice((i * PIECES + j) * DH, (i * PIECES + j + 1) * DH)
                                for pack, of, n in ((q_pack, scratch.q, i), (k_pack, scratch.k, j)):
                                    sp.dma_start(
                                        pack[rows, half], of[one, n, group * 32 : group * 32 + 32].rearrange("b (h d) t -> d (b h) t", d=DH)
                                    ).then_inc(packs_loaded[half], 16)
                        sp.dma_start(
                            q_pack[SHIFT_ROW:PACK_ROWS, half], scratch.shift[one, :, group * 4 : group * 4 + 4].rearrange("b i h t -> (b i) h t")
                        ).then_inc(packs_loaded[half], 16)
                        for t in range(2):
                            tile = group * 2 + t
                            if not (first and group == 0):
                                sp.wait_ge(misc_made, use(*before(b, group), t))
                            sp.dma_start(
                                sq[0:RQ, t, :], scratch.sparse_q[one, :, tile * P : tile * P + P].rearrange("b r t -> (b r) t")
                            ).then_inc(sq_loaded[t], 16)
                        if not (first and group < 2):
                            store(*before(*before(b, group)), outs)

                def end(b):
                    store(*before(b, LAST), outs)
                    store(b, LAST, outs)
                    for t in range(2):
                        sp.wait_ge(so_stored[t], 16 * B * GROUPS)

                sp.wait_ge(const_ready, 6)
                over_batches(sp, body, end)

            @block.gpsimd
            def _(pool):
                pool.memset(v_pad[:], 0.0).then_inc(const_ready, 1)
                pool.wait_ge(const_ready, 1)
                pool.memset(q_pack[64:128], 0.0).then_inc(const_ready, 1)
                pool.wait_ge(const_ready, 2)
                pool.memset(k_pack[64:128], 1.0).then_inc(const_ready, 1)
                pool.wait_ge(const_ready, 3)
                pool.memset(sq[RQ:P], 0.0).then_inc(const_ready, 1)
                pool.wait_ge(const_ready, 4)
                pool.iota(order[:], pattern=[[1, 8]], base=1, channel_multiplier=0, allow_small_or_imprecise_dtypes=True).then_inc(const_ready, 1)
                pool.wait_ge(const_ready, 5)
                for k, part in enumerate(TRUST):
                    pool.memset(trust[:, k, :], part / (T * T * DENSITY * MEAN_EXCESS))
                pool.memset(v_pad[:, :, :, :, DH : DH + 1], 1.0).then_inc(const_ready, 1)
                pool.wait_ge(const_ready, 6)
                with pool.Fori(0, B) as b:
                    for group in range(GROUPS):
                        if group >= 2:
                            pool.wait_ge(pv_done, (b * GROUPS + group - 1) * NT)
                        pool.tensor_copy(
                            v_pad[:, group % 2, :, :, 0:DH],
                            f.v[:, bass.ds(b * NT, NT), group * 32 : group * 32 + 32].rearrange("p n (h d) -> p n h d", d=DH),
                        ).then_inc(v_staged, 1)
                    pool.wait_ge(pv_done, (b + 1) * GROUPS * NT)

            @block.scalar
            def _(act):

                def rows_excess(b, group, t):
                    act.wait_ge(scores_kept, (b * GROUPS + group) * 2 + t + 1)
                    act.activation(
                        above[:, t, :], s[:, t, :], ACT.Relu, bias=f.minus_mean[:, bass.ds(b * NT + (group * 2 + t), 1)], accum_out=excess[:, t : t + 1]
                    ).then_inc(excess_ready, 1)

                def rows_exp(b, group, t, first):
                    act.wait_ge(max_ready, (b * GROUPS + group) * 2 + t + 1)
                    if not first:
                        act.wait_ge(misc_made, use(*before(b, group), 3 + 2 * t))
                    act.activation(e[:, t, :], s[:, t, :], ACT.Exp, bias=nmax[:, t : t + 1], accum_out=z[:, t : t + 1]).then_inc(sparse_exp, 1)

                def keep_turned(b, group, t, number):
                    act.wait_ge(misc_made, number)
                    act.activation(w_t[:], misc[:].rearrange("p (n c) -> p n c", n=NT), ACT.Copy).then_inc(w_t_ready, 1)

                def body(b, first):
                    for group in range(GROUPS):
                        alone = first and group == 0
                        prev = before(b, group)
                        side = {
                            ACT_AT[0]: lambda: rows_excess(b, group, 0),
                            ACT_AT[1]: lambda: rows_excess(b, group, 1),
                            ACT_AT[2]: lambda: rows_exp(b, group, 0, alone),
                            ACT_AT[3]: lambda: rows_exp(b, group, 1, alone),
                        }
                        if not alone:
                            side |= {
                                ACT_AT[4]: lambda: keep_turned(*prev, 0, use(*prev, 3)),
                                ACT_AT[5]: lambda: keep_turned(*prev, 1, use(*prev, 5)),
                            }
                        for n in range(STEPS):
                            kt, j = n // 4, n % 4
                            act.wait_ge(scored, b * PER + group * STEPS + n + 2)
                            if j == 0:
                                after(act, pv_done, b * GROUPS * NT + group * NT + kt - 1)
                            act.activation(probs[:, kt % 2, j, :], scores_ps[n % 2][:], ACT.Exp, scale=SCALE1).then_inc(exp_done, 1)
                            if n in side:
                                side[n]()

                def end(b):
                    for t in range(2):
                        keep_turned(b, LAST, t, last_use(3 + 2 * t))

                over_batches(act, body, end)

            @block.tensor
            def _(pe):

                def score(b, group, n):
                    kt, j = n // 4, n % 4
                    if n == 0:
                        pe.wait_ge(packs_loaded[group % 2], 16 * LOADS * (b * 2 + group // 2 + 1))
                    after(pe, exp_done, b * PER + group * STEPS + n - 1)
                    for c in range(2):
                        ins = pe.matmul(
                            scores_ps[n % 2][:, c * 512 : c * 512 + 512],
                            k_pack[:, group % 2, j, kt * P : kt * P + P],
                            q_pack[:, group % 2, j, c * 512 : c * 512 + 512],
                            start=True,
                            stop=True,
                        )
                    ins.then_inc(scored, 1)

                def values(b, group, kt, c):
                    if c == 0:
                        pe.wait_ge(exp_done, b * PER + group * STEPS + kt * 4 + 4)
                        if kt == 0:
                            pe.wait_ge(v_staged, b * GROUPS + group + 1)
                            after(pe, pv_kept, b * GROUPS + group)
                    for j in range(4):
                        ins = pe.matmul(
                            pv_ps[32 * j : 32 * j + 32, c, :],
                            v_pad[:, group % 2, kt, j, :],
                            probs[:, kt % 2, j, c * 512 : c * 512 + 512],
                            start=(kt == 0),
                            stop=(kt == NT - 1),
                        )
                    if c == 1:
                        ins.then_inc(pv_done, 1)

                def free(number):
                    after(pe, misc_used, number - 1)

                def sparse_scores(b, group, t):
                    free(use(b, group, t))
                    pe.wait_ge(sq_loaded[t], 16 * (b * GROUPS + group + 1))
                    for c in range(2):
                        ins = pe.matmul(misc[:, c * 512 : c * 512 + 512], sq[:, t, :], f.sparse_k[:, bass.ds(b * T + c * 512, 512)], start=True, stop=True)
                    ins.then_inc(misc_made, 1)

                def turn_out(b, group, number):
                    free(number)
                    pe.wait_ge(pv_kept, b * GROUPS + group + 1)
                    for n in range(NT):
                        ins = pe.transpose(misc[:, n * P : n * P + P], pv[:, n * P : n * P + P], g.ident[:])
                    ins.then_inc(misc_made, 1)

                def turn_weights(b, group, t, number):
                    free(number)
                    pe.wait_ge(w_ready, b * GROUPS + group + 1)
                    for n in range(NT):
                        ins = pe.transpose(misc[:, n * P : n * P + P], e[:, t, n * P : n * P + P], g.ident[:])
                    ins.then_inc(misc_made, 1)

                def sparse_values(b, group, t):
                    pe.wait_ge(w_t_ready, (b * GROUPS + group) * 2 + t + 1)
                    for n in range(NT):
                        ins = pe.matmul(
                            misc[:, 0:C],
                            w_t[:, n, :],
                            f.sparse_v[:, bass.ds(b * NT + n, 1), :].rearrange("p n c -> p (n c)"),
                            start=(n == 0),
                            stop=(n == NT - 1),
                        )
                    ins.then_inc(misc_made, 1)

                def body(b, first):
                    for group in range(GROUPS):
                        prev = before(b, group)
                        alone = first and group == 0
                        side = {PE_AT[0]: lambda: sparse_scores(b, group, 0), PE_AT[1]: lambda: sparse_scores(b, group, 1)}
                        if not alone:
                            side |= {
                                PE_AT[2]: lambda: turn_out(*prev, use(*prev, 2)),
                                PE_AT[3]: lambda: turn_weights(*prev, 0, use(*prev, 3)),
                                PE_AT[4]: lambda: sparse_values(*prev, 0),
                                PE_AT[5]: lambda: turn_weights(*prev, 1, use(*prev, 5)),
                                PE_AT[6]: lambda: sparse_values(*prev, 1),
                            }
                        for n in range(STEPS):
                            score(b, group, n)
                            if n % 4 in (1, 2):
                                if n >= 4:
                                    values(b, group, n // 4 - 1, n % 4 - 1)
                                elif not alone:
                                    values(*prev, NT - 1, n % 4 - 1)
                            if n in side:
                                side[n]()

                def end(b):
                    values(b, LAST, NT - 1, 0)
                    values(b, LAST, NT - 1, 1)
                    turn_out(b, LAST, last_use(2))
                    for t in range(2):
                        turn_weights(b, LAST, t, last_use(3 + 2 * t))
                        sparse_values(b, LAST, t)

                pe.wait_ge(const_ready, 6)
                pe.sem_inc(scored, 1)
                over_batches(pe, body, end)

            @block.vector
            def _(dve):

                def keep_pv(step, b, group):
                    dve.wait_ge(pv_done, (b * GROUPS + group + 1) * NT)
                    dve.tensor_copy(pv[:], pv_ps[:].rearrange("p c t -> p (c t)")).then_inc(pv_kept, 1)

                def keep_scores(step, b, group, t):
                    dve.wait_ge(misc_made, use(b, group, t))
                    dve.tensor_scalar(s[:, t, :], misc[:], 1.0, None, ALU.mult, ALU.max, accum_out=top[:, t : t + 1]).then_inc(scores_kept, 1)
                    dve.wait_ge(scores_kept, (b * GROUPS + group) * 2 + t + 1)
                    dve.sem_inc(misc_used, 1)
                    dve.tensor_scalar(nmax[:, t : t + 1], top[:, t : t + 1], -1.0, None, ALU.mult).then_inc(max_ready, 1)

                def heads_out(step, b, group, number):
                    dve.wait_ge(misc_made, number)
                    turned = misc[:].rearrange("p (n j c) -> p n j c", n=NT, j=4)
                    step(dve.reciprocal(inv[:], turned[:, :, :, DH]))
                    step.settle()
                    for n in range(NT):
                        step(
                            dve.tensor_tensor(
                                f.v[:, bass.ds(b * NT + n, 1), group * 32 : group * 32 + 32].rearrange("p n (j d) -> p (n j) d", d=DH),
                                turned[:, n, :, 0:DH],
                                inv[:, n, :].unsqueeze(2).to_broadcast([P, 4, DH]),
                                ALU.mult,
                            )
                        )
                    step(dve.reduce_max(worst[:, 0:1], inv[:].rearrange("p n j -> p (n j)"), AX.X))
                    step.settle()
                    dve.sem_inc(misc_used, 1)
                    step(dve.scalar_tensor_tensor(out=f.doubt[:, 0:1], in0=worst[:, 0:1], scalar=float(np.exp(FLOOR)), in1=f.doubt[:, 0:1], op0=ALU.is_gt, op1=ALU.max))

                def keep_out(step, b, group, t, number):
                    dve.wait_ge(misc_made, number)
                    after(dve, so_stored[t], 16 * (b * GROUPS + group))
                    dve.tensor_scalar(so[:, t, :], misc[:, 0:C], w_sum[:, group % 2, t : t + 1], None, ALU.mult).then_inc(out_ready, 1)
                    dve.wait_ge(out_ready, b * NT + group * 2 + t + 1)
                    dve.sem_inc(misc_used, 2)

                def start_search(step, b, group, t):
                    one = slice(t, t + 1)
                    dve.wait_ge(excess_ready, (b * GROUPS + group) * 2 + t + 1)
                    minus_mean = f.minus_mean[:, bass.ds(b * NT + (2 * group + t), 1)]
                    step(dve.scalar_tensor_tensor(out=at[:, one], in0=excess[:, one], scalar=Z_TOP / (T * MEAN_EXCESS), in1=minus_mean, op0=ALU.mult, op1=ALU.subtract))
                    step(dve.tensor_scalar(gain[:, :, t], trust[:, :, t], excess[:, one], None, ALU.mult))
                    step.settle()
                    step(dve.tensor_scalar(junk[:], s[:, t, :], at[:, one], None, ALU.is_ge, ALU.add, accum_out=count[:, one]))
                    step.settle()

                def search(step, k):
                    step(dve.tensor_scalar(off[:], count[:], -AIM, None, ALU.add))
                    step.settle()
                    step(dve.tensor_tensor(square[:], off[:], off[:], ALU.mult))
                    step(dve.tensor_tensor(off[:], off[:], gain[:, k, :], ALU.mult))
                    step.settle()
                    step(dve.scalar_tensor_tensor(out=off[:], in0=square[:], scalar=(AIM - IN_MIN + 0.5) ** 2, in1=off[:], op0=ALU.is_gt, op1=ALU.mult))
                    step.settle()
                    step(dve.tensor_tensor(at[:], at[:], off[:], ALU.add))
                    step.settle()
                    for t in range(2):
                        step(dve.tensor_scalar(junk[:], s[:, t, :], at[:, t : t + 1], None, ALU.is_ge, ALU.add, accum_out=count[:, t : t + 1]))
                        step.settle()

                def weigh(step, b, group, t):
                    one = slice(t, t + 1)
                    half = group % 2
                    if t == 0:
                        step(dve.tensor_scalar(rank[:], count[:], -1.0, float(TOP), ALU.mult, ALU.add))
                    dve.wait_ge(sparse_exp, (b * GROUPS + group) * 2 + t + 1)
                    step(dve.scalar_tensor_tensor(out=junk[:], in0=s[:, t, :], scalar=at[:, one], in1=e[:, t, :], op0=ALU.is_lt, op1=ALU.mult))
                    step.settle()
                    step(dve.max(near[:, t, :], junk[:]))
                    step.settle()
                    step(
                        dve.scalar_tensor_tensor(
                            out=pick[:], in0=order[:], scalar=rank[:, one], in1=near[:, t, :], op0=ALU.is_equal, op1=ALU.mult, accum_out=cut[:, one]
                        )
                    )
                    step.settle()
                    step(
                        dve.scalar_tensor_tensor(
                            out=e[:, t, :], in0=e[:, t, :], scalar=cut[:, one], in1=e[:, t, :], op0=ALU.is_ge, op1=ALU.mult, accum_out=w_sum[:, half, one]
                        )
                    )
                    if t == 1:
                        tiles = bass.ds(b * NT + 2 * group, 2)
                        step(dve.tensor_copy(nears[:, tiles, :], near[:]))
                        step(dve.tensor_copy(ranks[:, tiles], rank[:]))
                        step(dve.tensor_copy(cuts[:, tiles], cut[:]))
                        step.settle()
                        step(dve.scalar_tensor_tensor(out=w_sum[:, half, :], in0=z[:], scalar=1e-9, in1=w_sum[:, half, :], op0=ALU.mult, op1=ALU.add))
                        step.settle()
                        dve.reciprocal(w_sum[:, half, :], w_sum[:, half, :]).then_inc(w_ready, 1)
                        dve.wait_ge(w_ready, b * GROUPS + group + 1)
                    else:
                        step.settle()

                def doubts(step):
                    step(dve.tensor_scalar(wrong[:], ranks[:], float(TOP - IN_MAX), None, ALU.is_lt))
                    step(dve.tensor_scalar(tied[:], ranks[:], 1.0, None, ALU.add))
                    step.settle()
                    step(dve.scalar_tensor_tensor(out=wrong[:], in0=ranks[:], scalar=float(TOP - IN_MIN), in1=wrong[:], op0=ALU.is_gt, op1=ALU.max))
                    step(dve.tensor_tensor(nearer[:], bc(order[:], TILES), tied[:].unsqueeze(2).to_broadcast([P, TILES, 8]), ALU.is_equal))
                    step.settle()
                    step(dve.tensor_tensor(nearer[:], nearer[:], nears[:], ALU.mult))
                    step.settle()
                    step(dve.reduce_max(tied[:], nearer[:], AX.X))
                    step.settle()
                    step(dve.tensor_tensor(tied[:], tied[:], cuts[:], ALU.is_equal))
                    step.settle()
                    step(dve.scalar_tensor_tensor(out=tied[:], in0=cuts[:], scalar=0.0, in1=tied[:], op0=ALU.is_gt, op1=ALU.mult))
                    step.settle()
                    step(dve.tensor_tensor(wrong[:], wrong[:], tied[:], ALU.max))
                    step.settle()
                    step(dve.reduce_max(f.doubt[:, 1:2], wrong[:], AX.X))
                    step.settle()

                def finish(step, prev, between):
                    if prev:
                        weigh(step, *prev, 0)
                    between()
                    if prev:
                        keep_pv(step, *prev)
                        weigh(step, *prev, 1)

                def body(b, first):
                    step = Steps(dve, vec)
                    for group in range(GROUPS):
                        prev = None if first and group == 0 else before(b, group)
                        finish(step, prev, lambda: keep_scores(step, b, group, 0))
                        keep_scores(step, b, group, 1)
                        start_search(step, b, group, 0)
                        if prev:
                            heads_out(step, *prev, use(*prev, 2))
                        start_search(step, b, group, 1)
                        for k in range(SEARCH - 1):
                            search(step, k)
                            if prev and k in DVE_AT:
                                t = DVE_AT.index(k)
                                keep_out(step, *prev, t, use(*prev, 4 + 2 * t))
                    step.again()

                def end(b):
                    step = Steps(dve, vec)
                    finish(step, (b, LAST), lambda: None)
                    heads_out(step, b, LAST, last_use(2))
                    for t in range(2):
                        keep_out(step, b, LAST, t, last_use(4 + 2 * t))
                    doubts(step)
                    step.again()

                dve.wait_ge(const_ready, 6)
                step = Steps(dve, vec)
                step(dve.memset(f.doubt[:], 0.0))
                step.again()
                over_batches(dve, body, end)


def heads_again(nc, g, f, scratch):
    with ExitStack() as ctx:
        a = Alloc(nc, ctx, "_again")
        flag, flag_ready = doubt_flag(nc, g, f, a, 0)
        q_pack = a.sb("q_pack", [P, T], BF16)
        k_pack = a.sb("k_pack", [P, T], BF16)
        v = a.sb("v", [P, NT, DH])
        probs = a.sb("probs", [P, T])
        probs_t = a.sb("probs_t", [P, T])
        nmax = a.sb("minus_max", [P, 1])
        total = a.sb("total", [P, 1])
        scores_ps = a.ps("scores_ps", [P, T])
        turn_ps = a.ps("turn_ps", [P, T])
        out_ps = a.ps("out_ps", [P, 512])
        vec = a.sem("vec")
        cleared = a.sem("cleared")
        loaded = a.sem("loaded")
        scored = a.sem("scored")
        max_ready = a.sem("max_ready")
        probs_ready = a.sem("probs_ready")
        probs_turned = a.sem("probs_turned")
        probs_t_ready = a.sem("probs_t_ready")
        out_made = a.sem("out_made")
        done = a.sem("done")
        sp_rounds = a.sem("sp_rounds")
        LOADS = 2 * PIECES * PIECES + 1

        with nc.Block() as block:

            @block.sync
            def _(sp):
                sp.wait_ge(flag_ready, 1)
                with sp.If(sp.value_load(flag[0:1, 0:1], min_val=0, max_val=P) != 0):
                    sp.wait_ge(cleared, 2)
                    with sp.Fori(0, B) as b:
                        with sp.Fori(0, HEADS) as head:
                            at = bass.ds(b, 1)
                            dims = bass.ds(head * DH, DH)
                            for i in range(PIECES):
                                for j in range(PIECES):
                                    rows = slice((i * PIECES + j) * DH, (i * PIECES + j + 1) * DH)
                                    sp.dma_start(q_pack[rows, :], scratch.q[at, i, dims].rearrange("b d t -> (b d) t")).then_inc(loaded, 16)
                                    sp.dma_start(k_pack[rows, :], scratch.k[at, j, dims].rearrange("b d t -> (b d) t")).then_inc(loaded, 16)
                            sp.dma_start(v[:], scratch.v[at, :, :, dims].rearrange("b n p d -> p (b n) d")).then_inc(loaded, 16)
                            sp.wait_ge(done, (b * HEADS + head + 1) * NT)
                            sp.sem_inc(sp_rounds, 1)

            @block.vector
            def _(dve):
                dve.wait_ge(flag_ready, 1)
                with dve.If(dve.value_load(flag[0:1, 0:1], min_val=0, max_val=P) != 0):
                    dve.memset(q_pack[64:128], 0.0).then_inc(cleared, 1)
                    dve.memset(k_pack[64:128], 0.0).then_inc(cleared, 1)
                    with dve.Fori(0, B) as b:
                        with dve.Fori(0, HEADS) as head:
                            with dve.Fori(0, NT) as n:
                                step = Steps(dve, vec)
                                at = (b * HEADS + head) * NT + n
                                dve.wait_ge(scored, at + 1)
                                step(dve.tensor_reduce(nmax[:], scores_ps[:], AX.X, ALU.max, negate=True))
                                step.settle()
                                dve.tensor_scalar(nmax[:], nmax[:], SCALE1, None, ALU.mult).then_inc(max_ready, 1)
                                dve.wait_ge(out_made, at + 1)
                                step(dve.reciprocal(total[:], total[:]))
                                step.settle()
                                dve.tensor_scalar(
                                    f.v[:, bass.ds(b * NT + n, 1), bass.ds(head * DH, DH)].rearrange("p n d -> p (n d)"), out_ps[:, 0:DH], total[:, 0:1], None, ALU.mult
                                ).then_inc(done, 1)
                                step.again()

            @block.scalar
            def _(act):
                act.wait_ge(flag_ready, 1)
                with act.If(act.value_load(flag[0:1, 0:1], min_val=0, max_val=P) != 0):
                    with act.Fori(0, B * HEADS * NT) as at:
                        act.wait_ge(max_ready, at + 1)
                        act.activation(probs[:], scores_ps[:], ACT.Exp, bias=nmax[:, 0:1], scale=SCALE1, accum_out=total[:, 0:1]).then_inc(probs_ready, 1)
                        act.wait_ge(probs_turned, at + 1)
                        act.activation(probs_t[:], turn_ps[:], ACT.Copy).then_inc(probs_t_ready, 1)
                        act.wait_ge(done, at + 1)

            @block.tensor
            def _(pe):
                pe.wait_ge(flag_ready, 1)
                with pe.If(pe.value_load(flag[0:1, 0:1], min_val=0, max_val=P) != 0):
                    with pe.Fori(0, B * HEADS) as head:
                        with pe.Fori(0, NT) as n:
                            pe.wait_ge(loaded, head * (16 * LOADS) + 16 * LOADS)
                            at = head * NT + n
                            for c in range(2):
                                cols = slice(c * 512, c * 512 + 512)
                                ins = pe.matmul(scores_ps[:, cols], q_pack[:, bass.ds(n * P, P)], k_pack[:, cols], start=True, stop=True)
                            ins.then_inc(scored, 1)
                            pe.wait_ge(probs_ready, at + 1)
                            for m in range(NT):
                                ins = pe.transpose(turn_ps[:, m * P : m * P + P], probs[:, m * P : m * P + P], g.ident[:])
                            ins.then_inc(probs_turned, 1)
                            pe.wait_ge(probs_t_ready, at + 1)
                            for m in range(NT):
                                ins = pe.matmul(out_ps[:, 0:DH], probs_t[:, m * P : m * P + P], v[:, m, :], start=(m == 0), stop=(m == NT - 1))
                            ins.then_inc(out_made, 1)
                            pe.wait_ge(done, at + 1)


def sparse_again(nc, g, f, scratch):
    with ExitStack() as ctx:
        a = Alloc(nc, ctx, "_sparse_again")
        flag, flag_ready = doubt_flag(nc, g, f, a, 1)
        sq = a.sb("sq", [P, P])
        e = a.sb("e", [P, T])
        left = a.sb("left", [P, T])
        w_t = a.sb("w_t", [P, T])
        so = a.sb("so", [P, C])
        best = a.sb("best", [P, 8])
        nmax = a.sb("minus_max", [P, 1])
        z = a.sb("z", [P, 1])
        w_sum = a.sb("w_sum", [P, 1])
        scores_ps = a.ps("scores_ps", [P, T])
        turn_ps = a.ps("turn_ps", [P, T])
        out_ps = a.ps("out_ps", [P, 512])
        vec = a.sem("vec")
        cleared = a.sem("cleared")
        loaded = a.sem("loaded")
        scored = a.sem("scored")
        max_ready = a.sem("max_ready")
        exp_ready = a.sem("exp_ready")
        w_ready = a.sem("w_ready")
        w_turned = a.sem("w_turned")
        w_t_ready = a.sem("w_t_ready")
        out_made = a.sem("out_made")
        out_ready = a.sem("out_ready")
        stored = a.sem("stored")
        sp_rounds = a.sem("sp_rounds")
        ROUNDS, LAST = TOP // 8, TOP % 8

        with nc.Block() as block:

            @block.sync
            def _(sp):
                sp.wait_ge(flag_ready, 1)
                with sp.If(sp.value_load(flag[0:1, 0:1], min_val=0, max_val=P) != 0):
                    sp.wait_ge(cleared, 1)
                    with sp.Fori(0, B) as b:
                        with sp.Fori(0, NT) as n:
                            sp.dma_start(sq[0:RQ, :], scratch.sparse_q[bass.ds(b, 1), :, bass.ds(n * P, P)].rearrange("b r t -> (b r) t")).then_inc(loaded, 16)
                            sp.wait_ge(out_ready, b * NT + n + 1)
                            sp.dma_start(scratch.sparse_out[bass.ds(b, 1), bass.ds(n, 1)].rearrange("b n p c -> (b n p) c"), so[:]).then_inc(stored, 16)
                            sp.wait_ge(stored, (b * NT + n) * 16 + 16)
                            sp.sem_inc(sp_rounds, 1)

            @block.vector
            def _(dve):
                dve.wait_ge(flag_ready, 1)
                with dve.If(dve.value_load(flag[0:1, 0:1], min_val=0, max_val=P) != 0):
                    dve.memset(sq[RQ:P], 0.0).then_inc(cleared, 1)
                    with dve.Fori(0, TILES) as at:
                        step = Steps(dve, vec)
                        dve.wait_ge(scored, at + 1)
                        dve.tensor_reduce(nmax[:], scores_ps[:], AX.X, ALU.max, negate=True).then_inc(max_ready, 1)
                        dve.wait_ge(exp_ready, at + 1)
                        step(dve.tensor_copy(left[:], e[:]))
                        step.again()
                        with dve.Fori(0, ROUNDS) as _:
                            step = Steps(dve, vec)
                            step(dve.max(best[:], left[:]))
                            step.settle()
                            step(dve.match_replace(left[:], best[:], left[:], -1.0))
                            step.again()
                        step = Steps(dve, vec)
                        if LAST:
                            step(dve.max(best[:], left[:]))
                            step.settle()
                            step(dve.memset(best[:, LAST:8], 2.0))
                            step.settle()
                            step(dve.match_replace(left[:], best[:], left[:], -1.0))
                            step.settle()
                        step(dve.scalar_tensor_tensor(out=left[:], in0=left[:], scalar=0.0, in1=e[:], op0=ALU.is_lt, op1=ALU.mult, accum_out=w_sum[:]))
                        step.settle()
                        step(dve.scalar_tensor_tensor(out=w_sum[:], in0=z[:], scalar=1e-9, in1=w_sum[:], op0=ALU.mult, op1=ALU.add))
                        step.settle()
                        dve.reciprocal(w_sum[:], w_sum[:]).then_inc(w_ready, 1)
                        dve.wait_ge(out_made, at + 1)
                        dve.wait_ge(w_ready, at + 1)
                        dve.tensor_scalar(so[:], out_ps[:, 0:C], w_sum[:, 0:1], None, ALU.mult).then_inc(out_ready, 1)
                        step.again()

            @block.scalar
            def _(act):
                act.wait_ge(flag_ready, 1)
                with act.If(act.value_load(flag[0:1, 0:1], min_val=0, max_val=P) != 0):
                    with act.Fori(0, TILES) as at:
                        act.wait_ge(max_ready, at + 1)
                        act.activation(e[:], scores_ps[:], ACT.Exp, bias=nmax[:, 0:1], accum_out=z[:, 0:1]).then_inc(exp_ready, 1)
                        act.wait_ge(w_turned, at + 1)
                        act.activation(w_t[:], turn_ps[:], ACT.Copy).then_inc(w_t_ready, 1)

            @block.tensor
            def _(pe):
                pe.wait_ge(flag_ready, 1)
                with pe.If(pe.value_load(flag[0:1, 0:1], min_val=0, max_val=P) != 0):
                    with pe.Fori(0, B) as b:
                        with pe.Fori(0, NT) as n:
                            at = b * NT + n
                            pe.wait_ge(loaded, at * 16 + 16)
                            for c in range(2):
                                ins = pe.matmul(scores_ps[:, c * 512 : c * 512 + 512], sq[:], f.sparse_k[:, bass.ds(b * T + c * 512, 512)], start=True, stop=True)
                            ins.then_inc(scored, 1)
                            pe.wait_ge(w_ready, at + 1)
                            for m in range(NT):
                                ins = pe.transpose(turn_ps[:, m * P : m * P + P], left[:, m * P : m * P + P], g.ident[:])
                            ins.then_inc(w_turned, 1)
                            pe.wait_ge(w_t_ready, at + 1)
                            for m in range(NT):
                                ins = pe.matmul(
                                    out_ps[:, 0:C],
                                    w_t[:, m * P : m * P + P],
                                    f.sparse_v[:, bass.ds(b * NT + m, 1), :].rearrange("p n c -> p (n c)"),
                                    start=(m == 0),
                                    stop=(m == NT - 1),
                                )
                            ins.then_inc(out_made, 1)


def doubt_flag(nc, g, f, a, kind):
    flag = a.sb("flag", [P, 1], I32)
    doubt = a.sb("doubt_bf16", [P, 1], BF16)
    flag_ps = a.ps("flag_ps", [P, 1])
    doubt_ready = a.sem("doubt_ready")
    counted = a.sem("doubt_counted")
    flag_ready = a.sem("flag_ready")
    with nc.Block() as block:

        @block.vector
        def _(dve):
            dve.tensor_copy(doubt[:], f.doubt[:, kind : kind + 1]).then_inc(doubt_ready, 1)
            dve.wait_ge(counted, 1)
            dve.tensor_copy(flag[:], flag_ps[:]).then_inc(flag_ready, 1)

        @block.tensor
        def _(pe):
            pe.wait_ge(doubt_ready, 1)
            pe.matmul(flag_ps[:], g.ones_b[:], doubt[:], start=True, stop=True).then_inc(counted, 1)

    return flag, flag_ready


def finish_attention(nc, g, f, scratch):
    with ExitStack() as ctx:
        a = Alloc(nc, ctx)
        norm = Norm(a, "ln_post", g.minus_half)
        h = a.sb("h1_again", [P, NT, C])
        sparse = a.sb("sparse_in", [P, NT, C])
        ctx_rows = a.sb("ctx1_rows", [P, NT, C])
        ctx_t = a.sb("ctx1_t", [P, T])
        dense = a.sb("dense1", [P, NT, C])
        y = a.sb("y1", [P, NT, C])
        y_kept = a.sb("y1_kept", [P, NT, C])
        y_t = a.sb("y1_t", [P, T])
        ff = a.sb("ff1", [P, FC, T])
        out = a.sb("out1", [P, NT, C])
        gain = a.sb("gated_gain", [P, C])
        shift = a.sb("gated_shift", [P, C])
        lam_e = a.sb("lam_exp", [P, 1])
        sig = a.sb("sigmoid_lam", [P, 1])
        cosig = a.sb("one_minus_sigmoid", [P, 1])
        turn_ps = a.ps("post_turn_ps", [P, T])
        out_ps = a.ps("post_out_ps", [P, T])
        ff_ps = [a.ps(f"post_ff_ps{i}", [P, 512]) for i in range(4)]
        vec = a.sem("post_vec")
        vec_pool = a.sem("post_vec_pool")
        lam_ready = a.sem("lam_exp_ready")
        rows_loaded = a.sem("post_rows_loaded")
        rows_free = a.sem("post_rows_free")
        rows_ready = a.sem("ctx1_rows_ready")
        ctx_turned = a.sem("ctx1_turned")
        ctx_t_ready = a.sem("ctx1_t_ready")
        dense_made = a.sem("dense_made")
        out_used = a.sem("post_out_used")
        y_ready = a.sem("y1_ready")
        y_copied = a.sem("y1_copied")
        y_used = a.sem("y1_used")
        y_turned = a.sem("y1_turned")
        y_t_ready = a.sem("y1_t_ready")
        ff_made = a.sem("ff1_made")
        ff_act = a.sem("ff1_kept_act")
        down_made = a.sem("ff2_made")
        out_ready = a.sem("post_out_ready")
        done = a.sem("post_done")
        sp_rounds = a.sem("post_sp_rounds")
        flat = lambda t: t[:].rearrange("p n c -> p (n c)")

        def staggered(eng, first, second):
            first(0)
            with eng.Fori(0, B - 1) as b:
                first(b + 1)
                second(b)
            second(B - 1)

        def norm_no(b, half):
            if half == 0:
                return 2 * b if not isinstance(b, int) else max(2 * b, 1)
            return 2 * b + 3 if not isinstance(b, int) else 2 * B

        with nc.Block() as block:

            @block.sync
            def _(sp):
                with sp.Fori(0, B) as b:
                    one = bass.ds(b, 1)
                    sp.dma_start(h[:], scratch.h[one].rearrange("b n p c -> p (b n) c")).then_inc(rows_loaded, 16)
                    sp.dma_start(sparse[:], scratch.sparse_out[one].rearrange("b n p c -> p (b n) c")).then_inc(rows_loaded, 16)
                    sp.wait_ge(rows_free, b + 1)
                    sp.sem_inc(sp_rounds, 1)

            @block.gpsimd
            def _(pool):

                def first(b):
                    norm.pool(pool, norm_no(b, 0))

                def second(b):
                    norm.pool(pool, norm_no(b, 1))
                    step = Steps(pool, vec_pool)
                    pool.wait_ge(out_ready, b + 1)
                    step(pool.tensor_tensor(out[:], out[:], bc(shift[:], NT), ALU.add))
                    step.settle()
                    rows = g.x[:, bass.ds(b * NT, NT), :]
                    step(pool.tensor_tensor(rows, rows, out[:], ALU.add))
                    step.settle()
                    pool.sem_inc(done, 1)
                    step.again()

                pool.sem_inc(done, 1)
                staggered(pool, first, second)

            @block.vector
            def _(dve):
                step = Steps(dve, vec)
                dve.wait_ge(lam_ready, 1)
                step(dve.tensor_scalar(lam_e[:], lam_e[:], 1.0, None, ALU.add))
                step.settle()
                step(dve.reciprocal(sig[:], lam_e[:]))
                step.settle()
                step(dve.tensor_scalar(cosig[:], sig[:], -1.0, 1.0, ALU.mult, ALU.add))
                step.again()
                dve.sem_inc(y_used, 1)

                def first(b):
                    step = Steps(dve, vec)
                    dve.wait_ge(rows_loaded, 32 * (b + 1))
                    step(dve.scalar_tensor_tensor(out=flat(h), in0=flat(sparse), scalar=cosig[:, 0:1], in1=flat(h), op0=ALU.mult, op1=ALU.add))
                    dve.wait_ge(dense_made, b + 1)
                    step(dve.tensor_tensor(dense[:], out_ps[:].rearrange("p (n c) -> p n c", c=C), bc(g.row("L1_attn_out_proj_b"), NT), ALU.add))
                    step.settle()
                    dve.sem_inc(out_used, 1)
                    step(dve.scalar_tensor_tensor(out=flat(dense), in0=flat(dense), scalar=sig[:, 0:1], in1=flat(h), op0=ALU.mult, op1=ALU.add))
                    step.settle()
                    dve.sem_inc(rows_free, 1)

                    def ready():
                        dve.wait_ge(norm.rstd_ready, norm_no(b, 0))
                        if not isinstance(b, int):
                            dve.wait_ge(y_copied, b)
                            dve.wait_ge(y_turned, 2 * b)

                    layer_norm(dve, step, norm, dense, y[:], bc(g.row("L1_attn_ln1_g"), NT), ready)
                    step(dve.tensor_tensor(y[:], y[:], bc(g.row("L1_attn_ln1_b"), NT), ALU.add))
                    step.settle()
                    dve.sem_inc(y_ready, 1)
                    step.again()

                def second(b):
                    step = Steps(dve, vec)
                    dve.wait_ge(done, b + 1)
                    step(dve.tensor_tensor(gain[:], g.row("L1_attn_ln2_g"), g.mod_part(1, b, GA), ALU.mult))
                    step(dve.tensor_tensor(shift[:], g.row("L1_attn_ln2_b"), g.mod_part(1, b, GA), ALU.mult))
                    dve.wait_ge(down_made, b + 1)
                    step(dve.tensor_tensor(out[:], out_ps[:].rearrange("p (n c) -> p n c", c=C), bc(g.row("L1_attn_ff2_b"), NT), ALU.add))
                    step.settle()
                    dve.sem_inc(out_used, 1)
                    step(dve.tensor_tensor(out[:], out[:], y_kept[:], ALU.add))
                    step.settle()
                    dve.sem_inc(y_used, 1)
                    layer_norm(dve, step, norm, out, out[:], bc(gain[:], NT), lambda: dve.wait_ge(norm.rstd_ready, norm_no(b, 1)))
                    dve.sem_inc(out_ready, 1)
                    step.again()

                staggered(dve, first, second)

            @block.scalar
            def _(act):

                def first(b):
                    act.activation(ctx_rows[:], f.v[:, bass.ds(b * NT, NT), :], ACT.Copy).then_inc(rows_ready, 1)
                    for n in range(2):
                        act.wait_ge(ctx_turned, 2 * b + n + 1)
                        act.activation(ctx_t[:, n * 512 : n * 512 + 512], turn_ps[:, n * 512 : n * 512 + 512], ACT.Copy).then_inc(ctx_t_ready, 1)

                def second(b):
                    act.wait_ge(y_used, b + 1)
                    act.wait_ge(y_ready, b + 1)
                    act.activation(y_kept[:], y[:], ACT.Copy).then_inc(y_copied, 1)
                    for n in range(2):
                        act.wait_ge(y_turned, 2 * b + n + 1)
                        act.activation(y_t[:, n * 512 : n * 512 + 512], turn_ps[:, n * 512 : n * 512 + 512], ACT.Copy).then_inc(y_t_ready, 1)
                    for n in range(2):
                        for k in range(FC):
                            act.wait_ge(ff_made, b * 2 * FC + n * FC + k + 1)
                            act.activation(ff[:, k, n * 512 : n * 512 + 512], ff_ps[k][:], ACT.Relu, bias=g.bias(B_FF1 + k)).then_inc(ff_act, 1)

                act.activation(lam_e[:], g.lam[:], ACT.Exp, scale=-1.0).then_inc(lam_ready, 1)
                staggered(act, first, second)

            @block.tensor
            def _(pe):

                def turn(of, made):
                    for n in range(NT):
                        ins = pe.transpose(turn_ps[:, n * P : n * P + P], of[:, n, :], g.ident[:])
                        if n % 4 == 3:
                            ins.then_inc(made, 1)

                def first(b):
                    pe.wait_ge(rows_ready, b + 1)
                    turn(ctx_rows, ctx_turned)
                    pe.wait_ge(ctx_t_ready, 2 * b + 2)
                    if not isinstance(b, int):
                        pe.wait_ge(out_used, 2 * b - 1)
                    for n in range(NT):
                        ins = pe.matmul(out_ps[:, n * C : n * C + C], ctx_t[:, n * P : n * P + P], g.weights(W_OUT1), start=True, stop=True)
                    ins.then_inc(dense_made, 1)

                def second(b):
                    pe.wait_ge(y_ready, b + 1)
                    turn(y, y_turned)
                    for n in range(2):
                        pe.wait_ge(y_t_ready, 2 * b + n + 1)
                        for k in range(FC):
                            if n == 1:
                                pe.wait_ge(ff_act, b * 2 * FC + k + 1)
                            pe.matmul(ff_ps[k][:], g.weights(W_FF1 + k), y_t[:, n * 512 : n * 512 + 512], start=True, stop=True).then_inc(ff_made, 1)
                    pe.wait_ge(out_used, 2 * b + 2 if not isinstance(b, int) else 2 * B - 1)
                    for n in range(2):
                        pe.wait_ge(ff_act, b * 2 * FC + (n + 1) * FC)
                        for m in range(4 * n, 4 * n + 4):
                            for k in range(FC):
                                ins = pe.matmul(out_ps[:, m * C : m * C + C], ff[:, k, m * P : m * P + P], g.weights(W_FF2 + k), start=(k == 0), stop=(k == FC - 1))
                    ins.then_inc(down_made, 1)

                staggered(pe, first, second)


def fused_attention(nc, g, dram):
    with ExitStack() as ctx:
        f = Fused(Alloc(nc, ctx))
        scratch = Scratch(nc)
        prepare(nc, g, f, scratch, dram)
        attend(nc, g, f, scratch)
        heads_again(nc, g, f, scratch)
        sparse_again(nc, g, f, scratch)
        finish_attention(nc, g, f, scratch)


def adaln_program(nc, dram, out):
    with ExitStack() as whole:
        g = Shared(Alloc(nc, whole))
        rows = [ExpertRows(nc, layer) for layer in range(2)]
        with ExitStack() as layer0:
            a = Alloc(nc, layer0)
            g.wt0 = a.sb("weights0_t", [P, W_SLOTS_L0, P])
            g.mods[0] = a.sb("mod0", [P, B, 6 * C])
            setup(nc, g, dram)
            causal_attention(nc, g, rows)
            moe = Moe(a, rows[0], 0)
            route(nc, g, moe, dram, 0)
            experts0(nc, g, moe)
        with ExitStack() as attn1:
            fused_attention(nc, g, dram)
        with ExitStack() as ffn1:
            moe = Moe(Alloc(nc, ffn1), rows[1], 1)
            route(nc, g, moe, dram, 1)
            experts1(nc, g, moe)
        store(nc, g, out)


_INS = [
    "L0_attn_x",
    "L0_attn_qkv_w",
    "L0_attn_out_w",
    "L0_attn_out_b",
    "L0_ffn_router_w",
    "L0_ffn_expert_w1",
    "L0_ffn_expert_b1",
    "L0_ffn_expert_w2",
    "L0_ffn_expert_b2",
    "L0_c",
    "L0_wmod",
    "L1_attn_in_proj_w",
    "L1_attn_in_proj_b",
    "L1_attn_out_proj_w",
    "L1_attn_out_proj_b",
    "L1_attn_Qp_w",
    "L1_attn_Qp_b",
    "L1_attn_Kp_w",
    "L1_attn_Kp_b",
    "L1_attn_Vp_w",
    "L1_attn_Vp_b",
    "L1_attn_lam",
    "L1_attn_ff1_w",
    "L1_attn_ff1_b",
    "L1_attn_ff2_w",
    "L1_attn_ff2_b",
    "L1_attn_ln1_g",
    "L1_attn_ln1_b",
    "L1_attn_ln2_g",
    "L1_attn_ln2_b",
    "L1_ffn_Wr",
    "L1_ffn_W1",
    "L1_ffn_b1",
    "L1_ffn_W2",
    "L1_ffn_b2",
    "L1_c",
    "L1_wmod",
]
_OUT = (B, T, C)


def kernel(**inputs):
    import numpy as _np
    import concourse.bacc as _bacc
    from concourse import mybir as _mybir
    from concourse.bass_utils import run_bass_kernel_spmd as _run

    nc = _bacc.Bacc("TRN2", target_bir_lowering=False, num_devices=1)
    arrays, dram = {}, {}
    for name in _INS:
        a = _np.ascontiguousarray(inputs[name])
        if a.ndim == 0:
            a = a.reshape(1)
        arrays[f"in_{name}_dram"] = a
        dram[name] = nc.dram_tensor(f"in_{name}_dram", a.shape, _mybir.dt.from_np(a.dtype), kind="ExternalInput").ap()
    out = nc.dram_tensor("out_dram", _OUT, F32, kind="ExternalOutput").ap()
    adaln_program(nc, dram, out)
    r = _run(nc, [arrays], core_ids=[0])
    return r.results[0]["out_dram"]
```
